# Optimizing a Trainium2 kernel written in Bass

```python
import numpy as np
import jax
import jax.numpy as jnp

def _softmax(x, axis=-1):
    return jax.nn.softmax(x, axis=axis)

def _gelu(x):
    return jax.nn.gelu(x, approximate=True)

def _silu(x):
    return jax.nn.silu(x)

def _sigmoid(x):
    return jax.nn.sigmoid(x)

def _layernorm(x, axis=-1, eps=1e-05):
    m = jnp.mean(x, axis=axis, keepdims=True)
    v = jnp.var(x, axis=axis, keepdims=True)
    return (x - m) / jnp.sqrt(v + eps)

def _scatter_add(tgt, idx, src, axis=0):
    return tgt.at[idx].add(src)

def _segment_sum(src, seg, n):
    return jax.ops.segment_sum(src, seg, n)
kernel_name = 'mk_xattn_ffn_d1_seqx_r2_db0773'

def setup_inputs(seed: int=0):
    np.random.seed(seed)
    _w = jnp.asarray

    def _rec_inputs():
        import jax
        import jax.numpy as jnp
        _rk = jax.random.key(seed)
        x = 7.22e-05 + 1 * jax.random.normal(jax.random.fold_in(_rk, 1), (2, 2048, 512), jnp.float32)
        _lenS = 2048 - jax.random.randint(jax.random.fold_in(_rk, 7), (2,), 0, max(1, 2048 // 4) + 1, jnp.int32)
        _lenS2 = 77 - jax.random.randint(jax.random.fold_in(_rk, 8), (2,), 0, max(1, 77 // 4) + 1, jnp.int32)
        _ctx_1024P = jax.random.normal(jax.random.fold_in(_rk, 11), (2, 16, 512), jnp.float32)
        _ctx_1024c = jax.random.dirichlet(jax.random.fold_in(_rk, 511), 0.3 * jnp.ones((16,), jnp.float32), (2, 77))
        _ctx_1024t = jnp.einsum('bsk,bkd->bsd', _ctx_1024c, _ctx_1024P)
        _ctx_1024t = _ctx_1024t * jax.lax.rsqrt(jnp.mean(jnp.square(_ctx_1024t)) + 1e-12) * 0.953939
        ctx_1024 = 4.13588e-05 + 0.999923 * (_ctx_1024t + 0.3 * jax.random.normal(jax.random.fold_in(_rk, 611), (2, 77, 512), jnp.float32))
        _validS = jnp.arange(2048)[None, :] < _lenS[:, None]
        _validS2 = jnp.arange(77)[None, :] < _lenS2[:, None]
        _causal = jnp.tril(jnp.ones((2048, 2048), dtype=bool))
        mask_BxSxS2_ik1 = jnp.where(jnp.broadcast_to(_validS2[:, None, :], (2, 2048, 77)), 1, 0).astype(jnp.int32)
        return (x, ctx_1024, mask_BxSxS2_ik1)
    x, ctx_1024, mask_BxSxS2_ik1 = _rec_inputs()

    def _L0_xattn_setup():
        import jax, jax.numpy as jnp
        import numpy as np
        NEG = -9000000000000000.0
        EPS = 1e-05
        key = jax.random.key(seed)
        k1, k2, k3, k4 = jax.random.split(key, 4)
        B, S, D = (4, 1024, 512)
        q = jax.random.normal(k1, (B, S, D), dtype=jnp.float32)
        k = jax.random.normal(k2, (B, S, D), dtype=jnp.float32)
        v = jax.random.normal(k3, (B, S, D), dtype=jnp.float32)
        mask = jax.random.randint(k4, (B, S, S), 0, 2, dtype=jnp.int32)
        gamma = jnp.ones((D,), dtype=jnp.float32)
        beta = jnp.zeros((D,), dtype=jnp.float32)
        return {'q': q, 'k': k, 'v': v, 'mask': mask, 'gamma': gamma, 'beta': beta}
    _L0_xattn_all = _L0_xattn_setup()
    _L0_xattn_in = {k: v for k, v in _L0_xattn_all.items() if k in ('gamma', 'beta')}
    del _L0_xattn_all

    def _L0_ffn_setup():
        import jax, jax.numpy as jnp
        import numpy as np
        D_MODEL = 512
        N_HEADS = 16
        N_KV = 4
        NUM_REP = N_HEADS // N_KV
        HEAD_DIM = D_MODEL // N_HEADS
        N_EXPERTS = 8
        TOP_K = 2
        CAP_FACTOR = 1.25
        EPS_NORM = 1e-06

        def _rmsnorm(x, w):
            var = jnp.mean(x * x, axis=-1, keepdims=True)
            return w * (x * jax.lax.rsqrt(var + EPS_NORM))

        def _gqa(x, qw, qb, kw, kb, vw, vb, ow, ob):
            B, S, D = x.shape
            q = (x @ qw + qb).reshape(B, S, N_HEADS, HEAD_DIM).transpose(0, 2, 1, 3)
            k = (x @ kw + kb).reshape(B, S, N_KV, HEAD_DIM).transpose(0, 2, 1, 3)
            v = (x @ vw + vb).reshape(B, S, N_KV, HEAD_DIM).transpose(0, 2, 1, 3)
            k = jnp.repeat(k, NUM_REP, axis=1)
            v = jnp.repeat(v, NUM_REP, axis=1)
            scores = jnp.einsum('bhqd,bhkd->bhqk', q, k) / np.sqrt(HEAD_DIM).astype(np.float32)
            attn = jax.nn.softmax(scores, axis=-1)
            out = jnp.einsum('bhqk,bhkd->bhqd', attn, v)
            out = out.transpose(0, 2, 1, 3).reshape(B, S, D)
            return out @ ow + ob

        def _moe(x, gate_w, w1, w2):
            B, S, D = x.shape
            T = B * S
            x_flat = x.reshape(T, D)
            capacity = int(CAP_FACTOR * T * TOP_K / N_EXPERTS)
            logits = x_flat @ gate_w
            probs = jax.nn.sigmoid(logits)
            _, sel = jax.lax.top_k(probs, TOP_K)
            w_topk = jnp.take_along_axis(probs, sel, axis=1)
            w_topk = w_topk / (jnp.sum(w_topk, axis=-1, keepdims=True) + 1e-06)
            flat_sel = sel.reshape(-1)
            em = jax.nn.one_hot(flat_sel, N_EXPERTS, dtype=jnp.int32)
            ranks = jnp.take_along_axis(jnp.cumsum(em, axis=0), flat_sel[:, None], axis=1)[:, 0] - 1
            valid = ranks < capacity
            slot = flat_sel * capacity + ranks
            scatter_idx = jnp.where(valid, slot, N_EXPERTS * capacity)
            x_rep = jnp.repeat(x_flat, TOP_K, axis=0)
            padded = jnp.zeros((N_EXPERTS * capacity + 1, D), x.dtype).at[scatter_idx].set(x_rep)
            padded_x = padded[:N_EXPERTS * capacity].reshape(N_EXPERTS, capacity, D)
            h = jax.nn.gelu(jnp.einsum('ecd,edf->ecf', padded_x, w1), approximate=False)
            out_padded = jnp.einsum('ecf,efd->ecd', h, w2).reshape(N_EXPERTS * capacity, D)
            gather_idx = jnp.where(valid, slot, 0)
            out_rep = jnp.where(valid[:, None], out_padded[gather_idx], 0.0)
            out_w = out_rep * w_topk.reshape(-1)[:, None]
            return out_w.reshape(T, TOP_K, D).sum(axis=1).reshape(B, S, D)
        key = jax.random.key(seed)
        ks = jax.random.split(key, 12)
        s = 0.02
        return {'x': jax.random.normal(ks[0], (4, 512, D_MODEL), jnp.float32), 'qw': jax.random.normal(ks[1], (D_MODEL, D_MODEL), jnp.float32) * s, 'qb': jnp.zeros((D_MODEL,), jnp.float32), 'kw': jax.random.normal(ks[2], (D_MODEL, N_KV * HEAD_DIM), jnp.float32) * s, 'kb': jnp.zeros((N_KV * HEAD_DIM,), jnp.float32), 'vw': jax.random.normal(ks[3], (D_MODEL, N_KV * HEAD_DIM), jnp.float32) * s, 'vb': jnp.zeros((N_KV * HEAD_DIM,), jnp.float32), 'ow': jax.random.normal(ks[4], (D_MODEL, D_MODEL), jnp.float32) * s, 'ob': jnp.zeros((D_MODEL,), jnp.float32), 'gate_w': jax.random.normal(ks[5], (D_MODEL, N_EXPERTS), jnp.float32) * s, 'w1': jax.random.normal(ks[6], (N_EXPERTS, D_MODEL, 1024), jnp.float32) * s, 'w2': jax.random.normal(ks[7], (N_EXPERTS, 1024, D_MODEL), jnp.float32) * s, 'norm1_w': jnp.ones((D_MODEL,), jnp.float32), 'norm2_w': jnp.ones((D_MODEL,), jnp.float32)}
    _L0_ffn_all = _L0_ffn_setup()
    _L0_ffn_in = {k: v for k, v in _L0_ffn_all.items() if k in ('qw', 'qb', 'kw', 'kb', 'vw', 'vb', 'ow', 'ob', 'gate_w', 'w1', 'w2', 'norm1_w', 'norm2_w')}
    del _L0_ffn_all
    return {'x': x, 'ctx_1024': ctx_1024, 'mask_BxSxS2_ik1': mask_BxSxS2_ik1, 'L0_xattn_gamma': _L0_xattn_in['gamma'], 'L0_xattn_beta': _L0_xattn_in['beta'], 'L0_ffn_qw': _L0_ffn_in['qw'], 'L0_ffn_qb': _L0_ffn_in['qb'], 'L0_ffn_kw': _L0_ffn_in['kw'], 'L0_ffn_kb': _L0_ffn_in['kb'], 'L0_ffn_vw': _L0_ffn_in['vw'], 'L0_ffn_vb': _L0_ffn_in['vb'], 'L0_ffn_ow': _L0_ffn_in['ow'], 'L0_ffn_ob': _L0_ffn_in['ob'], 'L0_ffn_gate_w': _L0_ffn_in['gate_w'], 'L0_ffn_w1': _L0_ffn_in['w1'], 'L0_ffn_w2': _L0_ffn_in['w2'], 'L0_ffn_norm1_w': _L0_ffn_in['norm1_w'], 'L0_ffn_norm2_w': _L0_ffn_in['norm2_w']}

def reference(x, ctx_1024, mask_BxSxS2_ik1, L0_xattn_gamma, L0_xattn_beta, L0_ffn_qw, L0_ffn_qb, L0_ffn_kw, L0_ffn_kb, L0_ffn_vw, L0_ffn_vb, L0_ffn_ow, L0_ffn_ob, L0_ffn_gate_w, L0_ffn_w1, L0_ffn_w2, L0_ffn_norm1_w, L0_ffn_norm2_w):
    import jax
    import jax.numpy as jnp

    def _L0_xattn_ref(q, k, v, mask, gamma, beta):
        import jax, jax.numpy as jnp
        import numpy as np
        NEG = -9000000000000000.0
        EPS = 1e-05
        d_k = q.shape[-1]
        logits = jnp.einsum('bsd,btd->bst', q, k) / jnp.sqrt(jnp.asarray(d_k, q.dtype))
        logits = jnp.where(mask == 0, jnp.asarray(NEG, logits.dtype), logits)
        attn = jax.nn.softmax(logits, axis=-1)
        x = jnp.einsum('bst,btd->bsd', attn, v)
        mu = jnp.mean(x, axis=-1, keepdims=True)
        var = jnp.mean(jnp.square(x - mu), axis=-1, keepdims=True)
        xhat = (x - mu) * jax.lax.rsqrt(var + EPS)
        return xhat * gamma + beta

    def _L0_ffn_ref(x, qw, qb, kw, kb, vw, vb, ow, ob, gate_w, w1, w2, norm1_w, norm2_w):
        import jax, jax.numpy as jnp
        import numpy as np
        D_MODEL = 512
        N_HEADS = 16
        N_KV = 4
        NUM_REP = N_HEADS // N_KV
        HEAD_DIM = D_MODEL // N_HEADS
        N_EXPERTS = 8
        TOP_K = 2
        CAP_FACTOR = 1.25
        EPS_NORM = 1e-06

        def _rmsnorm(x, w):
            var = jnp.mean(x * x, axis=-1, keepdims=True)
            return w * (x * jax.lax.rsqrt(var + EPS_NORM))

        def _gqa(x, qw, qb, kw, kb, vw, vb, ow, ob):
            B, S, D = x.shape
            q = (x @ qw + qb).reshape(B, S, N_HEADS, HEAD_DIM).transpose(0, 2, 1, 3)
            k = (x @ kw + kb).reshape(B, S, N_KV, HEAD_DIM).transpose(0, 2, 1, 3)
            v = (x @ vw + vb).reshape(B, S, N_KV, HEAD_DIM).transpose(0, 2, 1, 3)
            k = jnp.repeat(k, NUM_REP, axis=1)
            v = jnp.repeat(v, NUM_REP, axis=1)
            scores = jnp.einsum('bhqd,bhkd->bhqk', q, k) / np.sqrt(HEAD_DIM).astype(np.float32)
            attn = jax.nn.softmax(scores, axis=-1)
            out = jnp.einsum('bhqk,bhkd->bhqd', attn, v)
            out = out.transpose(0, 2, 1, 3).reshape(B, S, D)
            return out @ ow + ob

        def _moe(x, gate_w, w1, w2):
            B, S, D = x.shape
            T = B * S
            x_flat = x.reshape(T, D)
            capacity = int(CAP_FACTOR * T * TOP_K / N_EXPERTS)
            logits = x_flat @ gate_w
            probs = jax.nn.sigmoid(logits)
            _, sel = jax.lax.top_k(probs, TOP_K)
            w_topk = jnp.take_along_axis(probs, sel, axis=1)
            w_topk = w_topk / (jnp.sum(w_topk, axis=-1, keepdims=True) + 1e-06)
            flat_sel = sel.reshape(-1)
            em = jax.nn.one_hot(flat_sel, N_EXPERTS, dtype=jnp.int32)
            ranks = jnp.take_along_axis(jnp.cumsum(em, axis=0), flat_sel[:, None], axis=1)[:, 0] - 1
            valid = ranks < capacity
            slot = flat_sel * capacity + ranks
            scatter_idx = jnp.where(valid, slot, N_EXPERTS * capacity)
            x_rep = jnp.repeat(x_flat, TOP_K, axis=0)
            padded = jnp.zeros((N_EXPERTS * capacity + 1, D), x.dtype).at[scatter_idx].set(x_rep)
            padded_x = padded[:N_EXPERTS * capacity].reshape(N_EXPERTS, capacity, D)
            h = jax.nn.gelu(jnp.einsum('ecd,edf->ecf', padded_x, w1), approximate=False)
            out_padded = jnp.einsum('ecf,efd->ecd', h, w2).reshape(N_EXPERTS * capacity, D)
            gather_idx = jnp.where(valid, slot, 0)
            out_rep = jnp.where(valid[:, None], out_padded[gather_idx], 0.0)
            out_w = out_rep * w_topk.reshape(-1)[:, None]
            return out_w.reshape(T, TOP_K, D).sum(axis=1).reshape(B, S, D)
        src = x + _gqa(x, qw, qb, kw, kb, vw, vb, ow, ob)
        src = _rmsnorm(src, norm1_w)
        src = src + _moe(src, gate_w, w1, w2)
        return _rmsnorm(src, norm2_w)
    x = x + _L0_xattn_ref(_layernorm(x, axis=-1), ctx_1024, ctx_1024, mask_BxSxS2_ik1, L0_xattn_gamma, L0_xattn_beta)
    x = x + _L0_ffn_ref(_layernorm(x, axis=-1), L0_ffn_qw, L0_ffn_qb, L0_ffn_kw, L0_ffn_kb, L0_ffn_vw, L0_ffn_vb, L0_ffn_ow, L0_ffn_ob, L0_ffn_gate_w, L0_ffn_w1, L0_ffn_w2, L0_ffn_norm1_w, L0_ffn_norm2_w)
    return x

_drawn_inputs = setup_inputs


def setup_inputs(seed=0):
    import zlib

    import numpy as np

    out = dict(_drawn_inputs(seed))
    spreads = {'L0_xattn_gamma': (1.0, 0.2),
     'L0_xattn_beta': (0.0, 0.1),
     'L0_ffn_qb': (0.0, 0.8),
     'L0_ffn_kb': (0.0, 0.8),
     'L0_ffn_vb': (0.0, 0.392),
     'L0_ffn_ob': (0.0, 0.1),
     'L0_ffn_norm1_w': (1.0, 0.2),
     'L0_ffn_norm2_w': (1.0, 0.2)}
    factors = {'L0_ffn_qw': 8.0, 'L0_ffn_kw': 8.0}
    for name, (base, spread) in spreads.items():
        noise = np.random.default_rng([zlib.crc32(name.encode()), seed]).standard_normal(out[name].shape)
        drawn = base * np.exp(spread * noise) if base else spread * noise
        out[name] = jnp.asarray(drawn.astype(out[name].dtype))
    for name, factor in factors.items():
        out[name] = (out[name] * factor).astype(out[name].dtype)
    return out
```

```python
from contextlib import ExitStack

import concourse.bass as bass
from concourse import mybir

F32 = mybir.dt.float32
F32R = mybir.dt.float32r
I32 = mybir.dt.int32
U32 = mybir.dt.uint32
ALU = mybir.AluOpType
ACT = mybir.ActivationFunctionType
AXX = mybir.AxisListType.X

P = 128
B, S, D = 2, 2048, 512
N = B * S
CT = 77
DK = D // P
H, KV, HD = 16, 4, 32
G = H // KV
CH = 512
TT = CH // P
NC = N // CH
CB = S // CH
KT = S // P
E, F = 8, 1024
CAP = int(1.25 * N * 2 / E)
NEG = -9e15
LN_EPS = 1e-5
RMS_EPS = 1e-6


class Scope:

    def __init__(self, nc, tag):
        self.nc, self.tag, self.stack = nc, tag, ExitStack()

    def __enter__(self):
        self.stack.__enter__()
        return self

    def __exit__(self, *a):
        return self.stack.__exit__(*a)

    def sb(self, name, shape, dt=F32):
        return self.stack.enter_context(self.nc.sbuf_tensor(f"{self.tag}_{name}", shape, dt))

    def ps(self, name, shape, dt=F32):
        return self.stack.enter_context(self.nc.psum_tensor(f"{self.tag}_{name}", shape, dt))

    def sem(self, name):
        return self.stack.enter_context(self.nc.semaphore(f"{self.tag}_{name}"))

    def block(self):
        return self.stack.enter_context(self.nc.Block())


def f32(ap):
    return ap.bitcast(F32)


def mm3(nc, out, ah, al, bh, bl, start, stop):
    nc.tensor.matmul(out, ah, bh, start=start, stop=False)
    nc.tensor.matmul(out, ah, bl, start=False, stop=False)
    return nc.tensor.matmul(out, al, bh, start=False, stop=stop)


def make_identity(nc, pool, ident, ident_zero, ident_made):
    nc.gpsimd.memset(ident[:], 0.0).then_inc(ident_zero, 1)
    pool.wait_ge(ident_zero, 1)
    nc.gpsimd.affine_select(out=ident[:], in_=ident[:], compare_op=ALU.not_equal, fill=1.0, base=0,
                            pattern=[[-1, P]], channel_multiplier=1).then_inc(ident_made, 1)


def over_rows(ap, rows=P):
    return ap.rearrange("(a n) -> a n", a=1).broadcast_to((rows, ap.shape[0]))


def phase_project(nc, x, ctx, mask, gamma, beta, qw, qb, kw, kb, vw, vb, x1_d, y_d, qh_d, ql_d, kh_d, kl_d, v_d):
    NM = KV + 1
    with Scope(nc, "p1") as s:
        ident = s.sb("ident", [P, P])
        w_raw = s.sb("w_raw", [P, DK, D + 2 * P])
        w_hi = s.sb("w_hi", [P, DK, D + 2 * P], F32R)
        w_lo = s.sb("w_lo", [P, DK, D + 2 * P], F32R)
        b_col = s.sb("b_col", [P, NM])
        vb_row = s.sb("vb_row", [P, P])
        gamma_row = s.sb("gamma_row", [P, D])
        beta_row = s.sb("beta_row", [P, D])
        ctx_n = s.sb("ctx_n", [CT, B, D])
        ctx_t = s.sb("ctx_t", [P, B, DK, CT])
        X = s.sb("X", [P, TT, D])
        MK = s.sb("MK", [P, TT, CT], I32)
        pen = s.sb("pen", [P, TT, CT])
        qn = s.sb("qn", [P, TT, D])
        qT = s.sb("qT", [P, DK, CH])
        lg = s.sb("lg", [P, TT, CT])
        pr = s.sb("pr", [P, TT, CT])
        prT = s.sb("prT", [CT, CH])
        att = s.sb("att", [P, TT, D])
        xb = s.sb("xb", [P, TT, D])
        x1 = s.sb("x1", [P, TT, D])
        y = s.sb("y", [P, TT, D])
        yTh = s.sb("yTh", [P, DK, CH], F32R)
        yTl = s.sb("yTl", [P, DK, CH], F32R)
        hi = s.sb("hi", [P, NM, CH], F32R)
        lo = s.sb("lo", [P, NM, CH], F32R)
        val = s.sb("val", [P, TT, P])
        stats = s.sb("stats", [P, 3, TT, 6])
        mv = s.sb("mv", [P, 3, TT, 2])
        var = s.sb("var", [P, 3, TT])
        rstd = s.sb("rstd", [P, 3, TT])
        half = s.sb("half", [P, TT])
        mx = s.sb("mx", [P, TT])
        nmx = s.sb("nmx", [P, TT])
        psum_e = s.sb("psum_e", [P, TT])
        rinv = s.sb("rinv", [P, TT])
        vr = s.sb("vr", [P, TT])
        s2 = s.sb("s2", [P, TT])
        ps_t = s.ps("ps_t", [P, 2, CH])
        ps_lg = s.ps("ps_lg", [P, TT, P])
        ps_pt = s.ps("ps_pt", [P, CH])
        ps_o = s.ps("ps_o", [P, 2, CH])
        ps_pj = s.ps("ps_pj", [P, 2, CH])

        w_in, ctx_in, vec_in = s.sem("w_in"), s.sem("ctx_in"), s.sem("vec_in")
        ident_zero, ident_made, half_made = s.sem("ident_zero"), s.sem("ident_made"), s.sem("half_made")
        wh_made, wl_made = s.sem("wh_made"), s.sem("wl_made")
        ctx_tr, ctx_t_made = s.sem("ctx_tr"), s.sem("ctx_t_made")
        x_in, mask_in = s.sem("x_in"), s.sem("mask_in")
        stat = [s.sem(f"stat{i}") for i in range(3)]
        aggr = [s.sem(f"aggr{i}") for i in range(3)]
        vared = [s.sem(f"vared{i}") for i in range(3)]
        rs = [s.sem(f"rs{i}") for i in range(3)]
        qn_made, q_tr, qT_made, lg_mm, pen_made = (s.sem(n) for n in ("qn_made", "q_tr", "qT_made", "lg_mm", "pen_made"))
        lg_made, mx_made, nmx_made, pr_made, p_tr = (s.sem(n) for n in ("lg_made", "mx_made", "nmx_made", "pr_made", "p_tr"))
        prT_made, o_mm, att_made, rinv_made = (s.sem(n) for n in ("prT_made", "o_mm", "att_made", "rinv_made"))
        vr1, s2_made, att_n, att_g = (s.sem(n) for n in ("vr1", "s2_made", "att_n", "att_g"))
        xb_made, x1_made, y_made, y_tr = (s.sem(n) for n in ("xb_made", "x1_made", "y_made", "y_tr"))
        yh_made, yl_made, pj_mm, hi_made, pj_out = (s.sem(n) for n in ("yh_made", "yl_made", "pj_mm", "hi_made", "pj_out"))
        x1_st, y_st, q_st, k_st, v_st = (s.sem(n) for n in ("x1_st", "y_st", "q_st", "k_st", "v_st"))
        gate_sem = s.sem("gate")
        block = s.block()

        def gate(eng):
            eng.sem_inc(gate_sem, 1)

        @block.sync
        def _(sp):
            sp.dma_start(w_raw[:, :, 0:D], qw.rearrange("(k p) n -> p k n", p=P)).then_inc(w_in, 16)
            sp.dma_start(w_raw[:, :, D:D + P], kw.rearrange("(k p) n -> p k n", p=P)).then_inc(w_in, 16)
            sp.dma_start(w_raw[:, :, D + P:], vw.rearrange("(k p) n -> p k n", p=P)).then_inc(w_in, 16)

            def load(c):
                sp.dma_start(X[:], x[bass.ds(c, 1)].rearrange("a (t p) d -> p (a t) d", p=P)).then_inc(x_in, 16)
                sp.dma_start(MK[:], mask[bass.ds(c, 1)].rearrange("a (t p) n -> p (a t) n", p=P)).then_inc(mask_in, 16)

            def store_first(c, tiles):
                sp.wait_ge(x1_made, tiles)
                gate(sp)
                sp.dma_start(x1_d[bass.ds(c, 1)].rearrange("a (t p) d -> p (a t) d", p=P), x1[:]).then_inc(x1_st, 16)
                sp.wait_ge(y_made, tiles)
                gate(sp)
                sp.dma_start(y_d[bass.ds(c, 1)].rearrange("a (t p) d -> p (a t) d", p=P), y[:]).then_inc(y_st, 16)

            def store_second(c, n):
                sp.wait_ge(pj_out, n)
                gate(sp)
                sp.dma_start(qh_d[bass.ds(c, 1)].rearrange("a (g p) q -> p (a g) q", p=P), f32(hi[:, 0:KV, :])).then_inc(q_st, 16)
                sp.dma_start(ql_d[bass.ds(c, 1)].rearrange("a (g p) q -> p (a g) q", p=P), f32(lo[:, 0:KV, :])).then_inc(q_st, 16)
                sp.dma_start(kh_d[bass.ds(c, 1)].rearrange("a p q -> p (a q)"), f32(hi[:, KV, :])).then_inc(k_st, 16)
                sp.dma_start(kl_d[bass.ds(c, 1)].rearrange("a p q -> p (a q)"), f32(lo[:, KV, :])).then_inc(k_st, 16)
                sp.dma_start(v_d[bass.ds(c, 1)].rearrange("a (t p) n -> p (a t) n", p=P), val[:]).then_inc(v_st, 16)

            load(0)
            sp.wait_ge(qn_made, TT)
            sp.wait_ge(xb_made, 1)
            sp.wait_ge(pen_made, 1)
            load(1)
            store_first(0, TT)
            with sp.Fori(1, NC - 1) as i:
                nxt, prev = sp.snap(i + 1), sp.snap(i - 1)
                one_n, out_n = sp.snap(i + 1), sp.snap(i * (NM + 1))
                tiles_n = sp.snap(i * TT + TT)
                sp.wait_ge(qn_made, tiles_n)
                gate(sp)
                sp.wait_ge(xb_made, one_n)
                gate(sp)
                sp.wait_ge(pen_made, one_n)
                gate(sp)
                load(nxt)
                store_second(prev, out_n)
                store_first(i, tiles_n)
            store_second(NC - 2, (NC - 1) * (NM + 1))
            store_first(NC - 1, NC * TT)
            store_second(NC - 1, NC * (NM + 1))
            for sem, n in ((x1_st, NC), (y_st, NC), (q_st, 2 * NC), (k_st, 2 * NC), (v_st, NC), (x_in, NC), (mask_in, NC)):
                sp.wait_ge(sem, 16 * n)

        @block.gpsimd
        def _(pool):
            make_identity(nc, pool, ident, ident_zero, ident_made)
            nc.gpsimd.memset(half[:], -0.5).then_inc(half_made, 1)
            pool.wait_ge(half_made, 1)

            def power(j, c, src):
                gate(pool)
                nc.gpsimd.tensor_scalar(var[:, j, :], src, LN_EPS, None, ALU.add).then_inc(vared[j], 1)
                pool.wait_ge(vared[j], c + 1)
                nc.gpsimd.tensor_tensor(rstd[:, j, :], var[:, j, :], half[:], ALU.pow).then_inc(rs[j], 1)

            def chunk(c, first=False):
                pool.wait_ge(aggr[0], TT * c + TT)
                power(0, c, mv[:, 0, :, 1])
                pool.wait_ge(x_in, 16 * c + 16)
                if not first:
                    pool.wait_ge(x1_made, TT * c)
                for t in range(TT):
                    last = nc.gpsimd.tensor_tensor(xb[:, t, :], X[:, t, :], beta_row[:], ALU.add)
                last.then_inc(xb_made, 1)
                pool.wait_ge(vr1, 2 * c + 2)
                power(1, c, vr[:])
                pool.wait_ge(xb_made, c + 1)
                if not first:
                    pool.wait_ge(x1_st, 16 * c)
                    pool.wait_ge(y_made, TT * c)
                for t in range(TT):
                    pool.wait_ge(att_n, TT * c + t + 1)
                    nc.gpsimd.tensor_tensor(att[:, t, :], att[:, t, :], gamma_row[:], ALU.mult).then_inc(att_g, 1)
                    pool.wait_ge(att_g, TT * c + t + 1)
                    nc.gpsimd.tensor_tensor(x1[:, t, :], att[:, t, :], xb[:, t, :], ALU.add).then_inc(x1_made, 1)
                pool.wait_ge(aggr[2], TT * c + TT)
                power(2, c, mv[:, 2, :, 1])

            pool.wait_ge(vec_in, 16 * 7)
            chunk(0, first=True)
            with pool.Fori(1, NC) as i:
                chunk(i)

        @block.scalar
        def _(act):
            act.dma_start(ctx_n[:], ctx.rearrange("b r d -> r b d")).then_inc(ctx_in, 16)
            act.dma_start(gamma_row[:], over_rows(gamma)).then_inc(vec_in, 16)
            act.dma_start(beta_row[:], over_rows(beta)).then_inc(vec_in, 16)
            act.dma_start(vb_row[:], over_rows(vb)).then_inc(vec_in, 16)
            qb_v = qb.rearrange("(g p a) -> g p a", p=P, a=1)
            for g in range(KV):
                act.dma_start(b_col[:, g:g + 1], qb_v[g]).then_inc(vec_in, 16)
            act.dma_start(b_col[:, KV:NM], kb.rearrange("(p a) -> p a", a=1)).then_inc(vec_in, 16)
            act.wait_ge(ctx_tr, 1)
            nc.scalar.activation(ctx_t[:, 0, :, :], ps_t[:, 0, 0:DK * P].rearrange("p (k n) -> p k n", k=DK)[:, :, 0:CT], ACT.Copy).then_inc(ctx_t_made, 1)
            act.wait_ge(ctx_tr, 2)
            nc.scalar.activation(ctx_t[:, 1, :, :], ps_t[:, 1, 0:DK * P].rearrange("p (k n) -> p k n", k=DK)[:, :, 0:CT], ACT.Copy).then_inc(ctx_t_made, 1)
            act.wait_ge(w_in, 48)
            for k in range(DK):
                nc.scalar.activation(w_hi[:, k, :], w_raw[:, k, :], ACT.Copy).then_inc(wh_made, 1)
            act.wait_ge(vec_in, 16 * 8)

            def first_part(c, first=False):
                for k in range(DK):
                    act.wait_ge(q_tr, DK * c + k + 1)
                    if not first:
                        act.wait_ge(lg_mm, c)
                    nc.scalar.activation(qT[:, k, :], ps_t[:, k % 2, :], ACT.Copy).then_inc(qT_made, 1)
                act.wait_ge(nmx_made, c + 1)
                if not first:
                    act.wait_ge(p_tr, c)
                    act.wait_ge(rinv_made, c)
                for t in range(TT):
                    nc.scalar.activation(pr[:, t, :], lg[:, t, :], ACT.Exp, bias=nmx[:, t:t + 1],
                                         accum_out=psum_e[:, t:t + 1]).then_inc(pr_made, 1)

            def first_end(c, first=False):
                act.wait_ge(p_tr, c + 1)
                if not first:
                    act.wait_ge(o_mm, TT * c)
                nc.scalar.activation(prT[:], ps_pt[0:CT, :], ACT.Copy).then_inc(prT_made, 1)
                if not first:
                    act.wait_ge(x1_made, TT * c)
                for t in range(TT):
                    act.wait_ge(o_mm, TT * c + t + 1)
                    nc.scalar.activation(att[:, t, :], ps_o[:, t % 2, :], ACT.Copy).then_inc(att_made, 1)

            def second_high(c, first=False):
                if not first:
                    act.wait_ge(pj_mm, (NM + 1) * c)
                for k in range(DK):
                    act.wait_ge(y_tr, DK * c + k + 1)
                    nc.scalar.activation(yTh[:, k, :], ps_t[:, k % 2, :], ACT.Copy).then_inc(yh_made, 1)

            def second_project(c, ms, first=False):
                for m in ms:
                    if not first and m == 0:
                        act.wait_ge(q_st, 32 * c)
                        act.wait_ge(k_st, 32 * c)
                    act.wait_ge(pj_mm, (NM + 1) * c + m + 1)
                    nc.scalar.activation(hi[:, m, :], ps_pj[:, m % 2, :], ACT.Identity, bias=b_col[:, m:m + 1]).then_inc(hi_made, 1)

            first_part(0, first=True)
            first_end(0, first=True)
            first_part(1)
            second_high(0, first=True)
            second_project(0, range(2), first=True)
            first_end(1)
            second_project(0, range(2, NM), first=True)
            with act.Fori(2, NC) as i:
                first_part(i)
                second_high(i - 1)
                second_project(i - 1, range(2))
                first_end(i)
                second_project(i - 1, range(2, NM))
            second_high(NC - 1)
            second_project(NC - 1, range(NM))

        @block.vector
        def _(dve):
            dve.wait_ge(w_in, 48)
            for k in range(DK):
                dve.wait_ge(wh_made, k + 1)
                nc.vector.tensor_tensor(w_lo[:, k, :], w_raw[:, k, :], f32(w_hi[:, k, :]), ALU.subtract).then_inc(wl_made, 1)
            dve.wait_ge(vec_in, 16 * 8)

            def moments(j, c, src, ready=None):
                for t in range(TT):
                    if ready is not None:
                        dve.wait_ge(ready, TT * c + t + 1)
                    nc.vector.bn_stats(stats[:, j, t, :], src[:, t, :]).then_inc(stat[j], 1)
                dve.wait_ge(stat[j], TT * c + TT)
                gate(dve)
                for t in range(TT):
                    nc.vector.bn_aggr(mv[:, j, t, :], stats[:, j, t, :]).then_inc(aggr[j], 1)

            def head(c, first=False):
                dve.wait_ge(x_in, 16 * c + 16)
                moments(0, c, X)
                dve.wait_ge(aggr[0], TT * c + TT)
                dve.wait_ge(mask_in, 16 * c + 16)
                if not first:
                    dve.wait_ge(lg_made, c)
                nc.vector.tensor_scalar(pen[:], MK[:], 0, NEG, ALU.is_equal, ALU.mult).then_inc(pen_made, 1)
                dve.wait_ge(rs[0], c + 1)
                if not first:
                    dve.wait_ge(q_tr, DK * c)
                for t in range(TT):
                    nc.vector.tensor_scalar(qn[:, t, :], X[:, t, :], mv[:, 0, t, 0:1], rstd[:, 0, t:t + 1],
                                            ALU.subtract, ALU.mult).then_inc(qn_made, 1)

            def softmax(c, first=False):
                dve.wait_ge(lg_mm, c + 1)
                dve.wait_ge(pen_made, c + 1)
                if not first:
                    dve.wait_ge(pr_made, TT * c)
                nc.vector.scalar_tensor_tensor(lg[:], ps_lg[:, :, 0:CT], float(D) ** -0.5, pen[:], ALU.mult, ALU.add).then_inc(lg_made, 1)
                dve.wait_ge(lg_made, c + 1)
                nc.vector.reduce_max(mx[:], lg[:], AXX).then_inc(mx_made, 1)
                dve.wait_ge(mx_made, c + 1)
                nc.vector.tensor_scalar(nmx[:], mx[:], -1.0, None, ALU.mult).then_inc(nmx_made, 1)

            def tail(c, first=False):
                dve.wait_ge(pr_made, TT * c + TT)
                nc.vector.reciprocal(rinv[:], psum_e[:]).then_inc(rinv_made, 1)
                moments(1, c, att, att_made)
                dve.wait_ge(aggr[1], TT * c + TT)
                dve.wait_ge(rinv_made, c + 1)
                nc.vector.tensor_tensor(vr[:], mv[:, 1, :, 1], rinv[:], ALU.mult).then_inc(vr1, 1)
                dve.wait_ge(vr1, 2 * c + 1)
                nc.vector.tensor_tensor(vr[:], vr[:], rinv[:], ALU.mult).then_inc(vr1, 1)
                dve.wait_ge(rs[1], c + 1)
                nc.vector.tensor_tensor(s2[:], rstd[:, 1, :], rinv[:], ALU.mult).then_inc(s2_made, 1)
                dve.wait_ge(s2_made, c + 1)
                for t in range(TT):
                    nc.vector.tensor_scalar(att[:, t, :], att[:, t, :], mv[:, 1, t, 0:1], s2[:, t:t + 1],
                                            ALU.subtract, ALU.mult).then_inc(att_n, 1)
                moments(2, c, x1, x1_made)
                dve.wait_ge(aggr[2], TT * c + TT)
                dve.wait_ge(rs[2], c + 1)
                if not first:
                    dve.wait_ge(y_tr, DK * c)
                    dve.wait_ge(y_st, 16 * c)
                for t in range(TT):
                    nc.vector.tensor_scalar(y[:, t, :], x1[:, t, :], mv[:, 2, t, 0:1], rstd[:, 2, t:t + 1],
                                            ALU.subtract, ALU.mult).then_inc(y_made, 1)

            def second_low(c, first=False):
                for k in range(DK):
                    dve.wait_ge(yh_made, DK * c + k + 1)
                    nc.vector.tensor_tensor(yTl[:, k, :], ps_t[:, k % 2, :], f32(yTh[:, k, :]), ALU.subtract).then_inc(yl_made, 1)

            def second_project(c, ms, first=False):
                for m in ms:
                    if not first and m == 0:
                        dve.wait_ge(q_st, 32 * c)
                        dve.wait_ge(k_st, 32 * c)
                        dve.wait_ge(v_st, 16 * c)
                    if m < NM:
                        dve.wait_ge(hi_made, NM * c + m + 1)
                        nc.vector.scalar_tensor_tensor(lo[:, m, :], ps_pj[:, m % 2, :], b_col[:, m:m + 1], f32(hi[:, m, :]),
                                                       ALU.add, ALU.subtract).then_inc(pj_out, 1)
                    else:
                        dve.wait_ge(pj_mm, (NM + 1) * c + m + 1)
                        nc.vector.tensor_tensor(val[:], ps_pj[:, m % 2, :].rearrange("p (t n) -> p t n", t=TT),
                                                vb_row[:].rearrange("p (a n) -> p a n", a=1).broadcast_to((P, TT, P)),
                                                ALU.add).then_inc(pj_out, 1)

            head(0, first=True)
            softmax(0, first=True)
            tail(0, first=True)
            head(1)
            softmax(1)
            second_low(0, first=True)
            second_project(0, range(2), first=True)
            tail(1)
            second_project(0, range(2, NM + 1), first=True)
            with dve.Fori(2, NC) as i:
                head(i)
                softmax(i)
                second_low(i - 1)
                second_project(i - 1, range(2))
                tail(i)
                second_project(i - 1, range(2, NM + 1))
            second_low(NC - 1)
            second_project(NC - 1, range(NM + 1))

        @block.tensor
        def _(pe):
            pe.wait_ge(ident_made, 1)
            pe.wait_ge(ctx_in, 16)
            for b in range(B):
                for k in range(DK):
                    last = nc.tensor.transpose(ps_t[:, b, k * P:k * P + CT], ctx_n[:, b, k * P:(k + 1) * P], ident[0:CT, 0:CT])
                last.then_inc(ctx_tr, 1)
            pe.wait_ge(ctx_t_made, 2)
            pe.wait_ge(wl_made, DK)

            def transposes(c, src, ready, done, evacuated):
                pe.wait_ge(ready, TT * c + TT)
                for k in range(DK):
                    if k >= 2:
                        pe.wait_ge(evacuated, DK * c + k - 1)
                    for t in range(TT):
                        last = nc.tensor.transpose(ps_t[:, k % 2, t * P:(t + 1) * P], src[:, t, k * P:(k + 1) * P], ident[:])
                    last.then_inc(done, 1)

            def first_part(c, first=False):
                transposes(c, qn, qn_made, q_tr, qT_made)
                pe.wait_ge(qT_made, DK * c + DK)
                if not first:
                    pe.wait_ge(lg_made, c)
                for t in range(TT):
                    for k in range(DK):
                        last = nc.tensor.matmul(ps_lg[:, t, 0:CT], qT[:, k, t * P:(t + 1) * P], ctx_t[:, batch(c), k, :].rearrange("p a n -> p (a n)"),
                                                start=(k == 0), stop=(k == DK - 1))
                last.then_inc(lg_mm, 1)

            def batch(c):
                return slice(0, 1) if isinstance(c, int) else bass.ds(c // CB, 1)

            def first_end(c, first=False):
                pe.wait_ge(pr_made, TT * c + TT)
                if not first:
                    pe.wait_ge(prT_made, c)
                for t in range(TT):
                    last = nc.tensor.transpose(ps_pt[0:CT, t * P:(t + 1) * P], pr[:, t, :], ident[:])
                last.then_inc(p_tr, 1)
                pe.wait_ge(prT_made, c + 1)
                for t in range(TT):
                    if not first or t >= 2:
                        pe.wait_ge(att_made, TT * c + t - 1)
                    nc.tensor.matmul(ps_o[:, t % 2, :], prT[:, t * P:(t + 1) * P], ctx_n[:, batch(c), :].rearrange("p a n -> p (a n)"),
                                     start=True, stop=True).then_inc(o_mm, 1)

            def second_transposes(c):
                transposes(c, y, y_made, y_tr, yl_made)
                pe.wait_ge(yl_made, DK * c + DK)

            def second_project(c, ms, first=False):
                for m in ms:
                    if not first or m >= 2:
                        pe.wait_ge(pj_out, (NM + 1) * c + m - 1)
                    if m < NM:
                        for k in range(DK):
                            cols = slice(m * P, (m + 1) * P)
                            last = mm3(nc, ps_pj[:, m % 2, :], w_hi[:, k, cols], w_lo[:, k, cols], yTh[:, k, :], yTl[:, k, :],
                                       k == 0, k == DK - 1)
                    else:
                        for t in range(TT):
                            for k in range(DK):
                                toks = slice(t * P, (t + 1) * P)
                                last = mm3(nc, ps_pj[:, m % 2, toks], yTh[:, k, toks], yTl[:, k, toks],
                                           w_hi[:, k, D + P:], w_lo[:, k, D + P:], k == 0, k == DK - 1)
                    last.then_inc(pj_mm, 1)

            first_part(0, first=True)
            first_end(0, first=True)
            first_part(1)
            second_transposes(0)
            second_project(0, range(2), first=True)
            first_end(1)
            second_project(0, range(2, NM + 1), first=True)
            with pe.Fori(2, NC) as i:
                first_part(i)
                second_transposes(i - 1)
                second_project(i - 1, range(2))
                first_end(i)
                second_project(i - 1, range(2, NM + 1))
            second_transposes(NC - 1)
            second_project(NC - 1, range(NM + 1))


def phase_attend(nc, y_d, qh_d, ql_d, kh_d, kl_d, v_d, ow, ob, norm1, gate_w, src_d, xe_d, slot_d, wt_d):
    BK = 3
    A_PER = 5
    NA = G * TT * (S // CH)
    NSC = G * KT
    PAIRS = KT // 2
    SCALE = float(HD) ** -0.5
    ROUTES, ROUTE_TOP = 23, 4
    ZR = 4
    NZ = E * CAP // (P * ZR)
    with Scope(nc, "p2") as s:
        ident = s.sb("ident", [P, P])
        ones = s.sb("ones", [P, P])
        before = s.sb("before", [P, P])
        ow_hi = s.sb("ow_hi", [P, KV, D], F32R)
        ow_lo = s.sb("ow_lo", [P, KV, D], F32R)
        ob_row = s.sb("ob_row", [P, D])
        norm_row = s.sb("norm_row", [P, D])
        gw = s.sb("gw", [P, DK, E])
        iota_e = s.sb("iota_e", [P, E])
        ecap = s.sb("ecap", [P, E])
        KS = s.sb("KS", [98, KV, S], F32R)
        QS = s.sb("QS", [98, KV, G, CH], F32R)
        VS = s.sb("VS", [P, KV, KT, HD])
        PR = s.sb("PR", [P, 4, G, CH])
        PP = s.sb("PP", [P, 2, G, CH])
        mxp = s.sb("mxp", [P, TT * G, S // CH])
        mxv = s.sb("mxv", [P, TT, G])
        mh = s.sb("mh", [G, CH], F32R)
        ml = s.sb("ml", [G, CH], F32R)
        pvs = s.sb("pvs", [P, CH])
        rec = s.sb("rec", [P, CH])
        at_hi = s.sb("at_hi", [P, KV, CH], F32R)
        at_lo = s.sb("at_lo", [P, KV, CH], F32R)
        Y = s.sb("Y", [P, TT, D])
        SR = s.sb("SR", [P, TT, D])
        srT = s.sb("srT", [P, TT, DK, P])
        sq = s.sb("sq", [P, D])
        ss = s.sb("ss", [P, TT])
        sv = s.sb("sv", [P, TT])
        sr_rstd = s.sb("sr_rstd", [P, TT])
        half = s.sb("half", [P, TT])
        lgt = s.sb("lgt", [P, TT, E])
        top = s.sb("top", [P, TT, 8])
        topi = s.sb("topi", [P, TT, 8], U32)
        topf = s.sb("topf", [P, TT, 2])
        oh = s.sb("oh", [P, 2, TT, E])
        sel = s.sb("sel", [P, TT, E])
        pe_ = s.sb("pe_", [P, TT, 2])
        wsum = s.sb("wsum", [P, TT])
        prefix = s.sb("prefix", [P, TT, E])
        base = s.sb("base", [P, TT + 1, E])
        total = s.sb("total", [P, TT, E])
        room = s.sb("room", [P, TT, E])
        prod = s.sb("prod", [P, TT, E])
        slot = s.sb("slot", [P, 2, TT])
        ok = s.sb("ok", [P, 2, TT])
        far = s.sb("far", [P, 2, TT])
        to_slot = s.sb("to_slot", [P, 2, TT], I32)
        from_slot = s.sb("from_slot", [P, 2, TT], I32)
        wt = s.sb("wt", [P, 2, TT])
        ps_a = s.ps("ps_a", [P, 2, CH])
        ps_b = s.ps("ps_b", [P, BK, CH])
        ps_pv = s.ps("ps_pv", [P, CH])
        ps_den = s.ps("ps_den", [P, CH])
        ps_m = s.ps("ps_m", [P, CH])

        (const_in, ident_zero, ident_made, const_made, owh_made, owl_made, zero_made, zero_st) = (
            s.sem(n) for n in ("const_in", "ident_zero", "ident_made", "const_made", "owh_made", "owl_made", "zero_made", "zero_st"))
        q_in = [s.sem(f"q_in{g}") for g in range(KV)]
        v_in = [s.sem(f"v_in{g}") for g in range(KV)]
        m_in = s.sem("m_in")
        a_mm, mxp_made, mxv_made, m_tr, mh_made, ml_made = (s.sem(n) for n in ("a_mm", "mxp_made", "mxv_made", "m_tr", "mh_made", "ml_made"))
        sc_mm, ex_made, pair_made, pv_mm, den_mm = (s.sem(n) for n in ("sc_mm", "ex_made", "pair_made", "pv_mm", "den_mm"))
        pvs_made, rec_made, att_made, ath_made, atl_made = (s.sem(n) for n in ("pvs_made", "rec_made", "att_made", "ath_made", "atl_made"))
        y_in, yob_made, o_mm, src_made, ss_made, sv_made, rstd_made = (s.sem(n) for n in ("y_in", "yob_made", "o_mm", "src_made", "ss_made", "sv_made", "rstd_made"))
        sn_made, sr_made, sr_tr, srT_made, g_mm, lgt_made = (s.sem(n) for n in ("sn_made", "sr_made", "sr_tr", "srT_made", "g_mm", "lgt_made"))
        route, exp_made, sel_made, rank_mm, ranked, slots_made = (s.sem(n) for n in ("route", "exp_made", "sel_made", "rank_mm", "ranked", "slots_made"))
        src_st, slot_st, wt_st, sent, gate_sem = (s.sem(n) for n in ("src_st", "slot_st", "wt_st", "sent", "gate"))
        picked, dve_const = s.sem("picked"), s.sem("dve_const")
        block = s.block()

        def gate(eng):
            eng.sem_inc(gate_sem, 1)

        def unit(c, g):
            return KV * c + g

        @block.sync
        def _(sp):
            def hold(sem, n):
                sp.wait_ge(sem, n)
                gate(sp)

            ow_raw = PR[:, 0, :, :]
            sp.dma_start(ow_raw, ow.rearrange("(g p) n -> p g n", p=P)).then_inc(const_in, 16)
            sp.dma_start(ob_row[:], over_rows(ob)).then_inc(const_in, 16)
            sp.dma_start(norm_row[:], over_rows(norm1)).then_inc(const_in, 16)
            sp.dma_start(gw[:], gate_w.rearrange("(k p) e -> p k e", p=P)).then_inc(const_in, 16)

            def load(c, g):
                row = c // CB * CB
                heads = slice(G * HD * g, G * HD * (g + 1))
                for part, src in ((0, qh_d), (1, qh_d), (2, ql_d)):
                    sp.dma_start(f32(QS[32 * part:32 * part + 32, g, :, :]),
                                 src[bass.ds(c, 1), heads, :].rearrange("a (j d) q -> d (a j) q", d=HD)).then_inc(q_in[g], 16)
                for part, src in ((0, kh_d), (1, kl_d), (2, kh_d)):
                    sp.dma_start(f32(KS[32 * part:32 * part + 32, g, :]).rearrange("d (n q) -> d n q", n=CB),
                                 src[bass.ds(row, CB), HD * g:HD * (g + 1), :].rearrange("n d q -> d n q")).then_inc(q_in[g], 16)
                sp.dma_start(VS[:, g, :, :].rearrange("p (n t) d -> p n t d", n=CB),
                             v_d[bass.ds(row, CB), :, HD * g:HD * (g + 1)].rearrange("n (t p) d -> p n t d", p=P)).then_inc(v_in[g], 16)

            def load_y(c):
                sp.dma_start(Y[:], y_d[bass.ds(c, 1)].rearrange("a (t p) d -> p (a t) d", p=P)).then_inc(y_in, 16)

            def maxima(u):
                hold(ml_made, u + 1)
                g = u % KV if isinstance(u, int) else None
                return g

            def maxima_to(g, n):
                hold(ml_made, n)
                sp.dma_start(f32(QS[96:97, g, :, :]), f32(mh[:])).then_inc(m_in, 16)
                sp.dma_start(f32(QS[97:98, g, :, :]), f32(ml[:])).then_inc(m_in, 16)

            def body(c, first=False, last=False):
                nxt = None if last else (c + 1 if isinstance(c, int) else sp.snap(c + 1))
                for g in range(KV):
                    if not (last and g == KV - 1):
                        maxima_to((g + 1) % KV, unit(c, g) + 2)
                    if g == 0 and not first:
                        hold(sr_made, TT * c)
                        sp.dma_start(src_d[bass.ds(c - 1, 1)].rearrange("a (t p) d -> p (a t) d", p=P), SR[:]).then_inc(src_st, 16)
                        if not first:
                            hold(src_made, TT * c)
                    if g == 0:
                        load_y(c)
                    if g == 2 and not first:
                        hold(slots_made, c)
                        store_slots(c - 1)
                    if not last:
                        hold(sc_mm, NSC * (unit(c, g) + 1))
                        if g > 0:
                            pass
                        hold(pv_mm, KT * (unit(c, g) + 1) - 2)
                        hold(pv_mm, KT * (unit(c, g) + 1))
                        load(nxt, g)

            def store_slots(c):
                sp.dma_start(slot_d[bass.ds(c, 1)].rearrange("a p n -> p (a n)"), from_slot[:].rearrange("p k t -> p (k t)")).then_inc(slot_st, 16)
                sp.dma_start(wt_d[bass.ds(c, 1)].rearrange("a p n -> p (a n)"), wt[:].rearrange("p k t -> p (k t)")).then_inc(wt_st, 16)

            for g in range(KV):
                load(0, g)
            zeros = SR[:].rearrange("p t d -> p (t d)")
            xe_rows = xe_d.rearrange("(n p r) d -> n p (r d)", p=P, r=ZR)
            hold(zero_made, 1)
            with sp.Fori(0, NZ) as i:
                sp.dma_start(xe_rows[bass.ds(i, 1)].rearrange("a p n -> p (a n)"), zeros).then_inc(zero_st, 16)
            maxima_to(0, 1)
            body(0, first=True)
            with sp.Fori(1, NC - 1) as i:
                body(i)
            body(NC - 1, last=True)
            hold(sr_made, TT * NC)
            sp.dma_start(src_d[NC - 1].rearrange("(t p) d -> p t d", p=P), SR[:]).then_inc(src_st, 16)
            hold(slots_made, NC)
            store_slots(NC - 1)
            for sem in (src_st, slot_st, wt_st, y_in):
                sp.wait_ge(sem, 16 * NC)
            sp.wait_ge(sent, 16 * 2 * TT * NC)
            sp.wait_ge(zero_st, 16 * NZ)

        @block.gpsimd
        def _(pool):
            make_identity(nc, pool, ident, ident_zero, ident_made)
            nc.gpsimd.memset(ones[:], 1.0).then_inc(const_made, 1)
            nc.gpsimd.memset(half[:], -0.5).then_inc(const_made, 1)
            for e in range(E):
                nc.gpsimd.memset(iota_e[:, e:e + 1], float(e)).then_inc(const_made, 1)
                nc.gpsimd.memset(ecap[:, e:e + 1], float(e * CAP)).then_inc(const_made, 1)
            pool.wait_ge(const_made, 2 + 2 * E)
            nc.gpsimd.affine_select(out=before[:], in_=ones[:], compare_op=ALU.is_gt, fill=0.0, base=0,
                                    pattern=[[1, P]], channel_multiplier=-1).then_inc(const_made, 1)
            pool.wait_ge(const_in, 64)

            def pair(u, q, first):
                pool.wait_ge(ex_made, NSC * u + G * (2 * q + 2))
                if not first or q >= 2:
                    done = PAIRS * u + q - 1 if q >= 2 else PAIRS * u - 1 - q
                    pool.wait_ge(den_mm, done)
                a = (2 * q) % 4
                nc.gpsimd.tensor_tensor(PP[:, q % 2, :, :], PR[:, a, :, :], PR[:, a + 1, :, :], ALU.add).then_inc(pair_made, 1)

            def add_bias(c):
                pool.wait_ge(y_in, 16 * c + 16)
                for t in range(TT):
                    nc.gpsimd.tensor_tensor(Y[:, t, :], Y[:, t, :], ob_row[:], ALU.add).then_inc(yob_made, 1)

            def norm_power(c):
                pool.wait_ge(ss_made, TT * c + TT)
                gate(pool)
                nc.gpsimd.tensor_scalar(sv[:], ss[:], 1.0 / D, RMS_EPS, ALU.mult, ALU.add).then_inc(sv_made, 1)
                pool.wait_ge(sv_made, c + 1)
                nc.gpsimd.tensor_tensor(sr_rstd[:], sv[:], half[:], ALU.pow).then_inc(rstd_made, 1)

            def norm_weight(c):
                for t in range(TT):
                    pool.wait_ge(sn_made, TT * c + t + 1)
                    nc.gpsimd.tensor_tensor(SR[:, t, :], SR[:, t, :], norm_row[:], ALU.mult).then_inc(sr_made, 1)

            def send(c):
                pool.wait_ge(slots_made, c + 1)
                gate(pool)
                for k in range(2):
                    for t in range(TT):
                        nc.gpsimd.indirect_dma_start(
                            out=xe_d, out_offset=bass.IndirectOffsetOnAxis(ap=to_slot[:, k, t:t + 1].bitcast(U32), axis=0),
                            in_=SR[:, t, :], in_offset=None, bounds_check=E * CAP - 1, oob_is_err=False).then_inc(sent, 16)

            def body(c, first=False):
                for g in range(KV):
                    for q in range(PAIRS - 1):
                        pair(unit(c, g), q, first and g == 0)
                        if g == 0 and not first:
                            if q == 2:
                                norm_power(c - 1)
                            if q == 3:
                                norm_weight(c - 1)
                        if g == 1 and not first and q == 5:
                            send(c - 1)
                        if g == 3 and q == 0:
                            add_bias(c)

            pool.wait_ge(zero_st, 16 * NZ)
            body(0, first=True)
            with pool.Fori(1, NC) as i:
                body(i)
            norm_power(NC - 1)
            norm_weight(NC - 1)
            send(NC - 1)

        @block.scalar
        def _(act):
            ow_raw = PR[:, 0, :, :]
            act.wait_ge(const_in, 64)
            for g in range(KV):
                nc.scalar.activation(ow_hi[:, g, :], ow_raw[:, g, :], ACT.Copy).then_inc(owh_made, 1)
            act.wait_ge(owl_made, KV)

            def exps(c, g, kt, first):
                u = unit(c, g)
                slot_ = kt % 4
                if kt >= 4:
                    act.wait_ge(pv_mm, KT * u + kt - 3)
                    act.wait_ge(pair_made, (PAIRS - 1) * u + (kt - 4) // 2 + 1)
                elif not first:
                    act.wait_ge(pv_mm, KT * u + kt - 3)
                    if kt < 2:
                        act.wait_ge(pair_made, (PAIRS - 1) * u)
                    else:
                        act.wait_ge(den_mm, PAIRS * u)
                for j in range(G):
                    n = NSC * g + G * kt + j
                    act.wait_ge(sc_mm, NSC * KV * c + n + 1)
                    nc.scalar.activation(PR[:, slot_, j, :], ps_b[:, n % BK, :], ACT.Exp, scale=SCALE).then_inc(ex_made, 1)

            def values_out(u, first=False):
                act.wait_ge(pv_mm, KT * u)
                if not first:
                    act.wait_ge(att_made, u - 1)
                nc.scalar.activation(pvs[:], ps_pv[:], ACT.Copy).then_inc(pvs_made, 1)

            def squares(c):
                for t in range(TT):
                    act.wait_ge(src_made, TT * c + t + 1)
                    if t > 0:
                        act.wait_ge(ss_made, TT * c + t)
                    nc.scalar.activation(sq[:], SR[:, t, :], ACT.Square, accum_out=ss[:, t:t + 1]).then_inc(ss_made, 1)

            def rows_out(c, t):
                act.wait_ge(sr_tr, TT * c + t + 1)
                nc.scalar.activation(srT[:, t, :, :], ps_m[:].rearrange("p (k n) -> p k n", k=DK), ACT.Copy).then_inc(srT_made, 1)

            def sigmoid_exp(c):
                act.wait_ge(route, ROUTE_TOP + ROUTES * c)
                nc.scalar.activation(pe_[:], top[:, :, 0:2], ACT.Exp, scale=-1.0).then_inc(exp_made, 1)

            def body(c, first=False):
                for g in range(KV):
                    for kt in range(KT):
                        exps(c, g, kt, first and g == 0)
                        if kt == 1 and not (first and g == 0):
                            values_out(unit(c, g), first and g == 1)
                        if g == 0 and not first:
                            if kt == 6:
                                squares(c - 1)
                            if 10 <= kt < 10 + TT:
                                rows_out(c - 1, kt - 10)
                        if g == 1 and not first and kt == 1:
                            sigmoid_exp(c - 1)

            body(0, first=True)
            with act.Fori(1, NC) as i:
                body(i)
            values_out(KV * NC)
            squares(NC - 1)
            for t in range(TT):
                rows_out(NC - 1, t)
            sigmoid_exp(NC - 1)

        @block.vector
        def _(dve):
            ow_raw = PR[:, 0, :, :]
            nc.vector.memset(SR[:], 0.0).then_inc(zero_made, 1)
            nc.vector.memset(f32(KS[96:98, :, :]), 1.0).then_inc(dve_const, 1)
            nc.vector.memset(base[:, TT, :], 0.0).then_inc(dve_const, 1)
            for g in range(KV):
                dve.wait_ge(owh_made, g + 1)
                nc.vector.tensor_tensor(ow_lo[:, g, :], ow_raw[:, g, :], f32(ow_hi[:, g, :]), ALU.subtract).then_inc(owl_made, 1)
            dve.wait_ge(const_made, 3 + 2 * E)
            dve.wait_ge(dve_const, 2)
            dve.wait_ge(ident_made, 1)

            def maximum(u, a):
                dve.wait_ge(a_mm, NA * u + a + 1)
                nc.vector.reduce_max(mxp[:, a // (S // CH), a % (S // CH):a % (S // CH) + 1], ps_a[:, a % 2, :], AXX).then_inc(mxp_made, 1)

            def maxima(u, first=False):
                dve.wait_ge(mxp_made, NA * (u + 1))
                if not first:
                    dve.wait_ge(m_tr, u)
                nc.vector.reduce_max(mxv[:].rearrange("p t j -> p (t j)"), mxp[:], AXX).then_inc(mxv_made, 1)

            def maxima_split(u, first=False):
                dve.wait_ge(m_tr, u + 1)
                if not first:
                    dve.wait_ge(m_in, 32 * u)
                nc.vector.tensor_scalar(mh[:], ps_m[0:G, :], -1.0, None, ALU.mult).then_inc(mh_made, 1)
                dve.wait_ge(mh_made, u + 1)
                nc.vector.scalar_tensor_tensor(ml[:], ps_m[0:G, :], -1.0, f32(mh[:]), ALU.mult, ALU.subtract).then_inc(ml_made, 1)

            def normalise(u, g):
                dve.wait_ge(den_mm, PAIRS * (u + 1))
                if not (isinstance(u, int) and u == 0):
                    dve.wait_ge(atl_made, u)
                nc.vector.reciprocal(rec[:], ps_den[:]).then_inc(rec_made, 1)
                dve.wait_ge(pvs_made, u + 1)
                dve.wait_ge(rec_made, u + 1)
                nc.vector.tensor_tensor(rec[:], pvs[:], rec[:], ALU.mult).then_inc(att_made, 1)
                dve.wait_ge(att_made, u + 1)
                nc.vector.tensor_copy(at_hi[:, g, :], rec[:]).then_inc(ath_made, 1)
                dve.wait_ge(ath_made, u + 1)
                nc.vector.tensor_tensor(at_lo[:, g, :], rec[:], f32(at_hi[:, g, :]), ALU.subtract).then_inc(atl_made, 1)

            def project_out(c, t, first=False):
                dve.wait_ge(o_mm, TT * c + t + 1)
                dve.wait_ge(yob_made, TT * c + t + 1)
                if not first and t == 0:
                    dve.wait_ge(src_st, 16 * c)
                    dve.wait_ge(sent, 16 * 2 * TT * c)
                nc.vector.tensor_tensor(SR[:, t, :], ps_m[:], Y[:, t, :], ALU.add).then_inc(src_made, 1)

            def norm(c):
                dve.wait_ge(rstd_made, c + 1)
                for t in range(TT):
                    nc.vector.tensor_scalar(SR[:, t, :], SR[:, t, :], sr_rstd[:, t:t + 1], None, ALU.mult).then_inc(sn_made, 1)

            def per_token(ap):
                return ap.rearrange("p (t a) -> p t a", a=1).broadcast_to((P, TT, E))

            def per_expert(ap):
                return ap.rearrange("p (a e) -> p a e", a=1).broadcast_to((P, TT, E))

            def step(c, k):
                dve.wait_ge(route, ROUTES * c + k)

            def choose(c, first=False):
                dve.wait_ge(g_mm, c + 1)
                if not first:
                    dve.wait_ge(exp_made, c)
                nc.vector.tensor_scalar(lgt[:], ps_m[:, 0:TT * E].rearrange("p (t e) -> p t e", t=TT), 17.5, None, ALU.min).then_inc(lgt_made, 1)
                dve.wait_ge(lgt_made, c + 1)
                gate(dve)
                for t in range(TT):
                    nc.vector.max(top[:, t, :], lgt[:, t, :]).then_inc(route, 1)
                step(c, TT)
                gate(dve)
                for t in range(TT):
                    nc.vector.max_index(topi[:, t, :], top[:, t, :], lgt[:, t, :]).then_inc(route, 1)
                step(c, 8)
                nc.vector.tensor_copy(topf[:], topi[:, :, 0:2]).then_inc(route, 1)
                step(c, 9)
                for k in range(2):
                    nc.vector.tensor_tensor(oh[:, k, :, :], topf[:, :, k:k + 1].broadcast_to((P, TT, E)), per_expert(iota_e[:]), ALU.is_equal).then_inc(route, 1)
                step(c, 11)
                nc.vector.tensor_tensor(sel[:], oh[:, 0, :, :], oh[:, 1, :, :], ALU.add).then_inc(sel_made, 1)

            def weights(c, first=False):
                dve.wait_ge(exp_made, c + 1)
                nc.vector.tensor_scalar(pe_[:], pe_[:], 1.0, None, ALU.add).then_inc(route, 1)
                step(c, 12)
                nc.vector.reciprocal(pe_[:], pe_[:]).then_inc(route, 1)
                step(c, 13)
                nc.vector.scalar_tensor_tensor(wsum[:], pe_[:, :, 0], 1e-6, pe_[:, :, 1], ALU.add, ALU.add).then_inc(route, 1)
                step(c, 14)
                nc.vector.reciprocal(wsum[:], wsum[:]).then_inc(route, 1)

            def place(c, first=False):
                dve.wait_ge(rank_mm, c + 1)
                k0 = 7 * c
                nc.vector.tensor_copy(total[:], ps_m[:, TT * E:2 * TT * E].rearrange("p (t e) -> p t e", t=TT)).then_inc(ranked, 1)
                nc.vector.tensor_copy(base[:, 0, :], base[:, TT, :]).then_inc(ranked, 1)
                for t in range(TT):
                    dve.wait_ge(ranked, k0 + 2 + t)
                    nc.vector.tensor_tensor(base[:, t + 1, :], base[:, t, :], total[:, t, :], ALU.add).then_inc(ranked, 1)
                dve.wait_ge(ranked, k0 + 6)
                nc.vector.tensor_tensor(prefix[:], ps_m[:, 0:TT * E].rearrange("p (t e) -> p t e", t=TT), base[:, 0:TT, :], ALU.add).then_inc(ranked, 1)
                dve.wait_ge(ranked, k0 + 7)
                nc.vector.tensor_scalar(room[:], prefix[:], float(CAP), None, ALU.is_lt).then_inc(route, 1)
                step(c, 16)
                nc.vector.tensor_tensor(prefix[:], prefix[:], per_expert(ecap[:]), ALU.add).then_inc(route, 1)
                step(c, 17)
                if not first:
                    dve.wait_ge(sent, 16 * 2 * TT * c)
                    dve.wait_ge(slot_st, 16 * c)
                    dve.wait_ge(wt_st, 16 * c)
                n = 0
                for k in range(2):
                    for out, of in ((slot, prefix), (ok, room)):
                        if n > 0:
                            dve.wait_ge(picked, 8 * c + 2 * n)
                        nc.vector.tensor_tensor(prod[:], oh[:, k, :, :], of[:], ALU.mult).then_inc(picked, 1)
                        dve.wait_ge(picked, 8 * c + 2 * n + 1)
                        nc.vector.reduce_sum(out[:, k, :], prod[:], AXX).then_inc(picked, 1)
                        n += 1
                dve.wait_ge(picked, 8 * c + 8)
                nc.vector.tensor_scalar(far[:], ok[:], -2.0 * E * CAP, 2.0 * E * CAP, ALU.mult, ALU.add).then_inc(route, 1)
                step(c, 18)
                nc.vector.tensor_tensor(to_slot[:], slot[:], far[:], ALU.add).then_inc(route, 1)
                nc.vector.tensor_tensor(from_slot[:], slot[:], ok[:], ALU.mult).then_inc(route, 1)
                nc.vector.tensor_tensor(wt[:], pe_[:].rearrange("p t k -> p k t"), ok[:], ALU.mult).then_inc(route, 1)
                step(c, 21)
                nc.vector.tensor_tensor(wt[:, 0, :], wt[:, 0, :], wsum[:], ALU.mult).then_inc(route, 1)
                nc.vector.tensor_tensor(wt[:, 1, :], wt[:, 1, :], wsum[:], ALU.mult).then_inc(route, 1)
                step(c, 23)
                nc.vector.tensor_copy(base[:, TT, :], base[:, TT, :]).then_inc(slots_made, 1)

            def body(c, first=False, last=False):
                for g in range(KV):
                    u = unit(c, g)
                    for kt in range(KT):
                        if not (last and g == KV - 1):
                            for a in range(A_PER * kt, min(NA, A_PER * (kt + 1))):
                                maximum(u + 1, a)
                            if kt == 13:
                                maxima(u + 1)
                            if kt == 14:
                                maxima_split(u + 1)
                        if kt == 2 and not (first and g == 0):
                            normalise(u - 1, (g - 1) % KV)
                        if g == 0 and not first:
                            if 3 <= kt < 3 + TT:
                                project_out(c - 1, kt - 3, False)
                            if kt == 9:
                                norm(c - 1)
                            if kt == 15:
                                choose(c - 1, False)
                        if g == 1 and not first:
                            if kt == 3:
                                weights(c - 1)
                            if kt == 5:
                                place(c - 1, False)

            for a in range(NA):
                maximum(0, a)
            maxima(0, first=True)
            maxima_split(0, first=True)
            body(0, first=True)
            with dve.Fori(1, NC - 1) as i:
                body(i)
            body(NC - 1, last=True)
            normalise(KV * NC - 1, KV - 1)
            for t in range(TT):
                project_out(NC - 1, t)
            norm(NC - 1)
            choose(NC - 1)
            weights(NC - 1)
            place(NC - 1)

        @block.tensor
        def _(pe):
            def score_maxima(u, g, a):
                t, j, kb = a // (G * CB), a // CB % G, a % CB
                pe.wait_ge(mxp_made, NA * u + a - 1)
                nc.tensor.matmul(ps_a[:, a % 2, :], QS[0:96, g, j, t * P:(t + 1) * P], KS[0:96, g, kb * CH:(kb + 1) * CH],
                                 start=True, stop=True).then_inc(a_mm, 1)

            def maxima_transposed(u):
                pe.wait_ge(mxv_made, u + 1)
                for t in range(TT):
                    last = nc.tensor.transpose(ps_m[0:G, t * P:(t + 1) * P], mxv[:, t, :], ident[:])
                last.then_inc(m_tr, 1)

            def scores(c, g, kt, j, first):
                n = NSC * g + G * kt + j
                if n >= BK:
                    pe.wait_ge(ex_made, NSC * KV * c + n - BK + 1)
                elif not first:
                    pe.wait_ge(ex_made, NSC * KV * c + (0 if n == 0 else n - BK + 1))
                nc.tensor.matmul(ps_b[:, n % BK, :], KS[:, g, kt * P:(kt + 1) * P], QS[:, g, j, :],
                                 start=True, stop=True).then_inc(sc_mm, 1)

            def values(u, g, kt):
                pe.wait_ge(ex_made, NSC * u + G * (kt + 1))
                for j in range(G):
                    last = nc.tensor.matmul(ps_pv[HD * j:HD * (j + 1), :], VS[:, g, kt, :], PR[:, kt % 4, j, :],
                                            start=(kt == 0), stop=(kt == KT - 1))
                last.then_inc(pv_mm, 1)

            def denominators(u, q):
                if q < PAIRS - 1:
                    pe.wait_ge(pair_made, (PAIRS - 1) * u + q + 1)
                    for j in range(G):
                        last = nc.tensor.matmul(ps_den[HD * j:HD * (j + 1), :], ones[:, 0:HD], PP[:, q % 2, j, :],
                                                start=(q == 0), stop=False)
                else:
                    for half_ in range(2):
                        for j in range(G):
                            last = nc.tensor.matmul(ps_den[HD * j:HD * (j + 1), :], ones[:, 0:HD], PR[:, 2 + half_, j, :],
                                                    start=False, stop=(half_ == 1))
                last.then_inc(den_mm, 1)

            def last_values(u, g, kt):
                values(u, g, KT - 2 + kt)
                if kt == 1:
                    denominators(u, PAIRS - 2)
                    denominators(u, PAIRS - 1)

            def project_out(c, t):
                if t == 0:
                    pe.wait_ge(atl_made, KV * (c + 1))
                    pe.wait_ge(ml_made, KV * (c + 1) + (0 if isinstance(c, int) and c == NC - 1 else 1))
                else:
                    pe.wait_ge(src_made, TT * c + t)
                for g in range(KV):
                    toks = slice(t * P, (t + 1) * P)
                    last = mm3(nc, ps_m[:], at_hi[:, g, toks], at_lo[:, g, toks], ow_hi[:, g, :], ow_lo[:, g, :],
                               g == 0, g == KV - 1)
                last.then_inc(o_mm, 1)

            def rows_transposed(c, t):
                pe.wait_ge(sr_made, TT * c + t + 1)
                if t == 0:
                    pe.wait_ge(src_made, TT * c + TT)
                else:
                    pe.wait_ge(srT_made, TT * c + t)
                for k in range(DK):
                    last = nc.tensor.transpose(ps_m[:, k * P:(k + 1) * P], SR[:, t, k * P:(k + 1) * P], ident[:])
                last.then_inc(sr_tr, 1)

            def logits(c):
                pe.wait_ge(srT_made, TT * c + TT)
                for t in range(TT):
                    for k in range(DK):
                        last = nc.tensor.matmul(ps_m[:, t * E:(t + 1) * E], srT[:, t, k, :], gw[:, k, :], start=(k == 0), stop=(k == DK - 1))
                last.then_inc(g_mm, 1)

            def ranks(c):
                pe.wait_ge(sel_made, c + 1)
                nc.tensor.matmul(ps_m[:, 0:TT * E], before[:], sel[:].rearrange("p t e -> p (t e)"), start=True, stop=True)
                nc.tensor.matmul(ps_m[:, TT * E:2 * TT * E], ones[:], sel[:].rearrange("p t e -> p (t e)"), start=True, stop=True).then_inc(rank_mm, 1)

            def body(c, first=False, last=False):
                for g in range(KV):
                    u = unit(c, g)
                    ahead = not (last and g == KV - 1)
                    nxt = (g + 1) % KV
                    if ahead:
                        pe.wait_ge(q_in[nxt], 96 * (c + (1 if nxt == 0 else 0)) + 96)
                    for kt in range(KT):
                        a = A_PER * kt
                        for j in range(G):
                            if kt == 0 and j == 0:
                                pe.wait_ge(m_in, 32 * (u + 1))
                            scores(c, g, kt, j, first)
                            for _ in range(2 if j == 0 else 1):
                                if ahead and a < NA:
                                    score_maxima(u + 1, nxt, a)
                                a += 1
                        if kt < 2:
                            if not (first and g == 0):
                                last_values(u - 1, (g - 1) % KV, kt)
                        else:
                            if kt == 2:
                                pe.wait_ge(v_in[g], 16 * c + 16)
                                if not (first and g == 0):
                                    pe.wait_ge(pvs_made, u)
                            values(u, g, kt - 2)
                        if kt % 2 == 1 and kt >= 5:
                            if kt == 5 and not (first and g == 0):
                                pe.wait_ge(rec_made, u)
                            denominators(u, (kt - 5) // 2)
                        if g == 0 and not first:
                            if 3 <= kt < 3 + TT:
                                project_out(c - 1, kt - 3)
                            if 10 <= kt < 10 + TT:
                                rows_transposed(c - 1, kt - 10)
                        if kt == 14 and ahead:
                            if g == 0 and not first:
                                pe.wait_ge(srT_made, TT * c)
                            elif g == 1 and not first:
                                pe.wait_ge(ranked, 7 * c)
                            maxima_transposed(u + 1)
                        if kt == 15 and g == 0 and not first:
                            pe.wait_ge(ml_made, u + 2)
                            logits(c - 1)
                        if kt == 4 and g == 1 and not first:
                            ranks(c - 1)

            pe.wait_ge(ident_made, 1)
            pe.wait_ge(const_made, 3 + 2 * E)
            pe.wait_ge(dve_const, 2)
            pe.wait_ge(owl_made, KV)
            pe.wait_ge(q_in[0], 96)
            for a in range(NA):
                if a < 2:
                    t, j, kb = a // (G * CB), a // CB % G, a % CB
                    nc.tensor.matmul(ps_a[:, a % 2, :], QS[0:96, 0, j, t * P:(t + 1) * P], KS[0:96, 0, kb * CH:(kb + 1) * CH],
                                     start=True, stop=True).then_inc(a_mm, 1)
                else:
                    score_maxima(0, 0, a)
            maxima_transposed(0)
            body(0, first=True)
            with pe.Fori(1, NC - 1) as i:
                body(i)
            body(NC - 1, last=True)
            for kt in range(2):
                last_values(KV * NC - 1, KV - 1, kt)
            for t in range(TT):
                project_out(NC - 1, t)
            for t in range(TT):
                rows_transposed(NC - 1, t)
            logits(NC - 1)
            ranks(NC - 1)


def phase_experts(nc, xe_d, w1, w2, ye_d):
    TILES = [3, 3, 2, 2]
    NB = len(TILES)
    WB = max(TILES)
    FK = F // P
    HB = 3
    FIRST = [sum(TILES[:b]) for b in range(NB)]
    NT = sum(TILES)
    assert NT * P == CAP and NB % 2 == 0
    with Scope(nc, "p3") as s:
        ident = s.sb("ident", [P, P])
        w1_raw = s.sb("w1_raw", [P, DK, F])
        w2_raw = s.sb("w2_raw", [P, FK, D])
        w1h = s.sb("w1h", [P, DK, F], F32R)
        w1l = s.sb("w1l", [P, DK, F], F32R)
        w2h = s.sb("w2h", [P, FK, D], F32R)
        w2l = s.sb("w2l", [P, FK, D], F32R)
        XE = s.sb("XE", [P, 2, WB, D])
        xTh = s.sb("xTh", [P, 2, DK, WB * P], F32R)
        xTl = s.sb("xTl", [P, 2, DK, WB * P], F32R)
        hf = s.sb("hf", [P, 2, WB * P])
        hh = s.sb("hh", [P, 2, FK, WB * P], F32R)
        hl = s.sb("hl", [P, 2, FK, WB * P], F32R)
        YE = s.sb("YE", [P, 2, D])
        ps_t = s.ps("ps_t", [P, 2, CH])
        ps_h = s.ps("ps_h", [P, HB + 1, CH])
        ps_y = s.ps("ps_y", [P, 2, CH])
        ident_zero, ident_made = s.sem("ident_zero"), s.sem("ident_made")
        w1_in, w2_in, w1h_made, w1l_made, w2h_made, w2l_made = (s.sem(n) for n in ("w1_in", "w2_in", "w1h_made", "w1l_made", "w2h_made", "w2l_made"))
        xe_in = [s.sem("xe_in0"), s.sem("xe_in1")]
        x_tr, xh_made, xl_made, h_mm, hf_made, hh_made, hl_made, y_mm, y_out = (
            s.sem(n) for n in ("x_tr", "xh_made", "xl_made", "h_mm", "hf_made", "hh_made", "hl_made", "y_mm", "y_out"))
        y_st = [s.sem("y_st0"), s.sem("y_st1")]
        gate_sem = s.sem("gate")
        block = s.block()

        def hold(eng, sem, n):
            eng.wait_ge(sem, n)
            eng.sem_inc(gate_sem, 1)

        xe_v = xe_d.rearrange("(e t p) d -> e p t d", p=P, t=NT)
        ye_v = ye_d.rearrange("(e t p) d -> e p t d", p=P, t=NT)
        w1_v = w1.rearrange("e (k p) f -> e p k f", p=P)
        w2_v = w2.rearrange("e (k p) d -> e p k d", p=P)

        @block.sync
        def _(sp):
            def load_block(e, b):
                sp.dma_start(XE[:, b % 2, 0:TILES[b], :],
                             xe_v[bass.ds(e, 1), :, FIRST[b]:FIRST[b] + TILES[b], :].rearrange("a p t d -> p (a t) d")).then_inc(xe_in[b % 2], 16)

            def load_w1(e):
                sp.dma_start(w1_raw[:], w1_v[bass.ds(e, 1)].rearrange("a p k f -> p (a k) f")).then_inc(w1_in, 16)

            def load_w2(e):
                sp.dma_start(w2_raw[:], w2_v[bass.ds(e, 1)].rearrange("a p k f -> p (a k) f")).then_inc(w2_in, 16)

            def body(e, last=False):
                for b in range(NB):
                    if b < NB - 2 or not last:
                        hold(sp, x_tr, DK * (NB * e + b + 1))
                        load_block(e + (b + 2) // NB, (b + 2) % NB)
                    if not last and b == 0:
                        hold(sp, w1l_made, DK * (e + 1))
                        load_w1(e + 1)
                    if not last and b == 1:
                        hold(sp, w2l_made, FK * (e + 1))
                        load_w2(e + 1)

            load_block(0, 0)
            load_w1(0)
            load_block(0, 1)
            load_w2(0)
            with sp.Fori(0, E - 1) as e:
                body(e)
            body(E - 1, last=True)

        @block.gpsimd
        def _(pool):
            make_identity(nc, pool, ident, ident_zero, ident_made)

            def store(e, b, t):
                n = FIRST[b] + t
                hold(pool, y_out, NT * e + n + 1)
                pool.dma_start(ye_v[bass.ds(e, 1), :, n:n + 1, :].rearrange("a p t d -> p (a t d)"), YE[:, n % 2, :]).then_inc(y_st[n % 2], 16)

            with pool.Fori(0, E) as e:
                for b in range(NB):
                    for t in range(TILES[b]):
                        store(e, b, t)
            for i in range(2):
                pool.wait_ge(y_st[i], 16 * E * NT // 2)

        @block.scalar
        def _(act):
            def split_w1(e):
                act.wait_ge(w1_in, 16 * e + 16)
                if not (isinstance(e, int) and e == 0):
                    act.wait_ge(h_mm, FK * NB * e)
                for k in range(DK):
                    nc.scalar.activation(w1h[:, k, :], w1_raw[:, k, :], ACT.Copy).then_inc(w1h_made, 1)

            def split_w2(e):
                act.wait_ge(w2_in, 16 * e + 16)
                if not (isinstance(e, int) and e == 0):
                    act.wait_ge(y_mm, NT * e)
                for k in range(FK):
                    nc.scalar.activation(w2h[:, k, :], w2_raw[:, k, :], ACT.Copy).then_inc(w2h_made, 1)

            def rows_high(e, b, first=False):
                n = TILES[b] * P
                m = NB * e + b
                for k in range(DK):
                    act.wait_ge(x_tr, DK * m + k + 1)
                    if k == 0 and not first:
                        act.wait_ge(h_mm, FK * (m - 1))
                    nc.scalar.activation(xTh[:, b % 2, k, 0:n], ps_t[:, k % 2, 0:n], ACT.Copy).then_inc(xh_made, 1)

            def hidden(e, b, first=False):
                n = TILES[b] * P
                m = NB * e + b
                for f in range(FK):
                    act.wait_ge(h_mm, FK * m + f + 1)
                    if not first or f >= 2:
                        act.wait_ge(hl_made, FK * m + f - 1)
                    nc.scalar.activation(hf[:, f % 2, 0:n], ps_h[:, f % (HB + 1), 0:n], ACT.Gelu).then_inc(hf_made, 1)
                    act.wait_ge(hf_made, FK * m + f + 1)
                    if f == 0 and not (first or (isinstance(e, int) and m < 2)):
                        act.wait_ge(y_mm, before_block(e, b))
                    nc.scalar.activation(hh[:, b % 2, f, 0:n], hf[:, f % 2, 0:n], ACT.Copy).then_inc(hh_made, 1)

            def before_block(e, b):
                return NT * e + FIRST[b - 1] if b >= 1 else NT * e - TILES[NB - 1]

            def body(e, first=False, last=False):
                for b in range(NB):
                    hidden(e, b, first and b == 0)
                    if b == NB - 1 and not last:
                        split_w1(e + 1)
                    if b < NB - 1:
                        rows_high(e, b + 1, first and b == 0)
                    elif not last:
                        rows_high(e + 1, 0)
                    if b == 0 and not first:
                        split_w2(e)

            split_w1(0)
            rows_high(0, 0, first=True)
            split_w2(0)
            body(0, first=True)
            with act.Fori(1, E - 1) as e:
                body(e)
            body(E - 1, last=True)

        @block.vector
        def _(dve):
            def split_w1(e):
                for k in range(DK):
                    dve.wait_ge(w1h_made, DK * e + k + 1)
                    nc.vector.tensor_tensor(w1l[:, k, :], w1_raw[:, k, :], f32(w1h[:, k, :]), ALU.subtract).then_inc(w1l_made, 1)

            def split_w2(e):
                for k in range(FK):
                    dve.wait_ge(w2h_made, FK * e + k + 1)
                    nc.vector.tensor_tensor(w2l[:, k, :], w2_raw[:, k, :], f32(w2h[:, k, :]), ALU.subtract).then_inc(w2l_made, 1)

            def rows_low(e, b):
                n = TILES[b] * P
                m = NB * e + b
                for k in range(DK):
                    dve.wait_ge(xh_made, DK * m + k + 1)
                    nc.vector.tensor_tensor(xTl[:, b % 2, k, 0:n], ps_t[:, k % 2, 0:n], f32(xTh[:, b % 2, k, 0:n]), ALU.subtract).then_inc(xl_made, 1)

            def hidden_low(e, b):
                n = TILES[b] * P
                m = NB * e + b
                for f in range(FK):
                    dve.wait_ge(hh_made, FK * m + f + 1)
                    nc.vector.tensor_tensor(hl[:, b % 2, f, 0:n], hf[:, f % 2, 0:n], f32(hh[:, b % 2, f, 0:n]), ALU.subtract).then_inc(hl_made, 1)

            def rows_out(e, b, first=False):
                for t in range(TILES[b]):
                    n = FIRST[b] + t
                    dve.wait_ge(y_mm, NT * e + n + 1)
                    if not first or n >= 2:
                        dve.wait_ge(y_st[n % 2], 16 * (NT // 2 * e + n // 2))
                    nc.vector.tensor_copy(YE[:, n % 2, :], ps_y[:, n % 2, :]).then_inc(y_out, 1)

            def body(e, first=False, last=False):
                for b in range(NB):
                    hidden_low(e, b)
                    if b == NB - 1 and not last:
                        split_w1(e + 1)
                    if b == 0 and not first:
                        rows_out_lag = (e - 1, NB - 1)
                    elif b > 0:
                        rows_out_lag = (e, b - 1)
                    else:
                        rows_out_lag = None
                    if b < NB - 1:
                        rows_low(e, b + 1)
                    elif not last:
                        rows_low(e + 1, 0)
                    if rows_out_lag:
                        rows_out(*rows_out_lag, first and rows_out_lag[1] == 0)
                    if b == 0 and not first:
                        split_w2(e)

            split_w1(0)
            rows_low(0, 0)
            split_w2(0)
            body(0, first=True)
            with dve.Fori(1, E - 1) as e:
                body(e)
            body(E - 1, last=True)
            rows_out(E - 1, NB - 1)

        @block.tensor
        def _(pe):
            def transposes(e, b, first=False):
                m = NB * e + b
                pe.wait_ge(xe_in[b % 2], 16 * (NB // 2 * e + b // 2) + 16)
                for k in range(DK):
                    if not first or k >= 2:
                        pe.wait_ge(xl_made, DK * m + k - 1)
                    for t in range(TILES[b]):
                        last = nc.tensor.transpose(ps_t[:, k % 2, t * P:(t + 1) * P], XE[:, b % 2, t, k * P:(k + 1) * P], ident[:])
                    last.then_inc(x_tr, 1)

            def up(e, b, first=False):
                n = TILES[b] * P
                m = NB * e + b
                pe.wait_ge(xl_made, DK * m + DK)
                if b == 0:
                    pe.wait_ge(w1l_made, DK * e + DK)
                for f in range(FK):
                    if not first or f > HB:
                        pe.wait_ge(hf_made, FK * m + f - HB)
                    for k in range(DK):
                        cols = slice(f * P, (f + 1) * P)
                        last = mm3(nc, ps_h[:, f % (HB + 1), 0:n], w1h[:, k, cols], w1l[:, k, cols],
                                   xTh[:, b % 2, k, 0:n], xTl[:, b % 2, k, 0:n], k == 0, k == DK - 1)
                    last.then_inc(h_mm, 1)

            def down(e, b, first=False):
                m = NB * e + b
                pe.wait_ge(hl_made, FK * m + FK)
                if b == 0:
                    pe.wait_ge(w2l_made, FK * e + FK)
                for t in range(TILES[b]):
                    n = FIRST[b] + t
                    if not first or n >= 2:
                        pe.wait_ge(y_out, NT * e + n - 1)
                    toks = slice(t * P, (t + 1) * P)
                    for f in range(FK):
                        last = mm3(nc, ps_y[:, n % 2, :], hh[:, b % 2, f, toks], hl[:, b % 2, f, toks],
                                   w2h[:, f, :], w2l[:, f, :], f == 0, f == FK - 1)
                    last.then_inc(y_mm, 1)

            def body(e, first=False, last=False):
                for b in range(NB):
                    up(e, b, first and b == 0)
                    if b < NB - 1:
                        transposes(e, b + 1)
                    elif not last:
                        transposes(e + 1, 0)
                    if b > 0:
                        down(e, b - 1, first and b == 1)
                    elif not first:
                        down(e - 1, NB - 1)

            pe.wait_ge(ident_made, 1)
            transposes(0, 0, first=True)
            body(0, first=True)
            with pe.Fori(1, E - 1) as e:
                body(e)
            body(E - 1, last=True)
            down(E - 1, NB - 1)


def phase_combine(nc, ye_d, src_d, x1_d, slot_d, wt_d, norm2, out):
    with Scope(nc, "p4") as s:
        norm_row = s.sb("norm_row", [P, D])
        slots = s.sb("slots", [P, NC, 2, TT], I32)
        wts = s.sb("wts", [P, NC, 2, TT])
        half = s.sb("half", [P, TT])
        SR = s.sb("SR", [P, 2, TT, D])
        X1 = s.sb("X1", [P, 2, TT, D])
        YG = s.sb("YG", [P, 2, TT, 2, D])
        OUT = s.sb("OUT", [P, 2, TT, D])
        sq = s.sb("sq", [P, D])
        ss = s.sb("ss", [P, 2, TT])
        sv = s.sb("sv", [P, 2, TT])
        rstd = s.sb("rstd", [P, 2, TT])
        const_in, half_made = s.sem("const_in"), s.sem("half_made")
        sr_in = [s.sem("sr_in0"), s.sem("sr_in1")]
        x1_in = [s.sem("x1_in0"), s.sem("x1_in1")]
        yg_in = [s.sem("yg_in0"), s.sem("yg_in1")]
        out_st = [s.sem("out_st0"), s.sem("out_st1")]
        add0, add1, ss_made, sv_made, rs_made, n_made, o_made, o_first = (s.sem(n) for n in ("add0", "add1", "ss_made", "sv_made", "rs_made", "n_made", "o_made", "o_first"))
        block = s.block()
        NCH = NC

        @block.sync
        def _(sp):
            sp.dma_start(slots[:].rearrange("p c k t -> p c (k t)"), slot_d.rearrange("c p n -> p c n")).then_inc(const_in, 16)
            sp.dma_start(wts[:].rearrange("p c k t -> p c (k t)"), wt_d.rearrange("c p n -> p c n")).then_inc(const_in, 16)
            sp.dma_start(norm_row[:], over_rows(norm2)).then_inc(const_in, 16)
            for c in range(NCH):
                i = c % 2
                if c >= 2:
                    sp.wait_ge(o_made, TT * (c - 1))
                sp.dma_start(SR[:, i, :, :], src_d[c].rearrange("(t p) d -> p t d", p=P)).then_inc(sr_in[i], 16)
                sp.dma_start(X1[:, i, :, :], x1_d[c].rearrange("(t p) d -> p t d", p=P)).then_inc(x1_in[i], 16)

        @block.gpsimd
        def _(pool):
            nc.gpsimd.memset(half[:], -0.5).then_inc(half_made, 1)
            pool.wait_ge(half_made, 1)
            pool.wait_ge(const_in, 48)

            def fetch(c):
                i = c % 2
                if c >= 2:
                    pool.wait_ge(add1, TT * (c - 1))
                for t in range(TT):
                    for k in range(2):
                        nc.gpsimd.indirect_dma_start(out=YG[:, i, t, k, :], out_offset=None, in_=ye_d,
                                                     in_offset=bass.IndirectOffsetOnAxis(ap=slots[:, c, k, t:t + 1].bitcast(U32), axis=0)).then_inc(yg_in[i], 16)

            fetch(0)
            for c in range(NCH):
                i = c % 2
                if c + 1 < NCH:
                    fetch(c + 1)
                pool.wait_ge(ss_made, TT * c + TT)
                nc.gpsimd.tensor_scalar(sv[:, i, :], ss[:, i, :], 1.0 / D, RMS_EPS, ALU.mult, ALU.add).then_inc(sv_made, 1)
                pool.wait_ge(sv_made, c + 1)
                nc.gpsimd.tensor_tensor(rstd[:, i, :], sv[:, i, :], half[:], ALU.pow).then_inc(rs_made, 1)

        @block.scalar
        def _(act):
            def store(c):
                i = c % 2
                act.wait_ge(o_made, TT * c + TT)
                act.dma_start(out[c].rearrange("(t p) d -> p t d", p=P), OUT[:, i, :, :]).then_inc(out_st[i], 16)

            for c in range(NCH):
                i = c % 2
                for t in range(TT):
                    act.wait_ge(add1, TT * c + t + 1)
                    if c + t > 0:
                        act.wait_ge(ss_made, TT * c + t)
                    nc.scalar.activation(sq[:], SR[:, i, t, :], ACT.Square, accum_out=ss[:, i, t:t + 1]).then_inc(ss_made, 1)
                if c > 0:
                    store(c - 1)
            store(NCH - 1)
            for i in range(2):
                act.wait_ge(out_st[i], 16 * NCH // 2)

        @block.vector
        def _(dve):
            dve.wait_ge(const_in, 48)

            def add(c):
                i = c % 2
                dve.wait_ge(sr_in[i], 16 * (c // 2 + 1))
                dve.wait_ge(yg_in[i], 16 * 2 * TT * (c // 2 + 1))
                for t in range(TT):
                    nc.vector.scalar_tensor_tensor(SR[:, i, t, :], YG[:, i, t, 0, :], wts[:, c, 0, t:t + 1], SR[:, i, t, :],
                                                   ALU.mult, ALU.add).then_inc(add0, 1)
                for t in range(TT):
                    dve.wait_ge(add0, TT * c + t + 1)
                    nc.vector.scalar_tensor_tensor(SR[:, i, t, :], YG[:, i, t, 1, :], wts[:, c, 1, t:t + 1], SR[:, i, t, :],
                                                   ALU.mult, ALU.add).then_inc(add1, 1)

            def finish(c):
                i = c % 2
                dve.wait_ge(rs_made, c + 1)
                dve.wait_ge(x1_in[i], 16 * (c // 2 + 1))
                if c >= 2:
                    dve.wait_ge(out_st[i], 16 * (c // 2))
                for t in range(TT):
                    nc.vector.scalar_tensor_tensor(OUT[:, i, t, :], SR[:, i, t, :], rstd[:, i, t:t + 1], norm_row[:],
                                                   ALU.mult, ALU.mult).then_inc(n_made, 1)
                for t in range(TT):
                    dve.wait_ge(n_made, TT * c + t + 1)
                    nc.vector.tensor_tensor(OUT[:, i, t, :], OUT[:, i, t, :], X1[:, i, t, :], ALU.add).then_inc(o_made, 1)

            add(0)
            for c in range(NCH):
                if c + 1 < NCH:
                    add(c + 1)
                finish(c)


def build_layer(nc, x, ctx_1024, mask, gamma, beta, qw, qb, kw, kb, vw, vb, ow, ob, gate_w, w1, w2, norm1, norm2, out):
    def scratch(name, shape, dt=F32):
        return nc.dram_tensor(name, shape, dt, kind="Internal").ap()

    x1_d, y_d, src_d = (scratch(n, (NC, CH, D)) for n in ("x1_d", "y_d", "src_d"))
    qh_d, ql_d = scratch("qh_d", (NC, D, CH)), scratch("ql_d", (NC, D, CH))
    kh_d, kl_d, v_d = scratch("kh_d", (NC, P, CH)), scratch("kl_d", (NC, P, CH)), scratch("v_d", (NC, CH, P))
    xe_d, ye_d = scratch("xe_d", (E * CAP, D)), scratch("ye_d", (E * CAP, D))
    slot_d, wt_d = scratch("slot_d", (NC, P, 2 * TT), I32), scratch("wt_d", (NC, P, 2 * TT))

    def chunks(ap):
        return ap.rearrange("b (n q) d -> (b n) q d", q=CH)

    phase_project(nc, chunks(x), ctx_1024, chunks(mask), gamma, beta, qw, qb, kw, kb, vw, vb,
                  x1_d, y_d, qh_d, ql_d, kh_d, kl_d, v_d)
    phase_attend(nc, y_d, qh_d, ql_d, kh_d, kl_d, v_d, ow, ob, norm1, gate_w, src_d, xe_d, slot_d, wt_d)
    phase_experts(nc, xe_d, w1, w2, ye_d)
    phase_combine(nc, ye_d, src_d, x1_d, slot_d, wt_d, norm2, chunks(out))


INPUTS = ["x", "ctx_1024", "mask_BxSxS2_ik1", "L0_xattn_gamma", "L0_xattn_beta", "L0_ffn_qw", "L0_ffn_qb", "L0_ffn_kw",
          "L0_ffn_kb", "L0_ffn_vw", "L0_ffn_vb", "L0_ffn_ow", "L0_ffn_ob", "L0_ffn_gate_w", "L0_ffn_w1", "L0_ffn_w2",
          "L0_ffn_norm1_w", "L0_ffn_norm2_w"]


def kernel(**inputs):
    import numpy as np
    import concourse.bacc as bacc
    from concourse.bass_utils import run_bass_kernel_spmd

    nc = bacc.Bacc("TRN2", target_bir_lowering=False, num_devices=1)
    arrays, args = {}, []
    for name in INPUTS:
        a = np.ascontiguousarray(inputs[name])
        arrays[f"in_{name}"] = a
        args.append(nc.dram_tensor(f"in_{name}", a.shape, mybir.dt.from_np(a.dtype), kind="ExternalInput").ap())
    args.append(nc.dram_tensor("out_dram", (B, S, D), F32, kind="ExternalOutput").ap())
    build_layer(nc, *args)
    return run_bass_kernel_spmd(nc, [arrays], core_ids=[0]).results[0]["out_dram"]
```

```python
from contextlib import ExitStack

import concourse.bass as bass
from concourse import mybir

F32 = mybir.dt.float32
F32R = mybir.dt.float32r
I32 = mybir.dt.int32
U32 = mybir.dt.uint32
ALU = mybir.AluOpType
ACT = mybir.ActivationFunctionType
AXX = mybir.AxisListType.X

P = 128
B, S, D = 2, 2048, 512
N = B * S
CT = 77
DK = D // P
H, KV, HD = 16, 4, 32
G = H // KV
CH = 512
TT = CH // P
NC = N // CH
CB = S // CH
KT = S // P
E, F = 8, 1024
CAP = int(1.25 * N * 2 / E)
NEG = -9e15
LN_EPS = 1e-5
RMS_EPS = 1e-6


class Scope:

    def __init__(self, nc, tag):
        self.nc, self.tag, self.stack = nc, tag, ExitStack()

    def __enter__(self):
        self.stack.__enter__()
        return self

    def __exit__(self, *a):
        return self.stack.__exit__(*a)

    def sb(self, name, shape, dt=F32):
        return self.stack.enter_context(self.nc.sbuf_tensor(f"{self.tag}_{name}", shape, dt))

    def ps(self, name, shape, dt=F32):
        return self.stack.enter_context(self.nc.psum_tensor(f"{self.tag}_{name}", shape, dt))

    def sem(self, name):
        return self.stack.enter_context(self.nc.semaphore(f"{self.tag}_{name}"))

    def block(self):
        return self.stack.enter_context(self.nc.Block())


def f32(ap):
    return ap.bitcast(F32)


def mm3(nc, out, ah, al, bh, bl, start, stop):
    nc.tensor.matmul(out, ah, bh, start=start, stop=False)
    nc.tensor.matmul(out, ah, bl, start=False, stop=False)
    return nc.tensor.matmul(out, al, bh, start=False, stop=stop)


def make_identity(nc, pool, ident, ident_zero, ident_made):
    nc.gpsimd.memset(ident[:], 0.0).then_inc(ident_zero, 1)
    pool.wait_ge(ident_zero, 1)
    nc.gpsimd.affine_select(out=ident[:], in_=ident[:], compare_op=ALU.not_equal, fill=1.0, base=0,
                            pattern=[[-1, P]], channel_multiplier=1).then_inc(ident_made, 1)


def over_rows(ap, rows=P):
    return ap.rearrange("(a n) -> a n", a=1).broadcast_to((rows, ap.shape[0]))


def phase_project(nc, x, ctx, mask, gamma, beta, qw, qb, kw, kb, vw, vb, x1_d, y_d, qh_d, ql_d, kh_d, kl_d, v_d):
    NM = KV + 1
    with Scope(nc, "p1") as s:
        ident = s.sb("ident", [P, P])
        w_raw = s.sb("w_raw", [P, DK, D + 2 * P])
        w_hi = s.sb("w_hi", [P, DK, D + 2 * P], F32R)
        w_lo = s.sb("w_lo", [P, DK, D + 2 * P], F32R)
        b_col = s.sb("b_col", [P, NM])
        vb_row = s.sb("vb_row", [P, P])
        gamma_row = s.sb("gamma_row", [P, D])
        beta_row = s.sb("beta_row", [P, D])
        ctx_n = s.sb("ctx_n", [CT, B, D])
        ctx_t = s.sb("ctx_t", [P, B, DK, CT])
        X = s.sb("X", [P, TT, D])
        MK = s.sb("MK", [P, TT, CT], I32)
        pen = s.sb("pen", [P, TT, CT])
        qn = s.sb("qn", [P, TT, D])
        qT = s.sb("qT", [P, DK, CH])
        lg = s.sb("lg", [P, TT, CT])
        pr = s.sb("pr", [P, TT, CT])
        prT = s.sb("prT", [CT, CH])
        att = s.sb("att", [P, TT, D])
        xb = s.sb("xb", [P, TT, D])
        x1 = s.sb("x1", [P, TT, D])
        y = s.sb("y", [P, TT, D])
        yTh = s.sb("yTh", [P, DK, CH], F32R)
        yTl = s.sb("yTl", [P, DK, CH], F32R)
        hi = s.sb("hi", [P, NM, CH], F32R)
        lo = s.sb("lo", [P, NM, CH], F32R)
        val = s.sb("val", [P, TT, P])
        stats = s.sb("stats", [P, 3, TT, 6])
        mv = s.sb("mv", [P, 3, TT, 2])
        var = s.sb("var", [P, 3, TT])
        rstd = s.sb("rstd", [P, 3, TT])
        half = s.sb("half", [P, TT])
        mx = s.sb("mx", [P, TT])
        nmx = s.sb("nmx", [P, TT])
        psum_e = s.sb("psum_e", [P, TT])
        rinv = s.sb("rinv", [P, TT])
        vr = s.sb("vr", [P, TT])
        s2 = s.sb("s2", [P, TT])
        ps_t = s.ps("ps_t", [P, 2, CH])
        ps_lg = s.ps("ps_lg", [P, TT, P])
        ps_pt = s.ps("ps_pt", [P, CH])
        ps_o = s.ps("ps_o", [P, 2, CH])
        ps_pj = s.ps("ps_pj", [P, 2, CH])

        w_in, ctx_in, vec_in = s.sem("w_in"), s.sem("ctx_in"), s.sem("vec_in")
        ident_zero, ident_made, half_made = s.sem("ident_zero"), s.sem("ident_made"), s.sem("half_made")
        wh_made, wl_made = s.sem("wh_made"), s.sem("wl_made")
        ctx_tr, ctx_t_made = s.sem("ctx_tr"), s.sem("ctx_t_made")
        x_in, mask_in = s.sem("x_in"), s.sem("mask_in")
        stat = [s.sem(f"stat{i}") for i in range(3)]
        aggr = [s.sem(f"aggr{i}") for i in range(3)]
        vared = [s.sem(f"vared{i}") for i in range(3)]
        rs = [s.sem(f"rs{i}") for i in range(3)]
        qn_made, q_tr, qT_made, lg_mm, pen_made = (s.sem(n) for n in ("qn_made", "q_tr", "qT_made", "lg_mm", "pen_made"))
        lg_made, mx_made, nmx_made, pr_made, p_tr = (s.sem(n) for n in ("lg_made", "mx_made", "nmx_made", "pr_made", "p_tr"))
        prT_made, o_mm, att_made, rinv_made = (s.sem(n) for n in ("prT_made", "o_mm", "att_made", "rinv_made"))
        vr1, s2_made, att_n, att_g = (s.sem(n) for n in ("vr1", "s2_made", "att_n", "att_g"))
        xb_made, x1_made, y_made, y_tr = (s.sem(n) for n in ("xb_made", "x1_made", "y_made", "y_tr"))
        yh_made, yl_made, pj_mm, hi_made, pj_out = (s.sem(n) for n in ("yh_made", "yl_made", "pj_mm", "hi_made", "pj_out"))
        x1_st, y_st, q_st, k_st, v_st = (s.sem(n) for n in ("x1_st", "y_st", "q_st", "k_st", "v_st"))
        gate_sem = s.sem("gate")
        block = s.block()

        def gate(eng):
            eng.sem_inc(gate_sem, 1)

        @block.sync
        def _(sp):
            sp.dma_start(w_raw[:, :, 0:D], qw.rearrange("(k p) n -> p k n", p=P)).then_inc(w_in, 16)
            sp.dma_start(w_raw[:, :, D:D + P], kw.rearrange("(k p) n -> p k n", p=P)).then_inc(w_in, 16)
            sp.dma_start(w_raw[:, :, D + P:], vw.rearrange("(k p) n -> p k n", p=P)).then_inc(w_in, 16)

            def load(c):
                sp.dma_start(X[:], x[bass.ds(c, 1)].rearrange("a (t p) d -> p (a t) d", p=P)).then_inc(x_in, 16)
                sp.dma_start(MK[:], mask[bass.ds(c, 1)].rearrange("a (t p) n -> p (a t) n", p=P)).then_inc(mask_in, 16)

            def store_first(c, tiles):
                sp.wait_ge(x1_made, tiles)
                gate(sp)
                sp.dma_start(x1_d[bass.ds(c, 1)].rearrange("a (t p) d -> p (a t) d", p=P), x1[:]).then_inc(x1_st, 16)
                sp.wait_ge(y_made, tiles)
                gate(sp)
                sp.dma_start(y_d[bass.ds(c, 1)].rearrange("a (t p) d -> p (a t) d", p=P), y[:]).then_inc(y_st, 16)

            def store_second(c, n):
                sp.wait_ge(pj_out, n)
                gate(sp)
                sp.dma_start(qh_d[bass.ds(c, 1)].rearrange("a (g p) q -> p (a g) q", p=P), f32(hi[:, 0:KV, :])).then_inc(q_st, 16)
                sp.dma_start(ql_d[bass.ds(c, 1)].rearrange("a (g p) q -> p (a g) q", p=P), f32(lo[:, 0:KV, :])).then_inc(q_st, 16)
                sp.dma_start(kh_d[bass.ds(c, 1)].rearrange("a p q -> p (a q)"), f32(hi[:, KV, :])).then_inc(k_st, 16)
                sp.dma_start(kl_d[bass.ds(c, 1)].rearrange("a p q -> p (a q)"), f32(lo[:, KV, :])).then_inc(k_st, 16)
                sp.dma_start(v_d[bass.ds(c, 1)].rearrange("a (t p) n -> p (a t) n", p=P), val[:]).then_inc(v_st, 16)

            load(0)
            sp.wait_ge(qn_made, TT)
            sp.wait_ge(xb_made, 1)
            sp.wait_ge(pen_made, 1)
            load(1)
            store_first(0, TT)
            with sp.Fori(1, NC - 1) as i:
                nxt, prev = sp.snap(i + 1), sp.snap(i - 1)
                one_n, out_n = sp.snap(i + 1), sp.snap(i * (NM + 1))
                tiles_n = sp.snap(i * TT + TT)
                sp.wait_ge(qn_made, tiles_n)
                gate(sp)
                sp.wait_ge(xb_made, one_n)
                gate(sp)
                sp.wait_ge(pen_made, one_n)
                gate(sp)
                load(nxt)
                store_second(prev, out_n)
                store_first(i, tiles_n)
            store_second(NC - 2, (NC - 1) * (NM + 1))
            store_first(NC - 1, NC * TT)
            store_second(NC - 1, NC * (NM + 1))
            for sem, n in ((x1_st, NC), (y_st, NC), (q_st, 2 * NC), (k_st, 2 * NC), (v_st, NC), (x_in, NC), (mask_in, NC)):
                sp.wait_ge(sem, 16 * n)

        @block.gpsimd
        def _(pool):
            make_identity(nc, pool, ident, ident_zero, ident_made)
            nc.gpsimd.memset(half[:], -0.5).then_inc(half_made, 1)
            pool.wait_ge(half_made, 1)

            def power(j, c, src):
                gate(pool)
                nc.gpsimd.tensor_scalar(var[:, j, :], src, LN_EPS, None, ALU.add).then_inc(vared[j], 1)
                pool.wait_ge(vared[j], c + 1)
                nc.gpsimd.tensor_tensor(rstd[:, j, :], var[:, j, :], half[:], ALU.pow).then_inc(rs[j], 1)

            def chunk(c, first=False):
                pool.wait_ge(aggr[0], TT * c + TT)
                power(0, c, mv[:, 0, :, 1])
                pool.wait_ge(x_in, 16 * c + 16)
                if not first:
                    pool.wait_ge(x1_made, TT * c)
                for t in range(TT):
                    last = nc.gpsimd.tensor_tensor(xb[:, t, :], X[:, t, :], beta_row[:], ALU.add)
                last.then_inc(xb_made, 1)
                pool.wait_ge(vr1, 2 * c + 2)
                power(1, c, vr[:])
                pool.wait_ge(xb_made, c + 1)
                if not first:
                    pool.wait_ge(x1_st, 16 * c)
                    pool.wait_ge(y_made, TT * c)
                for t in range(TT):
                    pool.wait_ge(att_n, TT * c + t + 1)
                    nc.gpsimd.tensor_tensor(att[:, t, :], att[:, t, :], gamma_row[:], ALU.mult).then_inc(att_g, 1)
                    pool.wait_ge(att_g, TT * c + t + 1)
                    nc.gpsimd.tensor_tensor(x1[:, t, :], att[:, t, :], xb[:, t, :], ALU.add).then_inc(x1_made, 1)
                pool.wait_ge(aggr[2], TT * c + TT)
                power(2, c, mv[:, 2, :, 1])

            pool.wait_ge(vec_in, 16 * 7)
            chunk(0, first=True)
            with pool.Fori(1, NC) as i:
                chunk(i)

        @block.scalar
        def _(act):
            act.dma_start(ctx_n[:], ctx.rearrange("b r d -> r b d")).then_inc(ctx_in, 16)
            act.dma_start(gamma_row[:], over_rows(gamma)).then_inc(vec_in, 16)
            act.dma_start(beta_row[:], over_rows(beta)).then_inc(vec_in, 16)
            act.dma_start(vb_row[:], over_rows(vb)).then_inc(vec_in, 16)
            qb_v = qb.rearrange("(g p a) -> g p a", p=P, a=1)
            for g in range(KV):
                act.dma_start(b_col[:, g:g + 1], qb_v[g]).then_inc(vec_in, 16)
            act.dma_start(b_col[:, KV:NM], kb.rearrange("(p a) -> p a", a=1)).then_inc(vec_in, 16)
            act.wait_ge(ctx_tr, 1)
            nc.scalar.activation(ctx_t[:, 0, :, :], ps_t[:, 0, 0:DK * P].rearrange("p (k n) -> p k n", k=DK)[:, :, 0:CT], ACT.Copy).then_inc(ctx_t_made, 1)
            act.wait_ge(ctx_tr, 2)
            nc.scalar.activation(ctx_t[:, 1, :, :], ps_t[:, 1, 0:DK * P].rearrange("p (k n) -> p k n", k=DK)[:, :, 0:CT], ACT.Copy).then_inc(ctx_t_made, 1)
            act.wait_ge(w_in, 48)
            for k in range(DK):
                nc.scalar.activation(w_hi[:, k, :], w_raw[:, k, :], ACT.Copy).then_inc(wh_made, 1)
            act.wait_ge(vec_in, 16 * 8)

            def first_part(c, first=False):
                for k in range(DK):
                    act.wait_ge(q_tr, DK * c + k + 1)
                    if not first:
                        act.wait_ge(lg_mm, c)
                    nc.scalar.activation(qT[:, k, :], ps_t[:, k % 2, :], ACT.Copy).then_inc(qT_made, 1)
                act.wait_ge(nmx_made, c + 1)
                if not first:
                    act.wait_ge(p_tr, c)
                    act.wait_ge(rinv_made, c)
                for t in range(TT):
                    nc.scalar.activation(pr[:, t, :], lg[:, t, :], ACT.Exp, bias=nmx[:, t:t + 1],
                                         accum_out=psum_e[:, t:t + 1]).then_inc(pr_made, 1)

            def first_end(c, first=False):
                act.wait_ge(p_tr, c + 1)
                if not first:
                    act.wait_ge(o_mm, TT * c)
                nc.scalar.activation(prT[:], ps_pt[0:CT, :], ACT.Copy).then_inc(prT_made, 1)
                if not first:
                    act.wait_ge(x1_made, TT * c)
                for t in range(TT):
                    act.wait_ge(o_mm, TT * c + t + 1)
                    nc.scalar.activation(att[:, t, :], ps_o[:, t % 2, :], ACT.Copy).then_inc(att_made, 1)

            def second_high(c, first=False):
                if not first:
                    act.wait_ge(pj_mm, (NM + 1) * c)
                for k in range(DK):
                    act.wait_ge(y_tr, DK * c + k + 1)
                    nc.scalar.activation(yTh[:, k, :], ps_t[:, k % 2, :], ACT.Copy).then_inc(yh_made, 1)

            def second_project(c, ms, first=False):
                for m in ms:
                    if not first and m == 0:
                        act.wait_ge(q_st, 32 * c)
                        act.wait_ge(k_st, 32 * c)
                    act.wait_ge(pj_mm, (NM + 1) * c + m + 1)
                    nc.scalar.activation(hi[:, m, :], ps_pj[:, m % 2, :], ACT.Identity, bias=b_col[:, m:m + 1]).then_inc(hi_made, 1)

            first_part(0, first=True)
            first_end(0, first=True)
            first_part(1)
            second_high(0, first=True)
            second_project(0, range(2), first=True)
            first_end(1)
            second_project(0, range(2, NM), first=True)
            with act.Fori(2, NC) as i:
                first_part(i)
                second_high(i - 1)
                second_project(i - 1, range(2))
                first_end(i)
                second_project(i - 1, range(2, NM))
            second_high(NC - 1)
            second_project(NC - 1, range(NM))

        @block.vector
        def _(dve):
            dve.wait_ge(w_in, 48)
            for k in range(DK):
                dve.wait_ge(wh_made, k + 1)
                nc.vector.tensor_tensor(w_lo[:, k, :], w_raw[:, k, :], f32(w_hi[:, k, :]), ALU.subtract).then_inc(wl_made, 1)
            dve.wait_ge(vec_in, 16 * 8)

            def moments(j, c, src, ready=None):
                for t in range(TT):
                    if ready is not None:
                        dve.wait_ge(ready, TT * c + t + 1)
                    nc.vector.bn_stats(stats[:, j, t, :], src[:, t, :]).then_inc(stat[j], 1)
                dve.wait_ge(stat[j], TT * c + TT)
                gate(dve)
                for t in range(TT):
                    nc.vector.bn_aggr(mv[:, j, t, :], stats[:, j, t, :]).then_inc(aggr[j], 1)

            def head(c, first=False):
                dve.wait_ge(x_in, 16 * c + 16)
                moments(0, c, X)
                dve.wait_ge(aggr[0], TT * c + TT)
                dve.wait_ge(mask_in, 16 * c + 16)
                if not first:
                    dve.wait_ge(lg_made, c)
                nc.vector.tensor_scalar(pen[:], MK[:], 0, NEG, ALU.is_equal, ALU.mult).then_inc(pen_made, 1)
                dve.wait_ge(rs[0], c + 1)
                if not first:
                    dve.wait_ge(q_tr, DK * c)
                for t in range(TT):
                    nc.vector.tensor_scalar(qn[:, t, :], X[:, t, :], mv[:, 0, t, 0:1], rstd[:, 0, t:t + 1],
                                            ALU.subtract, ALU.mult).then_inc(qn_made, 1)

            def softmax(c, first=False):
                dve.wait_ge(lg_mm, c + 1)
                dve.wait_ge(pen_made, c + 1)
                if not first:
                    dve.wait_ge(pr_made, TT * c)
                nc.vector.scalar_tensor_tensor(lg[:], ps_lg[:, :, 0:CT], float(D) ** -0.5, pen[:], ALU.mult, ALU.add).then_inc(lg_made, 1)
                dve.wait_ge(lg_made, c + 1)
                nc.vector.reduce_max(mx[:], lg[:], AXX).then_inc(mx_made, 1)
                dve.wait_ge(mx_made, c + 1)
                nc.vector.tensor_scalar(nmx[:], mx[:], -1.0, None, ALU.mult).then_inc(nmx_made, 1)

            def tail(c, first=False):
                dve.wait_ge(pr_made, TT * c + TT)
                nc.vector.reciprocal(rinv[:], psum_e[:]).then_inc(rinv_made, 1)
                moments(1, c, att, att_made)
                dve.wait_ge(aggr[1], TT * c + TT)
                dve.wait_ge(rinv_made, c + 1)
                nc.vector.tensor_tensor(vr[:], mv[:, 1, :, 1], rinv[:], ALU.mult).then_inc(vr1, 1)
                dve.wait_ge(vr1, 2 * c + 1)
                nc.vector.tensor_tensor(vr[:], vr[:], rinv[:], ALU.mult).then_inc(vr1, 1)
                dve.wait_ge(rs[1], c + 1)
                nc.vector.tensor_tensor(s2[:], rstd[:, 1, :], rinv[:], ALU.mult).then_inc(s2_made, 1)
                dve.wait_ge(s2_made, c + 1)
                for t in range(TT):
                    nc.vector.tensor_scalar(att[:, t, :], att[:, t, :], mv[:, 1, t, 0:1], s2[:, t:t + 1],
                                            ALU.subtract, ALU.mult).then_inc(att_n, 1)
                moments(2, c, x1, x1_made)
                dve.wait_ge(aggr[2], TT * c + TT)
                dve.wait_ge(rs[2], c + 1)
                if not first:
                    dve.wait_ge(y_tr, DK * c)
                    dve.wait_ge(y_st, 16 * c)
                for t in range(TT):
                    nc.vector.tensor_scalar(y[:, t, :], x1[:, t, :], mv[:, 2, t, 0:1], rstd[:, 2, t:t + 1],
                                            ALU.subtract, ALU.mult).then_inc(y_made, 1)

            def second_low(c, first=False):
                for k in range(DK):
                    dve.wait_ge(yh_made, DK * c + k + 1)
                    nc.vector.tensor_tensor(yTl[:, k, :], ps_t[:, k % 2, :], f32(yTh[:, k, :]), ALU.subtract).then_inc(yl_made, 1)

            def second_project(c, ms, first=False):
                for m in ms:
                    if not first and m == 0:
                        dve.wait_ge(q_st, 32 * c)
                        dve.wait_ge(k_st, 32 * c)
                        dve.wait_ge(v_st, 16 * c)
                    if m < NM:
                        dve.wait_ge(hi_made, NM * c + m + 1)
                        nc.vector.scalar_tensor_tensor(lo[:, m, :], ps_pj[:, m % 2, :], b_col[:, m:m + 1], f32(hi[:, m, :]),
                                                       ALU.add, ALU.subtract).then_inc(pj_out, 1)
                    else:
                        dve.wait_ge(pj_mm, (NM + 1) * c + m + 1)
                        nc.vector.tensor_tensor(val[:], ps_pj[:, m % 2, :].rearrange("p (t n) -> p t n", t=TT),
                                                vb_row[:].rearrange("p (a n) -> p a n", a=1).broadcast_to((P, TT, P)),
                                                ALU.add).then_inc(pj_out, 1)

            head(0, first=True)
            softmax(0, first=True)
            tail(0, first=True)
            head(1)
            softmax(1)
            second_low(0, first=True)
            second_project(0, range(2), first=True)
            tail(1)
            second_project(0, range(2, NM + 1), first=True)
            with dve.Fori(2, NC) as i:
                head(i)
                softmax(i)
                second_low(i - 1)
                second_project(i - 1, range(2))
                tail(i)
                second_project(i - 1, range(2, NM + 1))
            second_low(NC - 1)
            second_project(NC - 1, range(NM + 1))

        @block.tensor
        def _(pe):
            pe.wait_ge(ident_made, 1)
            pe.wait_ge(ctx_in, 16)
            for b in range(B):
                for k in range(DK):
                    last = nc.tensor.transpose(ps_t[:, b, k * P:k * P + CT], ctx_n[:, b, k * P:(k + 1) * P], ident[0:CT, 0:CT])
                last.then_inc(ctx_tr, 1)
            pe.wait_ge(ctx_t_made, 2)
            pe.wait_ge(wl_made, DK)

            def transposes(c, src, ready, done, evacuated):
                pe.wait_ge(ready, TT * c + TT)
                for k in range(DK):
                    if k >= 2:
                        pe.wait_ge(evacuated, DK * c + k - 1)
                    for t in range(TT):
                        last = nc.tensor.transpose(ps_t[:, k % 2, t * P:(t + 1) * P], src[:, t, k * P:(k + 1) * P], ident[:])
                    last.then_inc(done, 1)

            def first_part(c, first=False):
                transposes(c, qn, qn_made, q_tr, qT_made)
                pe.wait_ge(qT_made, DK * c + DK)
                if not first:
                    pe.wait_ge(lg_made, c)
                for t in range(TT):
                    for k in range(DK):
                        last = nc.tensor.matmul(ps_lg[:, t, 0:CT], qT[:, k, t * P:(t + 1) * P], ctx_t[:, batch(c), k, :].rearrange("p a n -> p (a n)"),
                                                start=(k == 0), stop=(k == DK - 1))
                last.then_inc(lg_mm, 1)

            def batch(c):
                return slice(0, 1) if isinstance(c, int) else bass.ds(c // CB, 1)

            def first_end(c, first=False):
                pe.wait_ge(pr_made, TT * c + TT)
                if not first:
                    pe.wait_ge(prT_made, c)
                for t in range(TT):
                    last = nc.tensor.transpose(ps_pt[0:CT, t * P:(t + 1) * P], pr[:, t, :], ident[:])
                last.then_inc(p_tr, 1)
                pe.wait_ge(prT_made, c + 1)
                for t in range(TT):
                    if not first or t >= 2:
                        pe.wait_ge(att_made, TT * c + t - 1)
                    nc.tensor.matmul(ps_o[:, t % 2, :], prT[:, t * P:(t + 1) * P], ctx_n[:, batch(c), :].rearrange("p a n -> p (a n)"),
                                     start=True, stop=True).then_inc(o_mm, 1)

            def second_transposes(c):
                transposes(c, y, y_made, y_tr, yl_made)
                pe.wait_ge(yl_made, DK * c + DK)

            def second_project(c, ms, first=False):
                for m in ms:
                    if not first or m >= 2:
                        pe.wait_ge(pj_out, (NM + 1) * c + m - 1)
                    if m < NM:
                        for k in range(DK):
                            cols = slice(m * P, (m + 1) * P)
                            last = mm3(nc, ps_pj[:, m % 2, :], w_hi[:, k, cols], w_lo[:, k, cols], yTh[:, k, :], yTl[:, k, :],
                                       k == 0, k == DK - 1)
                    else:
                        for t in range(TT):
                            for k in range(DK):
                                toks = slice(t * P, (t + 1) * P)
                                last = mm3(nc, ps_pj[:, m % 2, toks], yTh[:, k, toks], yTl[:, k, toks],
                                           w_hi[:, k, D + P:], w_lo[:, k, D + P:], k == 0, k == DK - 1)
                    last.then_inc(pj_mm, 1)

            first_part(0, first=True)
            first_end(0, first=True)
            first_part(1)
            second_transposes(0)
            second_project(0, range(2), first=True)
            first_end(1)
            second_project(0, range(2, NM + 1), first=True)
            with pe.Fori(2, NC) as i:
                first_part(i)
                second_transposes(i - 1)
                second_project(i - 1, range(2))
                first_end(i)
                second_project(i - 1, range(2, NM + 1))
            second_transposes(NC - 1)
            second_project(NC - 1, range(NM + 1))


def phase_attend(nc, y_d, qh_d, ql_d, kh_d, kl_d, v_d, ow, ob, norm1, gate_w, src_d, xe_d, slot_d, wt_d):
    AK, BK = 3, 2
    ORDER = ["VBDBAAABB", "VBAABABDBAAA", "BBVABBAAD", "ABBAAABBAV", "BAABVBAABA", "BVBAABAB", "VBABAABB", "VBABDABABAA",
             "BVBAABAB", "VBBDBABAA", "BABVABAABA", "BVABABADBAAA", "BBVAABAB", "DBAAABBVB", "BAAABVABB", "VBBAABABA"]
    TURN = 14
    A_AT = [sum(o.count("A") for o in ORDER[:kt]) for kt in range(KT + 1)]
    EARLY = A_AT[KT] - A_AT[TURN]

    ADDS = [(0, 0), (1, 2), (0, None), (1, 4), (0, 6), (1, 8), (0, 10), (1, 12), (1, None)]
    ADDED = {t: n + 1 for n, (_, t) in enumerate(ADDS) if t is not None}
    FREED = {1: 0, 4: 1, 5: 2, 6: 3, 7: 4}
    SUMS = [(0, 3), (1, 4), (0, 5), (1, 6), KT - 2, KT - 1, (1, 9)]
    NS = len(SUMS)
    SUM_AT = {7: 0, 9: 1, 11: 2, 13: 3, 0: 4, 1: 5, 2: 6}
    NA = G * TT * (S // CH)
    NSC = G * KT
    SCALE = float(HD) ** -0.5
    ROUTES, ROUTE_TOP = 23, 4
    ZR = 4
    NZ = E * CAP // (P * ZR)
    assert A_AT[KT] == NA
    with Scope(nc, "p2") as s:
        ident = s.sb("ident", [P, P])
        ones = s.sb("ones", [P, P])
        before = s.sb("before", [P, P])
        ow_hi = s.sb("ow_hi", [P, KV, D], F32R)
        ow_lo = s.sb("ow_lo", [P, KV, D], F32R)
        ob_row = s.sb("ob_row", [P, D])
        norm_row = s.sb("norm_row", [P, D])
        gw = s.sb("gw", [P, DK, E])
        iota_e = s.sb("iota_e", [P, E])
        ecap = s.sb("ecap", [P, E])
        KS = s.sb("KS", [98, KV, S], F32R)
        QS = s.sb("QS", [98, KV, G, CH], F32R)
        VS = s.sb("VS", [P, KV, KT, HD])
        PR = s.sb("PR", [P, 4, G, CH])
        PP = s.sb("PP", [P, 2, G, CH])
        mxp = s.sb("mxp", [P, TT * G, S // CH])
        mxv = s.sb("mxv", [P, TT, G])
        mh = s.sb("mh", [G, CH], F32R)
        ml = s.sb("ml", [G, CH], F32R)
        pvs = s.sb("pvs", [P, CH])
        att = s.sb("att", [P, CH])
        dens = s.sb("dens", [P, CH])
        at_hi = s.sb("at_hi", [P, KV, CH], F32R)
        at_lo = s.sb("at_lo", [P, KV, CH], F32R)
        Y = s.sb("Y", [P, TT, D])
        SR = s.sb("SR", [P, TT, D])
        srT = s.sb("srT", [P, TT, DK, P])
        sq = s.sb("sq", [P, D])
        ss = s.sb("ss", [P, TT])
        sv = s.sb("sv", [P, TT])
        sr_rstd = s.sb("sr_rstd", [P, TT])
        half = s.sb("half", [P, TT])
        lgt = s.sb("lgt", [P, TT, E])
        top = s.sb("top", [P, TT, 8])
        topi = s.sb("topi", [P, TT, 8], U32)
        topf = s.sb("topf", [P, TT, 2])
        oh = s.sb("oh", [P, 2, TT, E])
        sel = s.sb("sel", [P, TT, E])
        pe_ = s.sb("pe_", [P, TT, 2])
        wsum = s.sb("wsum", [P, TT])
        prefix = s.sb("prefix", [P, TT, E])
        base = s.sb("base", [P, TT + 1, E])
        total = s.sb("total", [P, TT, E])
        room = s.sb("room", [P, TT, E])
        prod = s.sb("prod", [P, TT, E])
        slot = s.sb("slot", [P, 2, TT])
        ok = s.sb("ok", [P, 2, TT])
        far = s.sb("far", [P, 2, TT])
        to_slot = s.sb("to_slot", [P, 2, TT], I32)
        from_slot = s.sb("from_slot", [P, 2, TT], I32)
        wt = s.sb("wt", [P, 2, TT])
        ps_a = s.ps("ps_a", [P, AK, CH])
        ps_b = s.ps("ps_b", [P, BK, CH])
        ps_pv = s.ps("ps_pv", [P, CH])
        ps_den = s.ps("ps_den", [P, CH])
        ps_m = s.ps("ps_m", [P, CH])

        (const_in, ident_zero, ident_made, const_made, owh_made, owl_made, zero_made, zero_st) = (
            s.sem(n) for n in ("const_in", "ident_zero", "ident_made", "const_made", "owh_made", "owl_made", "zero_made", "zero_st"))
        q_in = [s.sem(f"q_in{g}") for g in range(KV)]
        v_in = [s.sem(f"v_in{g}") for g in range(KV)]
        m_in = s.sem("m_in")
        a_mm, mxp_made, mxv_made, m_tr, mh_made, ml_made = (s.sem(n) for n in ("a_mm", "mxp_made", "mxv_made", "m_tr", "mh_made", "ml_made"))
        sc_mm, ex_made, add_made, pv_mm, den_mm = (s.sem(n) for n in ("sc_mm", "ex_made", "add_made", "pv_mm", "den_mm"))
        pvs_made, dens_made, att_made, ath_made, atl_made = (s.sem(n) for n in ("pvs_made", "dens_made", "att_made", "ath_made", "atl_made"))
        y_in, yob_made, o_mm, src_made, ss_made, sv_made, rstd_made = (s.sem(n) for n in ("y_in", "yob_made", "o_mm", "src_made", "ss_made", "sv_made", "rstd_made"))
        sr_made, sr_tr, srT_made, g_mm, lgt_made = (s.sem(n) for n in ("sr_made", "sr_tr", "srT_made", "g_mm", "lgt_made"))
        route, exp_made, sel_made, rank_mm, ranked, slots_made = (s.sem(n) for n in ("route", "exp_made", "sel_made", "rank_mm", "ranked", "slots_made"))
        src_st, slot_st, wt_st, sent, gate_sem = (s.sem(n) for n in ("src_st", "slot_st", "wt_st", "sent", "gate"))
        picked, dve_const, inverted = s.sem("picked"), s.sem("dve_const"), s.sem("inverted")
        block = s.block()

        def gate(eng):
            eng.sem_inc(gate_sem, 1)

        def unit(c, g):
            return KV * c + g

        def runs_ahead(c, g, kt, i, last):
            n = EARLY + A_AT[kt] + i
            off = 1 + n // NA
            return None if last and g + off >= KV else (unit(c, g) + off, (g + off) % KV, n % NA)

        @block.sync
        def _(sp):
            def hold(sem, n):
                sp.wait_ge(sem, n)
                gate(sp)

            ow_raw = PR[:, 0, :, :]
            sp.dma_start(ow_raw, ow.rearrange("(g p) n -> p g n", p=P)).then_inc(const_in, 16)
            sp.dma_start(ob_row[:], over_rows(ob)).then_inc(const_in, 16)
            sp.dma_start(norm_row[:], over_rows(norm1)).then_inc(const_in, 16)
            sp.dma_start(gw[:], gate_w.rearrange("(k p) e -> p k e", p=P)).then_inc(const_in, 16)

            def load(c, g):
                row = c // CB * CB
                heads = slice(G * HD * g, G * HD * (g + 1))
                for part, src in ((0, qh_d), (1, qh_d), (2, ql_d)):
                    sp.dma_start(f32(QS[32 * part:32 * part + 32, g, :, :]),
                                 src[bass.ds(c, 1), heads, :].rearrange("a (j d) q -> d (a j) q", d=HD)).then_inc(q_in[g], 16)
                for part, src in ((0, kh_d), (1, kl_d), (2, kh_d)):
                    sp.dma_start(f32(KS[32 * part:32 * part + 32, g, :]).rearrange("d (n q) -> d n q", n=CB),
                                 src[bass.ds(row, CB), HD * g:HD * (g + 1), :].rearrange("n d q -> d n q")).then_inc(q_in[g], 16)
                sp.dma_start(VS[:, g, :, :].rearrange("p (n t) d -> p n t d", n=CB),
                             v_d[bass.ds(row, CB), :, HD * g:HD * (g + 1)].rearrange("n (t p) d -> p n t d", p=P)).then_inc(v_in[g], 16)

            def load_y(c):
                sp.dma_start(Y[:], y_d[bass.ds(c, 1)].rearrange("a (t p) d -> p (a t) d", p=P)).then_inc(y_in, 16)

            def maxima_to(g, n):
                hold(ml_made, n)
                sp.dma_start(f32(QS[96:97, g, :, :]), f32(mh[:])).then_inc(m_in, 16)
                sp.dma_start(f32(QS[97:98, g, :, :]), f32(ml[:])).then_inc(m_in, 16)

            def body(c, first=False, last=False):
                nxt = None if last else (c + 1 if isinstance(c, int) else sp.snap(c + 1))
                for g in range(KV):
                    if not (last and g == KV - 1):
                        maxima_to((g + 1) % KV, unit(c, g) + 2)
                    if g == 0 and not first:
                        hold(sr_made, TT * c)
                        sp.dma_start(src_d[bass.ds(c - 1, 1)].rearrange("a (t p) d -> p (a t) d", p=P), SR[:]).then_inc(src_st, 16)
                        if not first:
                            hold(src_made, TT * c)
                    if g == 0:
                        load_y(c)
                    if first:
                        with sp.Fori(NZ // KV * g, NZ // KV * (g + 1)) as i:
                            sp.dma_start(xe_rows[bass.ds(i, 1)].rearrange("a p n -> p (a n)"), zeros).then_inc(zero_st, 16)
                    if g == 2 and not first:
                        hold(slots_made, c)
                        store_slots(c - 1)
                    if not last:
                        hold(sc_mm, NSC * (unit(c, g) + 1))
                        hold(pv_mm, KT * (unit(c, g) + 1))
                        load(nxt, g)

            def store_slots(c):
                sp.dma_start(slot_d[bass.ds(c, 1)].rearrange("a p n -> p (a n)"), from_slot[:].rearrange("p k t -> p (k t)")).then_inc(slot_st, 16)
                sp.dma_start(wt_d[bass.ds(c, 1)].rearrange("a p n -> p (a n)"), wt[:].rearrange("p k t -> p (k t)")).then_inc(wt_st, 16)

            for g in range(KV):
                load(0, g)
            zeros = SR[:].rearrange("p t d -> p (t d)")
            xe_rows = xe_d.rearrange("(n p r) d -> n p (r d)", p=P, r=ZR)
            hold(zero_made, 1)
            maxima_to(0, 1)
            body(0, first=True)
            with sp.Fori(1, NC - 1) as i:
                body(i)
            body(NC - 1, last=True)
            hold(sr_made, TT * NC)
            sp.dma_start(src_d[NC - 1].rearrange("(t p) d -> p t d", p=P), SR[:]).then_inc(src_st, 16)
            hold(slots_made, NC)
            store_slots(NC - 1)
            for sem in (src_st, slot_st, wt_st, y_in):
                sp.wait_ge(sem, 16 * NC)
            sp.wait_ge(sent, 16 * 2 * TT * NC)
            sp.wait_ge(zero_st, 16 * NZ)

        @block.gpsimd
        def _(pool):
            make_identity(nc, pool, ident, ident_zero, ident_made)
            nc.gpsimd.memset(ones[:], 1.0).then_inc(const_made, 1)
            nc.gpsimd.memset(half[:], -0.5).then_inc(const_made, 1)
            for e in range(E):
                nc.gpsimd.memset(iota_e[:, e:e + 1], float(e)).then_inc(const_made, 1)
                nc.gpsimd.memset(ecap[:, e:e + 1], float(e * CAP)).then_inc(const_made, 1)
            pool.wait_ge(const_made, 2 + 2 * E)
            nc.gpsimd.affine_select(out=before[:], in_=ones[:], compare_op=ALU.is_gt, fill=0.0, base=0,
                                    pattern=[[1, P]], channel_multiplier=-1).then_inc(const_made, 1)
            pool.wait_ge(const_in, 64)

            def add(u, n, first):
                buf, tile = ADDS[n]
                if n in FREED and not (first and FREED[n] == 0):
                    pool.wait_ge(den_mm, NS * u + FREED[n])
                if tile is None:
                    pool.wait_ge(add_made, len(ADDS) * u + n)
                    nc.gpsimd.tensor_tensor(PP[:, buf, :, :], PP[:, buf, :, :], PP[:, 1 - buf, :, :], ALU.add).then_inc(add_made, 1)
                else:
                    pool.wait_ge(ex_made, NSC * u + G * (tile + 2))
                    if ADDS[n - 1][1] is None and not (first and n == 0):
                        pool.wait_ge(add_made, len(ADDS) * u + n)
                    a = tile % 4
                    nc.gpsimd.tensor_tensor(PP[:, buf, :, :], PR[:, a, :, :], PR[:, a + 1, :, :], ALU.add).then_inc(add_made, 1)

            def add_bias(c):
                pool.wait_ge(y_in, 16 * c + 16)
                for t in range(TT):
                    nc.gpsimd.tensor_tensor(Y[:, t, :], Y[:, t, :], ob_row[:], ALU.add).then_inc(yob_made, 1)

            def norm_power(c):
                pool.wait_ge(ss_made, TT * c + TT)
                gate(pool)
                nc.gpsimd.tensor_scalar(sv[:], ss[:], 1.0 / D, RMS_EPS, ALU.mult, ALU.add).then_inc(sv_made, 1)
                pool.wait_ge(sv_made, c + 1)
                nc.gpsimd.tensor_tensor(sr_rstd[:], sv[:], half[:], ALU.pow).then_inc(rstd_made, 1)

            def send(c):
                pool.wait_ge(zero_st, 16 * NZ)
                pool.wait_ge(slots_made, c + 1)
                gate(pool)
                for k in range(2):
                    for t in range(TT):
                        nc.gpsimd.indirect_dma_start(
                            out=xe_d, out_offset=bass.IndirectOffsetOnAxis(ap=to_slot[:, k, t:t + 1].bitcast(U32), axis=0),
                            in_=SR[:, t, :], in_offset=None, bounds_check=E * CAP - 1, oob_is_err=False).then_inc(sent, 16)

            def body(c, first=False):
                for g in range(KV):
                    for n in range(len(ADDS)):
                        add(unit(c, g), n, first and g == 0)
                        if g == 0 and not first:
                            if n == 4:
                                norm_power(c - 1)
                        if g == 1 and not first and n == 8:
                            send(c - 1)
                        if g == 3 and n == 7:
                            add_bias(c)

            body(0, first=True)
            with pool.Fori(1, NC) as i:
                body(i)
            norm_power(NC - 1)
            send(NC - 1)

        @block.scalar
        def _(act):
            ow_raw = PR[:, 0, :, :]
            act.wait_ge(const_in, 64)
            for g in range(KV):
                nc.scalar.activation(ow_hi[:, g, :], ow_raw[:, g, :], ACT.Copy).then_inc(owh_made, 1)
            act.wait_ge(owl_made, KV)

            def exps(c, g, kt, first):
                u = unit(c, g)
                slot_ = kt % 4
                if kt >= 4:
                    act.wait_ge(pv_mm, KT * u + kt - 3)
                    act.wait_ge(add_made, len(ADDS) * u + ADDED[(kt - 4) // 2 * 2])
                elif not first:
                    act.wait_ge(pv_mm, KT * u + kt - 3)
                    if kt < 2:
                        act.wait_ge(add_made, len(ADDS) * (u - 1) + ADDED[KT - 4])
                    else:
                        act.wait_ge(den_mm, NS * u + kt - 4)
                for j in range(G):
                    n = NSC * g + G * kt + j
                    act.wait_ge(sc_mm, NSC * KV * c + n + 1)
                    nc.scalar.activation(PR[:, slot_, j, :], ps_b[:, n % BK, :], ACT.Exp, scale=SCALE).then_inc(ex_made, 1)

            def values_out(u, first=False):
                act.wait_ge(pv_mm, KT * u)
                if not first:
                    act.wait_ge(att_made, u - 1)
                nc.scalar.activation(pvs[:], ps_pv[:], ACT.Copy).then_inc(pvs_made, 1)

            def sums_out(u):
                act.wait_ge(den_mm, NS * u)
                nc.scalar.activation(dens[:], ps_den[:], ACT.Copy).then_inc(dens_made, 1)

            def squares(c, t):
                act.wait_ge(src_made, TT * c + t + 1)
                if t > 0:
                    act.wait_ge(ss_made, TT * c + t)
                nc.scalar.activation(sq[:], SR[:, t, :], ACT.Square, accum_out=ss[:, t:t + 1]).then_inc(ss_made, 1)

            def rows_out(c, t):
                act.wait_ge(sr_tr, TT * c + t + 1)
                nc.scalar.activation(srT[:, t, :, :], ps_m[:].rearrange("p (k n) -> p k n", k=DK), ACT.Copy).then_inc(srT_made, 1)

            def sigmoid_exp(c):
                act.wait_ge(route, ROUTE_TOP + ROUTES * c)
                nc.scalar.activation(pe_[:], top[:, :, 0:2], ACT.Exp, scale=-1.0).then_inc(exp_made, 1)

            def body(c, first=False):
                for g in range(KV):
                    for kt in range(KT):
                        exps(c, g, kt, first and g == 0)
                        if kt == 1 and not (first and g == 0):
                            values_out(unit(c, g), first and g == 1)
                        if kt == 2 and not (first and g == 0):
                            sums_out(unit(c, g))
                        if g == 0 and not first:
                            if 7 <= kt < 7 + TT:
                                squares(c - 1, kt - 7)
                            if 11 <= kt < 11 + TT:
                                rows_out(c - 1, kt - 11)
                        if g == 1 and not first and kt == 3:
                            sigmoid_exp(c - 1)

            body(0, first=True)
            with act.Fori(1, NC) as i:
                body(i)
            values_out(KV * NC)
            sums_out(KV * NC)
            for t in range(TT):
                squares(NC - 1, t)
            for t in range(TT):
                rows_out(NC - 1, t)
            sigmoid_exp(NC - 1)

        @block.vector
        def _(dve):
            ow_raw = PR[:, 0, :, :]
            nc.vector.memset(SR[:], 0.0).then_inc(zero_made, 1)
            nc.vector.memset(f32(KS[96:98, :, :]), 1.0).then_inc(dve_const, 1)
            nc.vector.memset(base[:, TT, :], 0.0).then_inc(dve_const, 1)
            for g in range(KV):
                dve.wait_ge(owh_made, g + 1)
                nc.vector.tensor_tensor(ow_lo[:, g, :], ow_raw[:, g, :], f32(ow_hi[:, g, :]), ALU.subtract).then_inc(owl_made, 1)
            dve.wait_ge(const_made, 3 + 2 * E)
            dve.wait_ge(dve_const, 2)
            dve.wait_ge(ident_made, 1)

            def maximum(u, g, a):
                dve.wait_ge(a_mm, NA * u + a + 1)
                if a == 0 and not (isinstance(u, int) and u == 0):
                    dve.wait_ge(mxv_made, u)
                nc.vector.reduce_max(mxp[:, a // (S // CH), a % (S // CH):a % (S // CH) + 1], ps_a[:, (NA * g + a) % AK, :], AXX).then_inc(mxp_made, 1)

            def maxima(u, first=False):
                dve.wait_ge(mxp_made, NA * (u + 1))
                if not first:
                    dve.wait_ge(m_tr, u)
                nc.vector.reduce_max(mxv[:].rearrange("p t j -> p (t j)"), mxp[:], AXX).then_inc(mxv_made, 1)

            def maxima_split(u, first=False):
                dve.wait_ge(m_tr, u + 1)
                if not first:
                    dve.wait_ge(m_in, 32 * u)
                nc.vector.tensor_scalar(mh[:], ps_m[0:G, :], -1.0, None, ALU.mult).then_inc(mh_made, 1)
                dve.wait_ge(mh_made, u + 1)
                nc.vector.scalar_tensor_tensor(ml[:], ps_m[0:G, :], -1.0, f32(mh[:]), ALU.mult, ALU.subtract).then_inc(ml_made, 1)

            def invert(u, part):
                dve.wait_ge(dens_made, u + 1)
                cols = slice(part * P, (part + 1) * P)
                nc.vector.reciprocal(dens[:, cols], dens[:, cols]).then_inc(inverted, 1)

            def normalise(u, g):
                dve.wait_ge(inverted, TT * u + TT)
                nc.vector.tensor_tensor(att[:], pvs[:], dens[:], ALU.mult).then_inc(att_made, 1)
                dve.wait_ge(att_made, u + 1)
                nc.vector.tensor_copy(at_hi[:, g, :], att[:]).then_inc(ath_made, 1)
                dve.wait_ge(ath_made, u + 1)
                nc.vector.tensor_tensor(at_lo[:, g, :], att[:], f32(at_hi[:, g, :]), ALU.subtract).then_inc(atl_made, 1)

            def project_out(c, t):
                dve.wait_ge(o_mm, TT * c + t + 1)
                dve.wait_ge(yob_made, TT * c + t + 1)
                if t == 0:
                    dve.wait_ge(zero_st, 16 * NZ)
                if not (isinstance(c, int) and c == 0) and t == 0:
                    dve.wait_ge(src_st, 16 * c)
                    dve.wait_ge(sent, 16 * 2 * TT * c)
                nc.vector.tensor_tensor(SR[:, t, :], ps_m[:], Y[:, t, :], ALU.add).then_inc(src_made, 1)

            def norm(c, t):
                dve.wait_ge(rstd_made, c + 1)
                nc.vector.scalar_tensor_tensor(SR[:, t, :], SR[:, t, :], sr_rstd[:, t:t + 1], norm_row[:], ALU.mult, ALU.mult).then_inc(sr_made, 1)

            def per_token(ap):
                return ap.rearrange("p (t a) -> p t a", a=1).broadcast_to((P, TT, E))

            def per_expert(ap):
                return ap.rearrange("p (a e) -> p a e", a=1).broadcast_to((P, TT, E))

            def step(c, k):
                dve.wait_ge(route, ROUTES * c + k)

            def choose(c):
                dve.wait_ge(g_mm, c + 1)
                if not (isinstance(c, int) and c == 0):
                    dve.wait_ge(exp_made, c)
                nc.vector.tensor_scalar(lgt[:], ps_m[:, 0:TT * E].rearrange("p (t e) -> p t e", t=TT), 17.5, None, ALU.min).then_inc(lgt_made, 1)
                dve.wait_ge(lgt_made, c + 1)
                gate(dve)
                for t in range(TT):
                    nc.vector.max(top[:, t, :], lgt[:, t, :]).then_inc(route, 1)

            def choose_both(c):
                step(c, TT)
                gate(dve)
                for t in range(TT):
                    nc.vector.max_index(topi[:, t, :], top[:, t, :], lgt[:, t, :]).then_inc(route, 1)
                step(c, 8)
                nc.vector.tensor_copy(topf[:], topi[:, :, 0:2]).then_inc(route, 1)
                step(c, 9)
                for k in range(2):
                    nc.vector.tensor_tensor(oh[:, k, :, :], topf[:, :, k:k + 1].broadcast_to((P, TT, E)), per_expert(iota_e[:]), ALU.is_equal).then_inc(route, 1)
                step(c, 11)
                nc.vector.tensor_tensor(sel[:], oh[:, 0, :, :], oh[:, 1, :, :], ALU.add).then_inc(sel_made, 1)

            def weights(c):
                dve.wait_ge(exp_made, c + 1)
                nc.vector.tensor_scalar(pe_[:], pe_[:], 1.0, None, ALU.add).then_inc(route, 1)
                step(c, 12)
                nc.vector.reciprocal(pe_[:], pe_[:]).then_inc(route, 1)
                step(c, 13)
                nc.vector.scalar_tensor_tensor(wsum[:], pe_[:, :, 0], 1e-6, pe_[:, :, 1], ALU.add, ALU.add).then_inc(route, 1)
                step(c, 14)
                nc.vector.reciprocal(wsum[:], wsum[:]).then_inc(route, 1)

            def rank(c):
                dve.wait_ge(rank_mm, c + 1)
                k0 = 7 * c
                nc.vector.tensor_copy(total[:], ps_m[:, TT * E:2 * TT * E].rearrange("p (t e) -> p t e", t=TT)).then_inc(ranked, 1)
                nc.vector.tensor_copy(base[:, 0, :], base[:, TT, :]).then_inc(ranked, 1)
                for t in range(TT):
                    dve.wait_ge(ranked, k0 + 2 + t)
                    nc.vector.tensor_tensor(base[:, t + 1, :], base[:, t, :], total[:, t, :], ALU.add).then_inc(ranked, 1)
                dve.wait_ge(ranked, k0 + 6)
                nc.vector.tensor_tensor(prefix[:], ps_m[:, 0:TT * E].rearrange("p (t e) -> p t e", t=TT), base[:, 0:TT, :], ALU.add).then_inc(ranked, 1)
                dve.wait_ge(ranked, k0 + 7)
                nc.vector.tensor_scalar(room[:], prefix[:], float(CAP), None, ALU.is_lt).then_inc(route, 1)
                step(c, 16)
                nc.vector.tensor_tensor(prefix[:], prefix[:], per_expert(ecap[:]), ALU.add).then_inc(route, 1)

            def place(c):
                step(c, 17)
                if not (isinstance(c, int) and c == 0):
                    dve.wait_ge(sent, 16 * 2 * TT * c)
                    dve.wait_ge(slot_st, 16 * c)
                    dve.wait_ge(wt_st, 16 * c)
                n = 0
                for k in range(2):
                    for out, of in ((slot, prefix), (ok, room)):
                        if n > 0:
                            dve.wait_ge(picked, 8 * c + 2 * n)
                        nc.vector.tensor_tensor(prod[:], oh[:, k, :, :], of[:], ALU.mult).then_inc(picked, 1)
                        dve.wait_ge(picked, 8 * c + 2 * n + 1)
                        nc.vector.reduce_sum(out[:, k, :], prod[:], AXX).then_inc(picked, 1)
                        n += 1

            def finish(c):
                dve.wait_ge(picked, 8 * c + 8)
                nc.vector.tensor_scalar(far[:], ok[:], -2.0 * E * CAP, 2.0 * E * CAP, ALU.mult, ALU.add).then_inc(route, 1)
                step(c, 18)
                nc.vector.tensor_tensor(to_slot[:], slot[:], far[:], ALU.add).then_inc(route, 1)
                nc.vector.tensor_tensor(from_slot[:], slot[:], ok[:], ALU.mult).then_inc(route, 1)
                nc.vector.tensor_tensor(wt[:], pe_[:].rearrange("p t k -> p k t"), ok[:], ALU.mult).then_inc(route, 1)
                step(c, 21)
                nc.vector.tensor_tensor(wt[:, 0, :], wt[:, 0, :], wsum[:], ALU.mult).then_inc(route, 1)
                nc.vector.tensor_tensor(wt[:, 1, :], wt[:, 1, :], wsum[:], ALU.mult).then_inc(route, 1)
                step(c, 23)
                nc.vector.tensor_copy(base[:, TT, :], base[:, TT, :]).then_inc(slots_made, 1)

            def body(c, first=False, last=False):
                for g in range(KV):
                    u = unit(c, g)
                    for kt in range(KT):
                        split_first = g == 0 and not first and kt == TURN + 1
                        if split_first:
                            maxima_split(u + 1)
                        for i in range(A_AT[kt + 1] - A_AT[kt]):
                            which = runs_ahead(c, g, kt, i, last)
                            if which:
                                maximum(*which)
                        if not (last and g == KV - 1):
                            if kt == TURN - 1:
                                maxima(u + 1)
                            if kt == TURN and not (g == 0 and not first):
                                maxima_split(u + 1)
                        if not (first and g == 0):
                            parts, done_at = ({3: (0,), 4: (1,), 5: (2, 3)}, 5) if g == 0 else ({3: (0,), 4: (1,), 5: (2,), 6: (3,)}, 7)
                            for part in parts.get(kt, ()):
                                invert(u - 1, part)
                            if kt == done_at:
                                normalise(u - 1, (g - 1) % KV)
                        if g == 0 and not first:
                            if 6 <= kt < 6 + TT:
                                project_out(c - 1, kt - 6)
                            if 10 <= kt < 10 + TT:
                                norm(c - 1, kt - 10)
                        if g == 1 and not first:
                            if kt == 1:
                                choose(c - 1)
                            if kt == 2:
                                choose_both(c - 1)
                            if kt == 4:
                                weights(c - 1)
                            if kt == 6:
                                rank(c - 1)
                            if kt == 9:
                                place(c - 1)
                            if kt == 10:
                                finish(c - 1)

            for a in range(NA):
                maximum(0, 0, a)
            maxima(0, first=True)
            for a in range(EARLY):
                maximum(1, 1, a)
            maxima_split(0, first=True)
            body(0, first=True)
            with dve.Fori(1, NC - 1) as i:
                body(i)
            body(NC - 1, last=True)
            for part in range(TT):
                invert(KV * NC - 1, part)
            normalise(KV * NC - 1, KV - 1)
            for t in range(TT):
                project_out(NC - 1, t)
            for t in range(TT):
                norm(NC - 1, t)
            choose(NC - 1)
            choose_both(NC - 1)
            weights(NC - 1)
            rank(NC - 1)
            place(NC - 1)
            finish(NC - 1)

        @block.tensor
        def _(pe):
            def score_maxima(u, g, a):
                t, j, kb = a // (G * CB), a // CB % G, a % CB
                n = NA * g + a
                pe.wait_ge(mxp_made, NA * u + a - (AK - 1 if n else 0))
                nc.tensor.matmul(ps_a[:, n % AK, :], QS[0:96, g, j, t * P:(t + 1) * P], KS[0:96, g, kb * CH:(kb + 1) * CH],
                                 start=True, stop=True).then_inc(a_mm, 1)

            def maxima_transposed(u):
                pe.wait_ge(mxv_made, u + 1)
                for t in range(TT):
                    last = nc.tensor.transpose(ps_m[0:G, t * P:(t + 1) * P], mxv[:, t, :], ident[:])
                last.then_inc(m_tr, 1)

            def scores(c, g, kt, j, first):
                n = NSC * g + G * kt + j
                if n >= BK:
                    pe.wait_ge(ex_made, NSC * KV * c + n - BK + 1)
                elif not first:
                    pe.wait_ge(ex_made, NSC * KV * c + n - BK + 1)
                nc.tensor.matmul(ps_b[:, n % BK, :], KS[:, g, kt * P:(kt + 1) * P], QS[:, g, j, :],
                                 start=True, stop=True).then_inc(sc_mm, 1)

            def values(u, g, kt):
                pe.wait_ge(ex_made, NSC * u + G * (kt + 1))
                for j in range(G):
                    last = nc.tensor.matmul(ps_pv[HD * j:HD * (j + 1), :], VS[:, g, kt, :], PR[:, kt % 4, j, :],
                                            start=(kt == 0), stop=(kt == KT - 1))
                last.then_inc(pv_mm, 1)

            def denominators(u, n):
                if isinstance(SUMS[n], tuple):
                    pe.wait_ge(add_made, len(ADDS) * u + SUMS[n][1])
                    src = PP[:, SUMS[n][0], :, :]
                else:
                    src = PR[:, SUMS[n] % 4, :, :]
                for j in range(G):
                    last = nc.tensor.matmul(ps_den[HD * j:HD * (j + 1), :], ones[:, 0:HD], src[:, j, :],
                                            start=(n == 0), stop=(n == NS - 1))
                last.then_inc(den_mm, 1)

            def project_out(c, t):
                if t == 0:
                    pe.wait_ge(atl_made, KV * (c + 1))
                    pe.wait_ge(ml_made, KV * (c + 1) + (0 if isinstance(c, int) and c == NC - 1 else 1))
                else:
                    pe.wait_ge(src_made, TT * c + t)
                for g in range(KV):
                    toks = slice(t * P, (t + 1) * P)
                    last = mm3(nc, ps_m[:], at_hi[:, g, toks], at_lo[:, g, toks], ow_hi[:, g, :], ow_lo[:, g, :],
                               g == 0, g == KV - 1)
                last.then_inc(o_mm, 1)

            def rows_transposed(c, t):
                pe.wait_ge(sr_made, TT * c + t + 1)
                if t == 0:
                    pe.wait_ge(src_made, TT * c + TT)
                else:
                    pe.wait_ge(srT_made, TT * c + t)
                for k in range(DK):
                    last = nc.tensor.transpose(ps_m[:, k * P:(k + 1) * P], SR[:, t, k * P:(k + 1) * P], ident[:])
                last.then_inc(sr_tr, 1)

            def logits(c, tiles):
                pe.wait_ge(srT_made, TT * c + TT)
                for t in tiles:
                    for k in range(DK):
                        last = nc.tensor.matmul(ps_m[:, t * E:(t + 1) * E], srT[:, t, k, :], gw[:, k, :], start=(k == 0), stop=(k == DK - 1))
                if t == TT - 1:
                    last.then_inc(g_mm, 1)

            def ranks(c):
                pe.wait_ge(sel_made, c + 1)
                nc.tensor.matmul(ps_m[:, 0:TT * E], before[:], sel[:].rearrange("p t e -> p (t e)"), start=True, stop=True)
                nc.tensor.matmul(ps_m[:, TT * E:2 * TT * E], ones[:], sel[:].rearrange("p t e -> p (t e)"), start=True, stop=True).then_inc(rank_mm, 1)

            def body(c, first=False, last=False):
                for g in range(KV):
                    u = unit(c, g)
                    ahead = not (last and g == KV - 1)
                    for kt in range(KT):
                        i, j = 0, 0
                        for what in ORDER[kt]:
                            if what == "A":
                                which = runs_ahead(c, g, kt, i, last)
                                if which:
                                    if which[2] == 0:
                                        pe.wait_ge(q_in[which[1]], 96 * (c + (g + 2) // KV) + 96)
                                    score_maxima(*which)
                                i += 1
                            elif what == "B":
                                if kt == 0 and j == 0:
                                    pe.wait_ge(m_in, 32 * (u + 1))
                                scores(c, g, kt, j, first)
                                j += 1
                            elif what == "V" and kt < 2:
                                if not (first and g == 0):
                                    values(u - 1, (g - 1) % KV, KT - 2 + kt)
                            elif what == "V":
                                if kt == 2:
                                    pe.wait_ge(v_in[g], 16 * c + 16)
                                    if not (first and g == 0):
                                        pe.wait_ge(pvs_made, u)
                                values(u, g, kt - 2)
                            elif SUM_AT[kt] >= NS - 3:
                                if not (first and g == 0):
                                    denominators(u - 1, SUM_AT[kt])
                            else:
                                if SUM_AT[kt] == 0 and not (first and g == 0):
                                    pe.wait_ge(dens_made, u)
                                denominators(u, SUM_AT[kt])
                            if kt == TURN and what == "V" and ahead and not (g == 0 and not first):
                                if g == 1 and not first:
                                    pe.wait_ge(ranked, 7 * c)
                                maxima_transposed(u + 1)
                        if g == 0 and not first:
                            if 6 <= kt < 6 + TT:
                                project_out(c - 1, kt - 6)
                            if 11 <= kt < 11 + TT:
                                rows_transposed(c - 1, kt - 11)
                        if kt == TURN and ahead and g == 0 and not first:
                            pe.wait_ge(srT_made, TT * c)
                            maxima_transposed(u + 1)
                        if kt == 15 and g == 0 and not first:
                            pe.wait_ge(ml_made, u + 2)
                            logits(c - 1, (0, 1))
                        if kt == 0 and g == 1 and not first:
                            logits(c - 1, (2, 3))
                        if kt == 5 and g == 1 and not first:
                            ranks(c - 1)

            pe.wait_ge(ident_made, 1)
            pe.wait_ge(const_made, 3 + 2 * E)
            pe.wait_ge(dve_const, 2)
            pe.wait_ge(owl_made, KV)
            pe.wait_ge(q_in[0], 96)
            for a in range(NA):
                if a < AK:
                    t, j, kb = a // (G * CB), a // CB % G, a % CB
                    nc.tensor.matmul(ps_a[:, a, :], QS[0:96, 0, j, t * P:(t + 1) * P], KS[0:96, 0, kb * CH:(kb + 1) * CH],
                                     start=True, stop=True).then_inc(a_mm, 1)
                else:
                    score_maxima(0, 0, a)
            pe.wait_ge(q_in[1], 96)
            for a in range(EARLY):
                score_maxima(1, 1, a)
            maxima_transposed(0)
            body(0, first=True)
            with pe.Fori(1, NC - 1) as i:
                body(i)
            body(NC - 1, last=True)
            for kt in range(2):
                values(KV * NC - 1, KV - 1, KT - 2 + kt)
            for n in range(NS - 3, NS):
                denominators(KV * NC - 1, n)
            for t in range(TT):
                project_out(NC - 1, t)
            for t in range(TT):
                rows_transposed(NC - 1, t)
            logits(NC - 1, range(TT))
            ranks(NC - 1)


def phase_experts(nc, xe_d, w1, w2, ye_d):
    TILES = [3, 3, 2, 2]
    NB = len(TILES)
    WB = max(TILES)
    FK = F // P
    HB = 3
    FIRST = [sum(TILES[:b]) for b in range(NB)]
    NT = sum(TILES)
    assert NT * P == CAP and NB % 2 == 0
    with Scope(nc, "p3") as s:
        ident = s.sb("ident", [P, P])
        w1_raw = s.sb("w1_raw", [P, DK, F])
        w2_raw = s.sb("w2_raw", [P, FK, D])
        w1h = s.sb("w1h", [P, DK, F], F32R)
        w1l = s.sb("w1l", [P, DK, F], F32R)
        w2h = s.sb("w2h", [P, FK, D], F32R)
        w2l = s.sb("w2l", [P, FK, D], F32R)
        XE = s.sb("XE", [P, 2, WB, D])
        xTh = s.sb("xTh", [P, 2, DK, WB * P], F32R)
        xTl = s.sb("xTl", [P, 2, DK, WB * P], F32R)
        hf = s.sb("hf", [P, 2, WB * P])
        hh = s.sb("hh", [P, 2, FK, WB * P], F32R)
        hl = s.sb("hl", [P, 2, FK, WB * P], F32R)
        YE = s.sb("YE", [P, 2, D])
        ps_t = s.ps("ps_t", [P, 2, CH])
        ps_h = s.ps("ps_h", [P, HB + 1, CH])
        ps_y = s.ps("ps_y", [P, 2, CH])
        ident_zero, ident_made = s.sem("ident_zero"), s.sem("ident_made")
        w1_in, w2_in, w1h_made, w1l_made, w2h_made, w2l_made = (s.sem(n) for n in ("w1_in", "w2_in", "w1h_made", "w1l_made", "w2h_made", "w2l_made"))
        xe_in = [s.sem("xe_in0"), s.sem("xe_in1")]
        x_tr, xh_made, xl_made, h_mm, hf_made, hh_made, hl_made, y_mm, y_out = (
            s.sem(n) for n in ("x_tr", "xh_made", "xl_made", "h_mm", "hf_made", "hh_made", "hl_made", "y_mm", "y_out"))
        y_st = [s.sem("y_st0"), s.sem("y_st1")]
        gate_sem = s.sem("gate")
        block = s.block()

        def hold(eng, sem, n):
            eng.wait_ge(sem, n)
            eng.sem_inc(gate_sem, 1)

        xe_v = xe_d.rearrange("(e t p) d -> e p t d", p=P, t=NT)
        ye_v = ye_d.rearrange("(e t p) d -> e p t d", p=P, t=NT)
        w1_v = w1.rearrange("e (k p) f -> e p k f", p=P)
        w2_v = w2.rearrange("e (k p) d -> e p k d", p=P)

        @block.sync
        def _(sp):
            def load_block(e, b):
                sp.dma_start(XE[:, b % 2, 0:TILES[b], :],
                             xe_v[bass.ds(e, 1), :, FIRST[b]:FIRST[b] + TILES[b], :].rearrange("a p t d -> p (a t) d")).then_inc(xe_in[b % 2], 16)

            def load_w1(e):
                sp.dma_start(w1_raw[:], w1_v[bass.ds(e, 1)].rearrange("a p k f -> p (a k) f")).then_inc(w1_in, 16)

            def load_w2(e):
                sp.dma_start(w2_raw[:], w2_v[bass.ds(e, 1)].rearrange("a p k f -> p (a k) f")).then_inc(w2_in, 16)

            def body(e, last=False):
                for b in range(NB):
                    if b < NB - 2 or not last:
                        hold(sp, x_tr, DK * (NB * e + b + 1))
                        load_block(e + (b + 2) // NB, (b + 2) % NB)
                    if not last and b == 0:
                        hold(sp, w1l_made, DK * (e + 1))
                        load_w1(e + 1)
                    if not last and b == 1:
                        hold(sp, w2l_made, FK * (e + 1))
                        load_w2(e + 1)

            load_block(0, 0)
            load_w1(0)
            load_block(0, 1)
            load_w2(0)
            with sp.Fori(0, E - 1) as e:
                body(e)
            body(E - 1, last=True)

        @block.gpsimd
        def _(pool):
            make_identity(nc, pool, ident, ident_zero, ident_made)

            def store(e, b, t):
                n = FIRST[b] + t
                hold(pool, y_out, NT * e + n + 1)
                pool.dma_start(ye_v[bass.ds(e, 1), :, n:n + 1, :].rearrange("a p t d -> p (a t d)"), YE[:, n % 2, :]).then_inc(y_st[n % 2], 16)

            with pool.Fori(0, E) as e:
                for b in range(NB):
                    for t in range(TILES[b]):
                        store(e, b, t)
            for i in range(2):
                pool.wait_ge(y_st[i], 16 * E * NT // 2)

        @block.scalar
        def _(act):
            def split_w1(e):
                act.wait_ge(w1_in, 16 * e + 16)
                if not (isinstance(e, int) and e == 0):
                    act.wait_ge(h_mm, FK * NB * e)
                for k in range(DK):
                    nc.scalar.activation(w1h[:, k, :], w1_raw[:, k, :], ACT.Copy).then_inc(w1h_made, 1)

            def split_w2(e):
                act.wait_ge(w2_in, 16 * e + 16)
                if not (isinstance(e, int) and e == 0):
                    act.wait_ge(y_mm, NT * e)
                for k in range(FK):
                    nc.scalar.activation(w2h[:, k, :], w2_raw[:, k, :], ACT.Copy).then_inc(w2h_made, 1)

            def rows_high(e, b, first=False):
                n = TILES[b] * P
                m = NB * e + b
                for k in range(DK):
                    act.wait_ge(x_tr, DK * m + k + 1)
                    if k == 0 and not first:
                        act.wait_ge(h_mm, FK * (m - 1))
                    nc.scalar.activation(xTh[:, b % 2, k, 0:n], ps_t[:, k % 2, 0:n], ACT.Copy).then_inc(xh_made, 1)

            def hidden(e, b, first=False):
                n = TILES[b] * P
                m = NB * e + b
                for f in range(FK):
                    act.wait_ge(h_mm, FK * m + f + 1)
                    if not first or f >= 2:
                        act.wait_ge(hl_made, FK * m + f - 1)
                    nc.scalar.activation(hf[:, f % 2, 0:n], ps_h[:, f % (HB + 1), 0:n], ACT.Gelu).then_inc(hf_made, 1)
                    act.wait_ge(hf_made, FK * m + f + 1)
                    if f == 0 and not (first or (isinstance(e, int) and m < 2)):
                        act.wait_ge(y_mm, before_block(e, b))
                    nc.scalar.activation(hh[:, b % 2, f, 0:n], hf[:, f % 2, 0:n], ACT.Copy).then_inc(hh_made, 1)

            def before_block(e, b):
                return NT * e + FIRST[b - 1] if b >= 1 else NT * e - TILES[NB - 1]

            def body(e, first=False, last=False):
                for b in range(NB):
                    hidden(e, b, first and b == 0)
                    if b == NB - 1 and not last:
                        split_w1(e + 1)
                    if b < NB - 1:
                        rows_high(e, b + 1, first and b == 0)
                    elif not last:
                        rows_high(e + 1, 0)
                    if b == 0 and not first:
                        split_w2(e)

            split_w1(0)
            rows_high(0, 0, first=True)
            split_w2(0)
            body(0, first=True)
            with act.Fori(1, E - 1) as e:
                body(e)
            body(E - 1, last=True)

        @block.vector
        def _(dve):
            def split_w1(e):
                for k in range(DK):
                    dve.wait_ge(w1h_made, DK * e + k + 1)
                    nc.vector.tensor_tensor(w1l[:, k, :], w1_raw[:, k, :], f32(w1h[:, k, :]), ALU.subtract).then_inc(w1l_made, 1)

            def split_w2(e):
                for k in range(FK):
                    dve.wait_ge(w2h_made, FK * e + k + 1)
                    nc.vector.tensor_tensor(w2l[:, k, :], w2_raw[:, k, :], f32(w2h[:, k, :]), ALU.subtract).then_inc(w2l_made, 1)

            def rows_low(e, b):
                n = TILES[b] * P
                m = NB * e + b
                for k in range(DK):
                    dve.wait_ge(xh_made, DK * m + k + 1)
                    nc.vector.tensor_tensor(xTl[:, b % 2, k, 0:n], ps_t[:, k % 2, 0:n], f32(xTh[:, b % 2, k, 0:n]), ALU.subtract).then_inc(xl_made, 1)

            def hidden_low(e, b):
                n = TILES[b] * P
                m = NB * e + b
                for f in range(FK):
                    dve.wait_ge(hh_made, FK * m + f + 1)
                    nc.vector.tensor_tensor(hl[:, b % 2, f, 0:n], hf[:, f % 2, 0:n], f32(hh[:, b % 2, f, 0:n]), ALU.subtract).then_inc(hl_made, 1)

            def rows_out(e, b, first=False):
                for t in range(TILES[b]):
                    n = FIRST[b] + t
                    dve.wait_ge(y_mm, NT * e + n + 1)
                    if not first or n >= 2:
                        dve.wait_ge(y_st[n % 2], 16 * (NT // 2 * e + n // 2))
                    nc.vector.tensor_copy(YE[:, n % 2, :], ps_y[:, n % 2, :]).then_inc(y_out, 1)

            def body(e, first=False, last=False):
                for b in range(NB):
                    hidden_low(e, b)
                    if b == NB - 1 and not last:
                        split_w1(e + 1)
                    if b == 0 and not first:
                        rows_out_lag = (e - 1, NB - 1)
                    elif b > 0:
                        rows_out_lag = (e, b - 1)
                    else:
                        rows_out_lag = None
                    if b < NB - 1:
                        rows_low(e, b + 1)
                    elif not last:
                        rows_low(e + 1, 0)
                    if rows_out_lag:
                        rows_out(*rows_out_lag, first and rows_out_lag[1] == 0)
                    if b == 0 and not first:
                        split_w2(e)

            split_w1(0)
            rows_low(0, 0)
            split_w2(0)
            body(0, first=True)
            with dve.Fori(1, E - 1) as e:
                body(e)
            body(E - 1, last=True)
            rows_out(E - 1, NB - 1)

        @block.tensor
        def _(pe):
            def transposes(e, b, first=False):
                m = NB * e + b
                pe.wait_ge(xe_in[b % 2], 16 * (NB // 2 * e + b // 2) + 16)
                for k in range(DK):
                    if not first or k >= 2:
                        pe.wait_ge(xl_made, DK * m + k - 1)
                    for t in range(TILES[b]):
                        last = nc.tensor.transpose(ps_t[:, k % 2, t * P:(t + 1) * P], XE[:, b % 2, t, k * P:(k + 1) * P], ident[:])
                    last.then_inc(x_tr, 1)

            def up(e, b, first=False):
                n = TILES[b] * P
                m = NB * e + b
                pe.wait_ge(xl_made, DK * m + DK)
                if b == 0:
                    pe.wait_ge(w1l_made, DK * e + DK)
                for f in range(FK):
                    if not first or f > HB:
                        pe.wait_ge(hf_made, FK * m + f - HB)
                    for k in range(DK):
                        cols = slice(f * P, (f + 1) * P)
                        last = mm3(nc, ps_h[:, f % (HB + 1), 0:n], w1h[:, k, cols], w1l[:, k, cols],
                                   xTh[:, b % 2, k, 0:n], xTl[:, b % 2, k, 0:n], k == 0, k == DK - 1)
                    last.then_inc(h_mm, 1)

            def down(e, b, first=False):
                m = NB * e + b
                pe.wait_ge(hl_made, FK * m + FK)
                if b == 0:
                    pe.wait_ge(w2l_made, FK * e + FK)
                for t in range(TILES[b]):
                    n = FIRST[b] + t
                    if not first or n >= 2:
                        pe.wait_ge(y_out, NT * e + n - 1)
                    toks = slice(t * P, (t + 1) * P)
                    for f in range(FK):
                        last = mm3(nc, ps_y[:, n % 2, :], hh[:, b % 2, f, toks], hl[:, b % 2, f, toks],
                                   w2h[:, f, :], w2l[:, f, :], f == 0, f == FK - 1)
                    last.then_inc(y_mm, 1)

            def body(e, first=False, last=False):
                for b in range(NB):
                    up(e, b, first and b == 0)
                    if b < NB - 1:
                        transposes(e, b + 1)
                    elif not last:
                        transposes(e + 1, 0)
                    if b > 0:
                        down(e, b - 1, first and b == 1)
                    elif not first:
                        down(e - 1, NB - 1)

            pe.wait_ge(ident_made, 1)
            transposes(0, 0, first=True)
            body(0, first=True)
            with pe.Fori(1, E - 1) as e:
                body(e)
            body(E - 1, last=True)
            down(E - 1, NB - 1)


def phase_combine(nc, ye_d, src_d, x1_d, slot_d, wt_d, norm2, out):
    with Scope(nc, "p4") as s:
        norm_row = s.sb("norm_row", [P, D])
        slots = s.sb("slots", [P, NC, 2, TT], I32)
        wts = s.sb("wts", [P, NC, 2, TT])
        half = s.sb("half", [P, TT])
        SR = s.sb("SR", [P, 2, TT, D])
        X1 = s.sb("X1", [P, 2, TT, D])
        YG = s.sb("YG", [P, 2, TT, 2, D])
        OUT = s.sb("OUT", [P, 2, TT, D])
        sq = s.sb("sq", [P, D])
        ss = s.sb("ss", [P, 2, TT])
        sv = s.sb("sv", [P, 2, TT])
        rstd = s.sb("rstd", [P, 2, TT])
        const_in, half_made = s.sem("const_in"), s.sem("half_made")
        sr_in = [s.sem("sr_in0"), s.sem("sr_in1")]
        x1_in = [s.sem("x1_in0"), s.sem("x1_in1")]
        yg_in = [s.sem("yg_in0"), s.sem("yg_in1")]
        out_st = [s.sem("out_st0"), s.sem("out_st1")]
        add0, add1, ss_made, sv_made, rs_made, n_made, o_made, o_first = (s.sem(n) for n in ("add0", "add1", "ss_made", "sv_made", "rs_made", "n_made", "o_made", "o_first"))
        block = s.block()
        NCH = NC

        @block.sync
        def _(sp):
            sp.dma_start(slots[:].rearrange("p c k t -> p c (k t)"), slot_d.rearrange("c p n -> p c n")).then_inc(const_in, 16)
            sp.dma_start(wts[:].rearrange("p c k t -> p c (k t)"), wt_d.rearrange("c p n -> p c n")).then_inc(const_in, 16)
            sp.dma_start(norm_row[:], over_rows(norm2)).then_inc(const_in, 16)
            for c in range(NCH):
                i = c % 2
                if c >= 2:
                    sp.wait_ge(o_made, TT * (c - 1))
                sp.dma_start(SR[:, i, :, :], src_d[c].rearrange("(t p) d -> p t d", p=P)).then_inc(sr_in[i], 16)
                sp.dma_start(X1[:, i, :, :], x1_d[c].rearrange("(t p) d -> p t d", p=P)).then_inc(x1_in[i], 16)

        @block.gpsimd
        def _(pool):
            nc.gpsimd.memset(half[:], -0.5).then_inc(half_made, 1)
            pool.wait_ge(half_made, 1)
            pool.wait_ge(const_in, 48)

            def fetch(c):
                i = c % 2
                if c >= 2:
                    pool.wait_ge(add1, TT * (c - 1))
                for t in range(TT):
                    for k in range(2):
                        nc.gpsimd.indirect_dma_start(out=YG[:, i, t, k, :], out_offset=None, in_=ye_d,
                                                     in_offset=bass.IndirectOffsetOnAxis(ap=slots[:, c, k, t:t + 1].bitcast(U32), axis=0)).then_inc(yg_in[i], 16)

            fetch(0)
            for c in range(NCH):
                i = c % 2
                if c + 1 < NCH:
                    fetch(c + 1)
                pool.wait_ge(ss_made, TT * c + TT)
                nc.gpsimd.tensor_scalar(sv[:, i, :], ss[:, i, :], 1.0 / D, RMS_EPS, ALU.mult, ALU.add).then_inc(sv_made, 1)
                pool.wait_ge(sv_made, c + 1)
                nc.gpsimd.tensor_tensor(rstd[:, i, :], sv[:, i, :], half[:], ALU.pow).then_inc(rs_made, 1)

        @block.scalar
        def _(act):
            def store(c):
                i = c % 2
                act.wait_ge(o_made, TT * c + TT)
                act.dma_start(out[c].rearrange("(t p) d -> p t d", p=P), OUT[:, i, :, :]).then_inc(out_st[i], 16)

            for c in range(NCH):
                i = c % 2
                for t in range(TT):
                    act.wait_ge(add1, TT * c + t + 1)
                    if c + t > 0:
                        act.wait_ge(ss_made, TT * c + t)
                    nc.scalar.activation(sq[:], SR[:, i, t, :], ACT.Square, accum_out=ss[:, i, t:t + 1]).then_inc(ss_made, 1)
                if c > 0:
                    store(c - 1)
            store(NCH - 1)
            for i in range(2):
                act.wait_ge(out_st[i], 16 * NCH // 2)

        @block.vector
        def _(dve):
            dve.wait_ge(const_in, 48)

            def add(c):
                i = c % 2
                dve.wait_ge(sr_in[i], 16 * (c // 2 + 1))
                dve.wait_ge(yg_in[i], 16 * 2 * TT * (c // 2 + 1))
                for t in range(TT):
                    nc.vector.scalar_tensor_tensor(SR[:, i, t, :], YG[:, i, t, 0, :], wts[:, c, 0, t:t + 1], SR[:, i, t, :],
                                                   ALU.mult, ALU.add).then_inc(add0, 1)
                for t in range(TT):
                    dve.wait_ge(add0, TT * c + t + 1)
                    nc.vector.scalar_tensor_tensor(SR[:, i, t, :], YG[:, i, t, 1, :], wts[:, c, 1, t:t + 1], SR[:, i, t, :],
                                                   ALU.mult, ALU.add).then_inc(add1, 1)

            def finish(c):
                i = c % 2
                dve.wait_ge(rs_made, c + 1)
                dve.wait_ge(x1_in[i], 16 * (c // 2 + 1))
                if c >= 2:
                    dve.wait_ge(out_st[i], 16 * (c // 2))
                for t in range(TT):
                    nc.vector.scalar_tensor_tensor(OUT[:, i, t, :], SR[:, i, t, :], rstd[:, i, t:t + 1], norm_row[:],
                                                   ALU.mult, ALU.mult).then_inc(n_made, 1)
                for t in range(TT):
                    dve.wait_ge(n_made, TT * c + t + 1)
                    nc.vector.tensor_tensor(OUT[:, i, t, :], OUT[:, i, t, :], X1[:, i, t, :], ALU.add).then_inc(o_made, 1)

            add(0)
            for c in range(NCH):
                if c + 1 < NCH:
                    add(c + 1)
                finish(c)


def build_layer(nc, x, ctx_1024, mask, gamma, beta, qw, qb, kw, kb, vw, vb, ow, ob, gate_w, w1, w2, norm1, norm2, out):
    def scratch(name, shape, dt=F32):
        return nc.dram_tensor(name, shape, dt, kind="Internal").ap()

    x1_d, y_d, src_d = (scratch(n, (NC, CH, D)) for n in ("x1_d", "y_d", "src_d"))
    qh_d, ql_d = scratch("qh_d", (NC, D, CH)), scratch("ql_d", (NC, D, CH))
    kh_d, kl_d, v_d = scratch("kh_d", (NC, P, CH)), scratch("kl_d", (NC, P, CH)), scratch("v_d", (NC, CH, P))
    xe_d, ye_d = scratch("xe_d", (E * CAP, D)), scratch("ye_d", (E * CAP, D))
    slot_d, wt_d = scratch("slot_d", (NC, P, 2 * TT), I32), scratch("wt_d", (NC, P, 2 * TT))

    def chunks(ap):
        return ap.rearrange("b (n q) d -> (b n) q d", q=CH)

    phase_project(nc, chunks(x), ctx_1024, chunks(mask), gamma, beta, qw, qb, kw, kb, vw, vb,
                  x1_d, y_d, qh_d, ql_d, kh_d, kl_d, v_d)
    phase_attend(nc, y_d, qh_d, ql_d, kh_d, kl_d, v_d, ow, ob, norm1, gate_w, src_d, xe_d, slot_d, wt_d)
    phase_experts(nc, xe_d, w1, w2, ye_d)
    phase_combine(nc, ye_d, src_d, x1_d, slot_d, wt_d, norm2, chunks(out))


INPUTS = ["x", "ctx_1024", "mask_BxSxS2_ik1", "L0_xattn_gamma", "L0_xattn_beta", "L0_ffn_qw", "L0_ffn_qb", "L0_ffn_kw",
          "L0_ffn_kb", "L0_ffn_vw", "L0_ffn_vb", "L0_ffn_ow", "L0_ffn_ob", "L0_ffn_gate_w", "L0_ffn_w1", "L0_ffn_w2",
          "L0_ffn_norm1_w", "L0_ffn_norm2_w"]


def kernel(**inputs):
    import numpy as np
    import concourse.bacc as bacc
    from concourse.bass_utils import run_bass_kernel_spmd

    nc = bacc.Bacc("TRN2", target_bir_lowering=False, num_devices=1)
    arrays, args = {}, []
    for name in INPUTS:
        a = np.ascontiguousarray(inputs[name])
        arrays[f"in_{name}"] = a
        args.append(nc.dram_tensor(f"in_{name}", a.shape, mybir.dt.from_np(a.dtype), kind="ExternalInput").ap())
    args.append(nc.dram_tensor("out_dram", (B, S, D), F32, kind="ExternalOutput").ap())
    build_layer(nc, *args)
    return run_bass_kernel_spmd(nc, [arrays], core_ids=[0]).results[0]["out_dram"]
```

```python
from contextlib import ExitStack

import concourse.bass as bass
from concourse import mybir

F32 = mybir.dt.float32
F32R = mybir.dt.float32r
I32 = mybir.dt.int32
U32 = mybir.dt.uint32
ALU = mybir.AluOpType
ACT = mybir.ActivationFunctionType
AXX = mybir.AxisListType.X

P = 128
B, S, D = 2, 2048, 512
N = B * S
CT = 77
DK = D // P
H, KV, HD = 16, 4, 32
G = H // KV
CH = 512
TT = CH // P
NC = N // CH
CB = S // CH
KT = S // P
E, F = 8, 1024
CAP = int(1.25 * N * 2 / E)
KEEP = 1
NEG = -9e15
LN_EPS = 1e-5
RMS_EPS = 1e-6


class Scope:

    taken = set()

    def __init__(self, nc, tag):
        self.nc, self.tag, self.stack = nc, tag, ExitStack()

    def __enter__(self):
        self.stack.__enter__()
        return self

    def __exit__(self, *a):
        return self.stack.__exit__(*a)

    def sb(self, name, shape, dt=F32):
        return self.stack.enter_context(self.nc.sbuf_tensor(f"{self.tag}_{name}", shape, dt))

    def ps(self, name, shape, dt=F32):
        return self.stack.enter_context(self.nc.psum_tensor(f"{self.tag}_{name}", shape, dt))

    def sem(self, name):
        handle = self.stack.enter_context(self.nc.semaphore(f"{self.tag}_{name}"))
        assert handle.num not in self.taken, "too many semaphores"
        self.taken.add(handle.num)
        return handle

    def block(self):
        return self.stack.enter_context(self.nc.Block())


def f32(ap):
    return ap.bitcast(F32)


def mm3(nc, out, ah, al, bh, bl, start, stop):
    nc.tensor.matmul(out, ah, bh, start=start, stop=False)
    nc.tensor.matmul(out, ah, bl, start=False, stop=False)
    return nc.tensor.matmul(out, al, bh, start=False, stop=stop)


def make_identity(nc, pool, ident, ident_made):
    nc.gpsimd.memset(ident[:], 0.0).then_inc(ident_made, 1)
    pool.wait_ge(ident_made, 1)
    nc.gpsimd.affine_select(out=ident[:], in_=ident[:], compare_op=ALU.not_equal, fill=1.0, base=0,
                            pattern=[[-1, P]], channel_multiplier=1).then_inc(ident_made, 1)


def over_rows(ap, rows=P):
    return ap.rearrange("(a n) -> a n", a=1).broadcast_to((rows, ap.shape[0]))


def phase_project(nc, x, ctx, mask, gamma, beta, qw, qb, kw, kb, vw, vb, ob, x1_d, y_d, qh_d, ql_d, kh_d, kl_d, v_d):
    NM = KV + 2
    KEYS, VALUES = KV, KV + 1
    STEPS = (0, 1, 2, 3, VALUES, KEYS)
    with Scope(nc, "p1") as s:
        ident = s.sb("ident", [P, P])
        w_raw = s.sb("w_raw", [P, DK, D + 2 * P])
        w_hi = s.sb("w_hi", [P, DK, D + 2 * P], F32R)
        w_lo = s.sb("w_lo", [P, DK, D + 2 * P], F32R)
        b_col = s.sb("b_col", [P, NM])
        gamma_row = s.sb("gamma_row", [P, D])
        beta_row = s.sb("beta_row", [P, D])
        ob_row = s.sb("ob_row", [P, D])
        ctx_n = s.sb("ctx_n", [CT, B, D])
        ctx_t = s.sb("ctx_t", [P, B, DK, CT])
        X = s.sb("X", [P, TT, D])
        MK = s.sb("MK", [P, TT, CT], I32)
        pen = s.sb("pen", [P, TT, CT])
        qn = s.sb("qn", [P, TT, D])
        qT = s.sb("qT", [P, DK, CH])
        lg = s.sb("lg", [P, TT, CT])
        pr = s.sb("pr", [P, TT, CT])
        prT = s.sb("prT", [CT, CH])
        att = s.sb("att", [P, TT, D])
        xb = s.sb("xb", [P, TT, D])
        x1 = s.sb("x1", [P, TT, D])
        y = s.sb("y", [P, TT, D])
        yb = s.sb("yb", [P, TT, D])
        yTh = s.sb("yTh", [P, DK, CH], F32R)
        yTl = s.sb("yTl", [P, DK, CH], F32R)
        hi = s.sb("hi", [P, KV + 1, CH], F32R)
        lo = s.sb("lo", [P, KV + 1, CH], F32R)
        vT = s.sb("vT", [P, CH])
        val = s.sb("val", [P, TT, P])
        stats = s.sb("stats", [P, 3, TT, 6])
        mv = s.sb("mv", [P, 3, TT, 2])
        var = s.sb("var", [P, 3, TT])
        rstd = s.sb("rstd", [P, 3, TT])
        half = s.sb("half", [P, TT])
        mx = s.sb("mx", [P, TT])
        nmx = s.sb("nmx", [P, TT])
        psum_e = s.sb("psum_e", [P, TT])
        rinv = s.sb("rinv", [P, TT])
        vr = s.sb("vr", [P, TT])
        s2 = s.sb("s2", [P, TT])
        ps_t = s.ps("ps_t", [P, 2, CH])
        ps_lg = s.ps("ps_lg", [P, TT, P])
        ps_pt = s.ps("ps_pt", [P, CH])
        ps_o = s.ps("ps_o", [P, 2, CH])
        ps_pj = s.ps("ps_pj", [P, 2, CH])

        w_in, ctx_in, vec_in = s.sem("w_in"), s.sem("ctx_in"), s.sem("vec_in")
        ident_made, half_made = s.sem("ident_made"), s.sem("half_made")
        wh_made, wl_made = s.sem("wh_made"), s.sem("wl_made")
        ctx_tr, ctx_t_made = s.sem("ctx_tr"), s.sem("ctx_t_made")
        x_in, mask_in = s.sem("x_in"), s.sem("mask_in")
        stat = [s.sem(f"stat{i}") for i in range(3)]
        aggr = [s.sem(f"aggr{i}") for i in range(3)]
        vared = [s.sem(f"vared{i}") for i in range(3)]
        rs = [s.sem(f"rs{i}") for i in range(3)]
        qn_made, q_tr, qT_made, lg_mm, pen_made = (s.sem(n) for n in ("qn_made", "q_tr", "qT_made", "lg_mm", "pen_made"))
        lg_made, mx_made, nmx_made, pr_made, p_tr = (s.sem(n) for n in ("lg_made", "mx_made", "nmx_made", "pr_made", "p_tr"))
        prT_made, o_mm, att_made, rinv_made = (s.sem(n) for n in ("prT_made", "o_mm", "att_made", "rinv_made"))
        vr1, s2_made, att_n = (s.sem(n) for n in ("vr1", "s2_made", "att_n"))
        xb_made, x1_made, y_made, y_tr = (s.sem(n) for n in ("xb_made", "x1_made", "y_made", "y_tr"))
        yh_made, yl_made, pj_mm, hi_made, pj_out = (s.sem(n) for n in ("yh_made", "yl_made", "pj_mm", "hi_made", "pj_out"))
        v_tr, val_made, yb_made = s.sem("v_tr"), s.sem("val_made"), s.sem("yb_made")
        x1_st, y_st, qa_st, qb_st, k_st, v_st = (s.sem(n) for n in ("x1_st", "y_st", "qa_st", "qb_st", "k_st", "v_st"))
        gate_sem = s.sem("gate")
        block = s.block()

        def gate(eng):
            eng.sem_inc(gate_sem, 1)

        @block.sync
        def _(sp):
            def load(c):
                sp.dma_start(X[:], x[bass.ds(c, 1)].rearrange("a (t p) d -> p (a t) d", p=P)).then_inc(x_in, 16)
                sp.dma_start(MK[:], mask[bass.ds(c, 1)].rearrange("a (t p) n -> p (a t) n", p=P)).then_inc(mask_in, 16)

            def hold(sem, n):
                sp.wait_ge(sem, n)
                gate(sp)

            def store_x1(c):
                hold(x1_made, TT * c + TT)
                sp.dma_start(x1_d[bass.ds(c, 1)].rearrange("a (t p) d -> p (a t) d", p=P), x1[:]).then_inc(x1_st, 16)

            def store_y(c):
                hold(yb_made, c + 1)
                sp.dma_start(y_d[bass.ds(c, 1)].rearrange("a (t p) d -> p (a t) d", p=P), yb[:]).then_inc(y_st, 16)

            def store_queries(c, part, sem):
                for d, src in ((qh_d, hi), (ql_d, lo)):
                    sp.dma_start(d[bass.ds(c, 1), 2 * P * part:2 * P * (part + 1), :].rearrange("a (g p) q -> p (a g) q", p=P),
                                 f32(src[:, 2 * part:2 * part + 2, :])).then_inc(sem, 16)

            def store_projections(c, part):
                if part == 0:
                    hold(pj_out, NM * c + 2)
                    store_queries(c, 0, qa_st)
                else:
                    hold(pj_out, NM * c + 4)
                    store_queries(c, 1, qb_st)
                    hold(pj_out, NM * c + NM)
                    sp.dma_start(kh_d[bass.ds(c, 1)].rearrange("a p q -> p (a q)"), f32(hi[:, KV, :])).then_inc(k_st, 16)
                    sp.dma_start(kl_d[bass.ds(c, 1)].rearrange("a p q -> p (a q)"), f32(lo[:, KV, :])).then_inc(k_st, 16)
                    hold(val_made, c + 1)
                    sp.dma_start(v_d[bass.ds(c, 1)].rearrange("a (t p) n -> p (a t) n", p=P), val[:]).then_inc(v_st, 16)

            def reload(c):
                hold(xb_made, c)
                hold(qn_made, TT * c)
                hold(pen_made, c)
                load(c)

            load(0)
            for cols, w in ((slice(0, D), qw), (slice(D, D + P), kw), (slice(D + P, D + 2 * P), vw)):
                sp.dma_start(w_raw[:, :, cols], w.rearrange("(k p) n -> p k n", p=P)).then_inc(w_in, 16)
            reload(1)
            store_x1(0)
            store_y(0)
            with sp.Fori(1, NC - 1) as i:
                before_ = sp.snap(i - 1)
                reload(sp.snap(i + 1))
                store_projections(before_, 0)
                store_x1(i)
                store_projections(before_, 1)
                store_y(i)
            store_projections(NC - 2, 0)
            store_x1(NC - 1)
            store_projections(NC - 2, 1)
            store_y(NC - 1)
            store_projections(NC - 1, 0)
            store_projections(NC - 1, 1)
            for sem, n in ((x1_st, NC), (y_st, NC), (qa_st, 2 * NC), (qb_st, 2 * NC), (k_st, 2 * NC), (v_st, NC), (x_in, NC), (mask_in, NC)):
                sp.wait_ge(sem, 16 * n)

        @block.gpsimd
        def _(pool):
            make_identity(nc, pool, ident, ident_made)
            nc.gpsimd.memset(half[:], -0.5).then_inc(half_made, 1)
            pool.wait_ge(half_made, 1)

            def power(j, c, src):
                gate(pool)
                nc.gpsimd.tensor_scalar(var[:, j, :], src, LN_EPS, None, ALU.add).then_inc(vared[j], 1)
                pool.wait_ge(vared[j], c + 1)
                nc.gpsimd.tensor_tensor(rstd[:, j, :], var[:, j, :], half[:], ALU.pow).then_inc(rs[j], 1)

            def residual(c):
                pool.wait_ge(x_in, 16 * c + 16)
                if not (isinstance(c, int) and c == 0):
                    pool.wait_ge(x1_made, TT * c)
                for t in range(TT):
                    last = nc.gpsimd.tensor_tensor(xb[:, t, :], X[:, t, :], beta_row[:], ALU.add)
                last.then_inc(xb_made, 1)

            def chunk(c, has_next=True):
                pool.wait_ge(vr1, 2 * c + 2)
                power(1, c, vr[:])
                if has_next:
                    pool.wait_ge(aggr[0], TT * c + 2 * TT)
                    power(0, c + 1, mv[:, 0, :, 1])
                pool.wait_ge(aggr[2], TT * c + TT)
                power(2, c, mv[:, 2, :, 1])
                if has_next:
                    residual(c + 1)
                if not (isinstance(c, int) and c == 0):
                    pool.wait_ge(y_st, 16 * c)
                for t in range(TT):
                    pool.wait_ge(y_made, TT * c + t + 1)
                    last = nc.gpsimd.tensor_tensor(yb[:, t, :], y[:, t, :], ob_row[:], ALU.add)
                last.then_inc(yb_made, 1)

            pool.wait_ge(aggr[0], TT)
            power(0, 0, mv[:, 0, :, 1])
            pool.wait_ge(vec_in, 16 * 9)
            residual(0)
            chunk(0)
            with pool.Fori(1, NC - 1) as i:
                chunk(i)
            chunk(NC - 1, has_next=False)

        @block.scalar
        def _(act):
            act.dma_start(ctx_n[:], ctx.rearrange("b r d -> r b d")).then_inc(ctx_in, 16)
            act.dma_start(gamma_row[:], over_rows(gamma)).then_inc(vec_in, 16)
            act.dma_start(beta_row[:], over_rows(beta)).then_inc(vec_in, 16)
            act.dma_start(ob_row[:], over_rows(ob)).then_inc(vec_in, 16)
            qb_v = qb.rearrange("(g p a) -> g p a", p=P, a=1)
            for g in range(KV):
                act.dma_start(b_col[:, g:g + 1], qb_v[g]).then_inc(vec_in, 16)
            act.dma_start(b_col[:, KEYS:KEYS + 1], kb.rearrange("(p a) -> p a", a=1)).then_inc(vec_in, 16)
            act.dma_start(b_col[:, VALUES:VALUES + 1], vb.rearrange("(p a) -> p a", a=1)).then_inc(vec_in, 16)
            act.wait_ge(ctx_tr, 1)
            nc.scalar.activation(ctx_t[:, 0, :, :], ps_t[:, 0, 0:DK * P].rearrange("p (k n) -> p k n", k=DK)[:, :, 0:CT], ACT.Copy).then_inc(ctx_t_made, 1)
            act.wait_ge(ctx_tr, 2)
            nc.scalar.activation(ctx_t[:, 1, :, :], ps_t[:, 1, 0:DK * P].rearrange("p (k n) -> p k n", k=DK)[:, :, 0:CT], ACT.Copy).then_inc(ctx_t_made, 1)

            def queries_out(c, first=False):
                for k in range(DK):
                    act.wait_ge(q_tr, DK * c + k + 1)
                    if not first:
                        act.wait_ge(lg_mm, c)
                    nc.scalar.activation(qT[:, k, :], ps_t[:, k % 2, :], ACT.Copy).then_inc(qT_made, 1)

            def exps(c, first=False):
                act.wait_ge(nmx_made, c + 1)
                if not first:
                    act.wait_ge(p_tr, c)
                    act.wait_ge(rinv_made, c)
                for t in range(TT):
                    nc.scalar.activation(pr[:, t, :], lg[:, t, :], ACT.Exp, bias=nmx[:, t:t + 1],
                                         accum_out=psum_e[:, t:t + 1]).then_inc(pr_made, 1)

            def probabilities_out(c, first=False):
                act.wait_ge(p_tr, c + 1)
                if not first:
                    act.wait_ge(o_mm, TT * c)
                nc.scalar.activation(prT[:], ps_pt[0:CT, :], ACT.Copy).then_inc(prT_made, 1)

            def attention_out(c, first=False):
                if not first:
                    act.wait_ge(x1_made, TT * c)
                for t in range(TT):
                    act.wait_ge(o_mm, TT * c + t + 1)
                    nc.scalar.activation(att[:, t, :], ps_o[:, t % 2, :], ACT.Copy).then_inc(att_made, 1)

            def y_high(c, ks, first=False):
                if not first:
                    act.wait_ge(pj_mm, NM * c)
                for k in ks:
                    act.wait_ge(y_tr, DK * c + k + 1)
                    nc.scalar.activation(yTh[:, k, :], ps_t[:, k % 2, :], ACT.Copy).then_inc(yh_made, 1)

            def high(c, n, first=False):
                m = STEPS[n]
                if m == VALUES:
                    return
                if not first and m in (0, 2, KEYS):
                    act.wait_ge({0: qa_st, 2: qb_st, KEYS: k_st}[m], 32 * c)
                act.wait_ge(pj_mm, NM * c + n + 1)
                nc.scalar.activation(hi[:, m, :], ps_pj[:, n % 2, :], ACT.Identity, bias=b_col[:, m:m + 1]).then_inc(hi_made, 1)

            def values_out(c, first=False):
                act.wait_ge(v_tr, c + 1)
                if not first:
                    act.wait_ge(v_st, 16 * c)
                nc.scalar.activation(val[:], ps_pt[:].rearrange("p (t n) -> p t n", t=TT), ACT.Copy).then_inc(val_made, 1)

            def chunk(c, first_project=False):
                queries_out(c)
                y_high(c - 1, (0, 1), first_project)
                exps(c)
                y_high(c - 1, (2, 3), first_project)
                probabilities_out(c)
                high(c - 1, 0, first_project)
                attention_out(c)
                for n in range(1, NM):
                    high(c - 1, n, first_project)
                values_out(c - 1, first_project)

            queries_out(0, first=True)
            act.wait_ge(w_in, 48)
            for k in range(DK):
                nc.scalar.activation(w_hi[:, k, :], w_raw[:, k, :], ACT.Copy).then_inc(wh_made, 1)
            exps(0, first=True)
            probabilities_out(0, first=True)
            attention_out(0, first=True)
            act.wait_ge(vec_in, 16 * 9)
            chunk(1, first_project=True)
            with act.Fori(2, NC) as i:
                chunk(i)
            y_high(NC - 1, range(DK))
            for n in range(NM):
                high(NC - 1, n)
            values_out(NC - 1)

        @block.vector
        def _(dve):
            def moments(j, c, src, ready=None):
                for t in range(TT):
                    if ready is not None:
                        dve.wait_ge(ready, TT * c + t + 1)
                    nc.vector.bn_stats(stats[:, j, t, :], src[:, t, :]).then_inc(stat[j], 1)
                dve.wait_ge(stat[j], TT * c + TT)
                gate(dve)
                for t in range(TT):
                    nc.vector.bn_aggr(mv[:, j, t, :], stats[:, j, t, :]).then_inc(aggr[j], 1)

            def head_statistics(c, first=False):
                dve.wait_ge(x_in, 16 * c + 16)
                if not first:
                    dve.wait_ge(qn_made, TT * c)
                    dve.wait_ge(rs[0], c)
                moments(0, c, X)
                dve.wait_ge(mask_in, 16 * c + 16)
                if not first:
                    dve.wait_ge(lg_made, c)
                nc.vector.tensor_scalar(pen[:], MK[:], 0, NEG, ALU.is_equal, ALU.mult).then_inc(pen_made, 1)

            def head_normalise(c, first=False):
                dve.wait_ge(aggr[0], TT * c + TT)
                dve.wait_ge(rs[0], c + 1)
                if not first:
                    dve.wait_ge(q_tr, DK * c)
                for t in range(TT):
                    nc.vector.tensor_scalar(qn[:, t, :], X[:, t, :], mv[:, 0, t, 0:1], rstd[:, 0, t:t + 1],
                                            ALU.subtract, ALU.mult).then_inc(qn_made, 1)

            def softmax(c, first=False):
                dve.wait_ge(lg_mm, c + 1)
                dve.wait_ge(pen_made, c + 1)
                if not first:
                    dve.wait_ge(pr_made, TT * c)
                nc.vector.scalar_tensor_tensor(lg[:], ps_lg[:, :, 0:CT], float(D) ** -0.5, pen[:], ALU.mult, ALU.add).then_inc(lg_made, 1)
                dve.wait_ge(lg_made, c + 1)
                nc.vector.reduce_max(mx[:], lg[:], AXX).then_inc(mx_made, 1)
                dve.wait_ge(mx_made, c + 1)
                nc.vector.tensor_scalar(nmx[:], mx[:], -1.0, None, ALU.mult).then_inc(nmx_made, 1)

            def attention_statistics(c):
                dve.wait_ge(pr_made, TT * c + TT)
                nc.vector.reciprocal(rinv[:], psum_e[:]).then_inc(rinv_made, 1)
                moments(1, c, att, att_made)
                dve.wait_ge(aggr[1], TT * c + TT)
                dve.wait_ge(rinv_made, c + 1)
                nc.vector.tensor_tensor(vr[:], mv[:, 1, :, 1], rinv[:], ALU.mult).then_inc(vr1, 1)
                dve.wait_ge(vr1, 2 * c + 1)
                nc.vector.tensor_tensor(vr[:], vr[:], rinv[:], ALU.mult).then_inc(vr1, 1)

            def attention_scaled(c):
                dve.wait_ge(rs[1], c + 1)
                nc.vector.tensor_tensor(s2[:], rstd[:, 1, :], rinv[:], ALU.mult).then_inc(s2_made, 1)
                for t in range(TT):
                    nc.vector.scalar_tensor_tensor(att[:, t, :], att[:, t, :], mv[:, 1, t, 0:1], gamma_row[:],
                                                   ALU.subtract, ALU.mult).then_inc(att_n, 1)

            def attention_added(c, first=False):
                dve.wait_ge(s2_made, c + 1)
                dve.wait_ge(xb_made, c + 1)
                if not first:
                    dve.wait_ge(x1_st, 16 * c)
                    dve.wait_ge(y_made, TT * c)
                for t in range(TT):
                    dve.wait_ge(att_n, TT * c + t + 1)
                    nc.vector.scalar_tensor_tensor(x1[:, t, :], att[:, t, :], s2[:, t:t + 1], xb[:, t, :],
                                                   ALU.mult, ALU.add).then_inc(x1_made, 1)

            def y_normalise(c, first=False):
                dve.wait_ge(aggr[2], TT * c + TT)
                dve.wait_ge(rs[2], c + 1)
                if not first:
                    dve.wait_ge(y_tr, DK * c)
                    dve.wait_ge(yb_made, c)
                for t in range(TT):
                    nc.vector.tensor_scalar(y[:, t, :], x1[:, t, :], mv[:, 2, t, 0:1], rstd[:, 2, t:t + 1],
                                            ALU.subtract, ALU.mult).then_inc(y_made, 1)

            def second_low(c, first=False):
                for k in range(DK):
                    dve.wait_ge(yh_made, DK * c + k + 1)
                    nc.vector.tensor_tensor(yTl[:, k, :], ps_t[:, k % 2, :], f32(yTh[:, k, :]), ALU.subtract).then_inc(yl_made, 1)

            def projected(c, n, first=False):
                m = STEPS[n]
                if m == VALUES:
                    dve.wait_ge(pj_mm, NM * c + n + 1)
                    if not first:
                        dve.wait_ge(v_tr, c)
                    nc.vector.tensor_scalar(vT[:], ps_pj[:, n % 2, :], b_col[:, m:m + 1], None, ALU.add).then_inc(pj_out, 1)
                else:
                    if not first and m in (0, 2, KEYS):
                        dve.wait_ge({0: qa_st, 2: qb_st, KEYS: k_st}[m], 32 * c)
                    dve.wait_ge(hi_made, (NM - 1) * c + min(n, 4) + 1)
                    nc.vector.scalar_tensor_tensor(lo[:, m, :], ps_pj[:, n % 2, :], b_col[:, m:m + 1], f32(hi[:, m, :]),
                                                   ALU.add, ALU.subtract).then_inc(pj_out, 1)

            def chunk(c, has_next=True, first=False, project=True, first_project=False):
                def out(n):
                    if project:
                        projected(c - 1, n, first_project)

                softmax(c, first)
                if project:
                    second_low(c - 1)
                out(0)
                attention_statistics(c)
                out(1)
                if has_next:
                    head_statistics(c + 1)
                out(2)
                attention_scaled(c)
                out(3)
                attention_added(c, first)
                out(4)
                if has_next:
                    head_normalise(c + 1)
                moments(2, c, x1, x1_made)
                out(5)
                y_normalise(c, first)

            head_statistics(0, first=True)
            head_normalise(0, first=True)
            dve.wait_ge(w_in, 48)
            dve.wait_ge(vec_in, 16 * 9)
            chunk(0, first=True, project=False)
            for k in range(DK):
                dve.wait_ge(wh_made, k + 1)
                nc.vector.tensor_tensor(w_lo[:, k, :], w_raw[:, k, :], f32(w_hi[:, k, :]), ALU.subtract).then_inc(wl_made, 1)
            chunk(1, first_project=True)
            with dve.Fori(2, NC - 1) as i:
                chunk(i)
            chunk(NC - 1, has_next=False)
            second_low(NC - 1)
            for n in range(NM):
                projected(NC - 1, n)

        @block.tensor
        def _(pe):
            pe.wait_ge(ident_made, 2)
            pe.wait_ge(ctx_in, 16)
            for b in range(B):
                for k in range(DK):
                    last = nc.tensor.transpose(ps_t[:, b, k * P:k * P + CT], ctx_n[:, b, k * P:(k + 1) * P], ident[0:CT, 0:CT])
                last.then_inc(ctx_tr, 1)
            pe.wait_ge(ctx_t_made, 2)

            def transposes(c, src, ready, done, evacuated):
                pe.wait_ge(ready, TT * c + TT)
                for k in range(DK):
                    if k >= 2:
                        pe.wait_ge(evacuated, DK * c + k - 1)
                    for t in range(TT):
                        last = nc.tensor.transpose(ps_t[:, k % 2, t * P:(t + 1) * P], src[:, t, k * P:(k + 1) * P], ident[:])
                    last.then_inc(done, 1)

            def first_part(c, first=False):
                transposes(c, qn, qn_made, q_tr, qT_made)
                pe.wait_ge(qT_made, DK * c + DK)
                if not first:
                    pe.wait_ge(lg_made, c)
                for t in range(TT):
                    for k in range(DK):
                        last = nc.tensor.matmul(ps_lg[:, t, 0:CT], qT[:, k, t * P:(t + 1) * P], ctx_t[:, batch(c), k, :].rearrange("p a n -> p (a n)"),
                                                start=(k == 0), stop=(k == DK - 1))
                last.then_inc(lg_mm, 1)

            def batch(c):
                return slice(0, 1) if isinstance(c, int) else bass.ds(c // CB, 1)

            def probabilities(c, first=False):
                pe.wait_ge(pr_made, TT * c + TT)
                if not first:
                    pe.wait_ge(prT_made, c)
                    if not (isinstance(c, int) and c == 1):
                        pe.wait_ge(val_made, c - 1)
                for t in range(TT):
                    last = nc.tensor.transpose(ps_pt[0:CT, t * P:(t + 1) * P], pr[:, t, :], ident[:])
                last.then_inc(p_tr, 1)

            def attention(c, first=False):
                pe.wait_ge(prT_made, c + 1)
                for t in range(TT):
                    if not first or t >= 2:
                        pe.wait_ge(att_made, TT * c + t - 1)
                    nc.tensor.matmul(ps_o[:, t % 2, :], prT[:, t * P:(t + 1) * P], ctx_n[:, batch(c), :].rearrange("p a n -> p (a n)"),
                                     start=True, stop=True).then_inc(o_mm, 1)

            def project(c, n, first=False):
                if n == 0:
                    pe.wait_ge(yl_made, DK * c + DK)
                if not first or n >= 2:
                    pe.wait_ge(pj_out, NM * c + n - 1)
                cols = slice(STEPS[n] * P, (STEPS[n] + 1) * P)
                for k in range(DK):
                    last = mm3(nc, ps_pj[:, n % 2, :], w_hi[:, k, cols], w_lo[:, k, cols], yTh[:, k, :], yTl[:, k, :],
                               k == 0, k == DK - 1)
                last.then_inc(pj_mm, 1)

            def values_transposed(c):
                pe.wait_ge(pj_out, NM * c + STEPS.index(VALUES) + 1)
                pe.wait_ge(prT_made, c + 2 if not (isinstance(c, int) and c == NC - 1) else NC)
                for t in range(TT):
                    last = nc.tensor.transpose(ps_pt[:, t * P:(t + 1) * P], vT[:, t * P:(t + 1) * P], ident[:])
                last.then_inc(v_tr, 1)

            def chunk(c, first_project=False):
                first_part(c)
                transposes(c - 1, y, y_made, y_tr, yl_made)
                probabilities(c)
                if first_project:
                    pe.wait_ge(wl_made, DK)
                project(c - 1, 0, first_project)
                attention(c)
                for n in range(1, NM):
                    project(c - 1, n, first_project)
                values_transposed(c - 1)

            first_part(0, first=True)
            probabilities(0, first=True)
            attention(0, first=True)
            chunk(1, first_project=True)
            with pe.Fori(2, NC) as i:
                chunk(i)
            transposes(NC - 1, y, y_made, y_tr, yl_made)
            for n in range(NM):
                project(NC - 1, n)
            values_transposed(NC - 1)


def phase_attend(nc, y_d, qh_d, ql_d, kh_d, kl_d, v_d, ow, norm1, gate_w, src_d, xe_d, slot_d, wt_d):
    AK, BK = 3, 2
    ORDER = ["VABABADBBA", "VBABAABDBAA", "BBAAVABBD", "AABABABABV", "BBAAAVBBAAA", "BBVBBAAA", "BVBAAABB", "VAABBDBABAA",
             "BVBAAABB", "VBBDBBAAA", "BVBAABAB", "VBAABABDBAAA", "BBVBBAAA", "BDAABBAVAAB", "BVBAABAB", "VBABAABAB"]
    TURN = 13
    LATE_TURN = 14
    A_AT = [sum(o.count("A") for o in ORDER[:kt]) for kt in range(KT + 1)]
    EARLY = A_AT[KT] - A_AT[TURN]

    ADDS = [(0, 0), (1, 2), (0, None), (1, 4), (0, 6), (1, 8), (0, 10), (1, 12), (1, None)]
    ADDED = {t: n + 1 for n, (_, t) in enumerate(ADDS) if t is not None}
    FREED = {1: 0, 4: 1, 5: 2, 6: 3, 7: 4}
    SUMS = [(0, 3), (1, 4), (0, 5), (1, 6), KT - 2, KT - 1, (1, 9)]
    NS = len(SUMS)
    SUM_AT = {7: 0, 9: 1, 11: 2, 13: 3, 0: 4, 1: 5, 2: 6}
    SENDS = {(2, 0): (0,), (2, 5): (1,), (2, 6): (2,), (2, 8): (3, 4), (3, 0): (5,), (3, 5): (6,), (3, 6): (7,)}
    NA = G * TT * (S // CH)
    NSC = G * KT
    SCALE = float(HD) ** -0.5
    ROUTES, ROUTE_TOP = 23, 4
    ZR = 4
    NZ = E * CAP // (P * ZR)
    assert A_AT[KT] == NA
    with Scope(nc, "p2") as s:
        ident = s.sb("ident", [P, P])
        ones = s.sb("ones", [P, P])
        before = s.sb("before", [P, P])
        ow_hi = s.sb("ow_hi", [P, KV, D], F32R)
        ow_lo = s.sb("ow_lo", [P, KV, D], F32R)
        norm_row = s.sb("norm_row", [P, D])
        gw = s.sb("gw", [P, DK, E])
        iota_e = s.sb("iota_e", [P, E])
        ecap = s.sb("ecap", [P, E])
        KS = s.sb("KS", [98, KV, S], F32R)
        QS = s.sb("QS", [98, KV, G, CH], F32R)
        VS = s.sb("VS", [P, KV, KT, HD])
        PR = s.sb("PR", [P, 4, G, CH])
        PP = s.sb("PP", [P, 2, G, CH])
        mxp = s.sb("mxp", [P, TT * G, S // CH])
        mxv = s.sb("mxv", [P, TT, G])
        mh = s.sb("mh", [G, CH], F32R)
        ml = s.sb("ml", [G, CH], F32R)
        pvs = s.sb("pvs", [P, CH])
        att = s.sb("att", [P, CH])
        dens = s.sb("dens", [P, CH])
        at_hi = s.sb("at_hi", [P, KV, CH], F32R)
        at_lo = s.sb("at_lo", [P, KV, CH], F32R)
        Y = s.sb("Y", [P, TT, D])
        SR = s.sb("SR", [P, TT, D])
        srT = s.sb("srT", [P, TT, DK, P])
        sq = s.sb("sq", [P, D])
        ss = s.sb("ss", [P, TT])
        sv = s.sb("sv", [P, TT])
        sr_rstd = s.sb("sr_rstd", [P, TT])
        half = s.sb("half", [P, TT])
        lgt = s.sb("lgt", [P, TT, E])
        top = s.sb("top", [P, TT, 8])
        topi = s.sb("topi", [P, TT, 8], U32)
        topf = s.sb("topf", [P, TT, 2])
        oh = s.sb("oh", [P, 2, TT, E])
        sel = s.sb("sel", [P, TT, E])
        sigm = s.sb("sigm", [P, TT, 2])
        wsum = s.sb("wsum", [P, TT])
        prefix = s.sb("prefix", [P, TT, E])
        base = s.sb("base", [P, TT + 1, E])
        total = s.sb("total", [P, TT, E])
        room = s.sb("room", [P, TT, E])
        prod = s.sb("prod", [P, TT, E])
        slot = s.sb("slot", [P, 2, TT])
        ok = s.sb("ok", [P, 2, TT])
        far = s.sb("far", [P, 2, TT])
        to_slot = s.sb("to_slot", [P, 2, TT], I32)
        from_slot = s.sb("from_slot", [P, 2, TT], I32)
        wt = s.sb("wt", [P, 2, TT])
        ps_a = s.ps("ps_a", [P, AK, CH])
        ps_b = s.ps("ps_b", [P, BK, CH])
        ps_pv = s.ps("ps_pv", [P, CH])
        ps_den = s.ps("ps_den", [P, CH])
        ps_m = s.ps("ps_m", [P, CH])

        (const_in, ident_made, const_made, owh_made, owl_made, zero_made, zero_st) = (
            s.sem(n) for n in ("const_in", "ident_made", "const_made", "owh_made", "owl_made", "zero_made", "zero_st"))
        q_in = [s.sem(f"q_in{g}") for g in range(KV)]
        v_in = [s.sem(f"v_in{g}") for g in range(KV)]
        m_in = s.sem("m_in")
        a_mm, mxp_made, mxv_made, m_tr, mh_made, ml_made = (s.sem(n) for n in ("a_mm", "mxp_made", "mxv_made", "m_tr", "mh_made", "ml_made"))
        sc_mm, ex_made, add_made, pv_mm, den_mm = (s.sem(n) for n in ("sc_mm", "ex_made", "add_made", "pv_mm", "den_mm"))
        pvs_made, dens_made, att_made, ath_made, atl_made = (s.sem(n) for n in ("pvs_made", "dens_made", "att_made", "ath_made", "atl_made"))
        y_in, o_mm, src_made, ss_made, sv_made, rstd_made = (s.sem(n) for n in ("y_in", "o_mm", "src_made", "ss_made", "sv_made", "rstd_made"))
        sr_made, sr_tr, srT_made, g_mm, lgt_made = (s.sem(n) for n in ("sr_made", "sr_tr", "srT_made", "g_mm", "lgt_made"))
        route, exp_made, sel_made, rank_mm, ranked, slots_made = (s.sem(n) for n in ("route", "exp_made", "sel_made", "rank_mm", "ranked", "slots_made"))
        src_st, slot_st, wt_st, sent, gate_sem = (s.sem(n) for n in ("src_st", "slot_st", "wt_st", "sent", "gate"))
        picked, dve_const, inverted = s.sem("picked"), s.sem("dve_const"), s.sem("inverted")
        block = s.block()

        def gate(eng):
            eng.sem_inc(gate_sem, 1)

        def unit(c, g):
            return KV * c + g

        def final(c):
            return isinstance(c, int) and c == NC - 1

        def bank(c, t):
            return ps_a[:, t, :] if final(c) and t < AK else ps_m[:]

        def runs_ahead(c, g, kt, i, last):
            n = EARLY + A_AT[kt] + i
            off = 1 + n // NA
            return None if last and g + off >= KV else (unit(c, g) + off, (g + off) % KV, n % NA)

        @block.sync
        def _(sp):
            def hold(sem, n):
                sp.wait_ge(sem, n)
                gate(sp)

            def load(c, g):
                row = c // CB * CB
                heads = slice(G * HD * g, G * HD * (g + 1))
                for part, src in ((0, qh_d), (1, qh_d), (2, ql_d)):
                    sp.dma_start(f32(QS[32 * part:32 * part + 32, g, :, :]),
                                 src[bass.ds(c, 1), heads, :].rearrange("a (j d) q -> d (a j) q", d=HD)).then_inc(q_in[g], 16)
                for part, src in ((0, kh_d), (1, kl_d), (2, kh_d)):
                    sp.dma_start(f32(KS[32 * part:32 * part + 32, g, :]).rearrange("d (n q) -> d n q", n=CB),
                                 src[bass.ds(row, CB), HD * g:HD * (g + 1), :].rearrange("n d q -> d n q")).then_inc(q_in[g], 16)
                sp.dma_start(VS[:, g, :, :].rearrange("p (n t) d -> p n t d", n=CB),
                             v_d[bass.ds(row, CB), :, HD * g:HD * (g + 1)].rearrange("n (t p) d -> p n t d", p=P)).then_inc(v_in[g], 16)

            def load_y(c):
                sp.dma_start(Y[:], y_d[bass.ds(c, 1)].rearrange("a (t p) d -> p (a t) d", p=P)).then_inc(y_in, 16)

            def maxima_to(g, n):
                hold(ml_made, n)
                sp.dma_start(f32(QS[96:97, g, :, :]), f32(mh[:])).then_inc(m_in, 16)
                sp.dma_start(f32(QS[97:98, g, :, :]), f32(ml[:])).then_inc(m_in, 16)

            def body(c, first=False, last=False):
                nxt = None if last else (c + 1 if isinstance(c, int) else sp.snap(c + 1))
                for g in range(KV):
                    if not (last and g == KV - 1):
                        maxima_to((g + 1) % KV, unit(c, g) + 2)
                    if g == 0 and not first:
                        hold(sr_made, TT * c)
                        sp.dma_start(src_d[bass.ds(c - 1, 1)].rearrange("a (t p) d -> p (a t) d", p=P), SR[:]).then_inc(src_st, 16)
                        hold(src_made, TT * c)
                    if g == 0:
                        load_y(c)
                    if first:
                        with sp.Fori(NZ // KV * g, NZ // KV * (g + 1)) as i:
                            sp.dma_start(xe_rows[bass.ds(i, 1)].rearrange("a p n -> p (a n)"), zeros).then_inc(zero_st, 16)
                    if g == 3 and not first:
                        hold(slots_made, c)
                        store_slots(c - 1)
                    if not last:
                        hold(sc_mm, NSC * (unit(c, g) + 1))
                        hold(pv_mm, KT * (unit(c, g) + 1))
                        load(nxt, g)

            def store_slots(c):
                sp.dma_start(slot_d[bass.ds(c, 1)].rearrange("a p n -> p (a n)"), from_slot[:].rearrange("p k t -> p (k t)")).then_inc(slot_st, 16)
                sp.dma_start(wt_d[bass.ds(c, 1)].rearrange("a p n -> p (a n)"), wt[:].rearrange("p k t -> p (k t)")).then_inc(wt_st, 16)

            load(0, 0)
            ow_raw = PR[:, 0, :, :]
            sp.dma_start(ow_raw, ow.rearrange("(g p) n -> p g n", p=P)).then_inc(const_in, 16)
            sp.dma_start(norm_row[:], over_rows(norm1)).then_inc(const_in, 16)
            sp.dma_start(gw[:], gate_w.rearrange("(k p) e -> p k e", p=P)).then_inc(const_in, 16)
            for g in range(1, KV):
                load(0, g)
            zeros = SR[:].rearrange("p t d -> p (t d)")
            xe_rows = xe_d.rearrange("(n p r) d -> n p (r d)", p=P, r=ZR)
            maxima_to(0, 1)
            hold(zero_made, 1)
            body(0, first=True)
            with sp.Fori(1, NC - 1) as i:
                body(i)
            body(NC - 1, last=True)
            hold(sr_made, TT * NC)
            sp.dma_start(src_d[NC - 1].rearrange("(t p) d -> p t d", p=P), SR[:]).then_inc(src_st, 16)
            hold(slots_made, NC)
            store_slots(NC - 1)
            for sem in (src_st, slot_st, wt_st, y_in):
                sp.wait_ge(sem, 16 * NC)
            sp.wait_ge(sent, 16 * 2 * TT * NC)
            sp.wait_ge(zero_st, 16 * NZ)

        @block.gpsimd
        def _(pool):
            make_identity(nc, pool, ident, ident_made)
            nc.gpsimd.memset(ones[:], 1.0).then_inc(const_made, 1)
            nc.gpsimd.memset(half[:], -0.5).then_inc(const_made, 1)
            for e in range(E):
                nc.gpsimd.memset(iota_e[:, e:e + 1], float(e)).then_inc(const_made, 1)
                nc.gpsimd.memset(ecap[:, e:e + 1], float(e * CAP)).then_inc(const_made, 1)
            pool.wait_ge(const_made, 2 + 2 * E)
            nc.gpsimd.affine_select(out=before[:], in_=ones[:], compare_op=ALU.is_gt, fill=0.0, base=0,
                                    pattern=[[1, P]], channel_multiplier=-1).then_inc(const_made, 1)
            pool.wait_ge(const_in, 48)

            def add(u, n, first):
                buf, tile = ADDS[n]
                if n in FREED and not (first and FREED[n] == 0):
                    pool.wait_ge(den_mm, NS * u + FREED[n])
                if tile is None:
                    pool.wait_ge(add_made, len(ADDS) * u + n)
                    nc.gpsimd.tensor_tensor(PP[:, buf, :, :], PP[:, buf, :, :], PP[:, 1 - buf, :, :], ALU.add).then_inc(add_made, 1)
                else:
                    pool.wait_ge(ex_made, NSC * u + G * (tile + 2))
                    if ADDS[n - 1][1] is None and not (first and n == 0):
                        pool.wait_ge(add_made, len(ADDS) * u + n)
                    a = tile % 4
                    nc.gpsimd.tensor_tensor(PP[:, buf, :, :], PR[:, a, :, :], PR[:, a + 1, :, :], ALU.add).then_inc(add_made, 1)

            def norm_power(c):
                pool.wait_ge(ss_made, TT * c + TT)
                gate(pool)
                nc.gpsimd.tensor_scalar(sv[:], ss[:], 1.0 / D, RMS_EPS, ALU.mult, ALU.add).then_inc(sv_made, 1)
                pool.wait_ge(sv_made, c + 1)
                nc.gpsimd.tensor_tensor(sr_rstd[:], sv[:], half[:], ALU.pow).then_inc(rstd_made, 1)

            def send(c, ns):
                if 0 in ns:
                    pool.wait_ge(zero_st, 16 * NZ)
                    pool.wait_ge(slots_made, c + 1)
                    gate(pool)
                for n in ns:
                    k, t = n // TT, n % TT
                    nc.gpsimd.indirect_dma_start(
                        out=xe_d, out_offset=bass.IndirectOffsetOnAxis(ap=to_slot[:, k, t:t + 1].bitcast(U32), axis=0),
                        in_=SR[:, t, :], in_offset=None, bounds_check=E * CAP - 1, oob_is_err=False).then_inc(sent, 16)

            def body(c, first=False):
                for g in range(KV):
                    for n in range(len(ADDS)):
                        add(unit(c, g), n, first and g == 0)
                        if g == 0 and not first:
                            if n == 4:
                                norm_power(c - 1)
                        if (g, n) in SENDS and not first:
                            send(c - 1, SENDS[g, n])

            body(0, first=True)
            with pool.Fori(1, NC) as i:
                body(i)
            norm_power(NC - 1)
            send(NC - 1, range(2 * TT))

        @block.scalar
        def _(act):
            ow_raw = PR[:, 0, :, :]
            act.wait_ge(const_in, 48)
            for g in range(KV):
                nc.scalar.activation(ow_hi[:, g, :], ow_raw[:, g, :], ACT.Copy).then_inc(owh_made, 1)
            act.wait_ge(owl_made, KV)

            def exps(c, g, kt, first):
                u = unit(c, g)
                slot_ = kt % 4
                if kt >= 4:
                    act.wait_ge(pv_mm, KT * u + kt - 3)
                    act.wait_ge(add_made, len(ADDS) * u + ADDED[(kt - 4) // 2 * 2])
                elif not first:
                    act.wait_ge(pv_mm, KT * u + kt - 3)
                    if kt < 2:
                        act.wait_ge(add_made, len(ADDS) * (u - 1) + ADDED[KT - 4])
                    else:
                        act.wait_ge(den_mm, NS * u + kt - 4)
                for j in range(G):
                    n = NSC * g + G * kt + j
                    act.wait_ge(sc_mm, NSC * KV * c + n + 1)
                    nc.scalar.activation(PR[:, slot_, j, :], ps_b[:, n % BK, :], ACT.Exp, scale=SCALE).then_inc(ex_made, 1)

            def values_out(u, first=False):
                act.wait_ge(pv_mm, KT * u)
                if not first:
                    act.wait_ge(att_made, u - 1)
                nc.scalar.activation(pvs[:], ps_pv[:], ACT.Copy).then_inc(pvs_made, 1)

            def sums_out(u):
                act.wait_ge(den_mm, NS * u)
                nc.scalar.activation(dens[:], ps_den[:], ACT.Copy).then_inc(dens_made, 1)

            def squares(c, t):
                act.wait_ge(src_made, TT * c + t + 1)
                if t > 0:
                    act.wait_ge(ss_made, TT * c + t)
                nc.scalar.activation(sq[:], SR[:, t, :], ACT.Square, accum_out=ss[:, t:t + 1]).then_inc(ss_made, 1)

            def rows_out(c, t):
                act.wait_ge(sr_tr, TT * c + t + 1)
                nc.scalar.activation(srT[:, t, :, :], bank(c, t).rearrange("p (k n) -> p k n", k=DK), ACT.Copy).then_inc(srT_made, 1)

            def sigmoid_exp(c):
                act.wait_ge(route, ROUTE_TOP + ROUTES * c)
                nc.scalar.activation(sigm[:], top[:, :, 0:2], ACT.Exp, scale=-1.0).then_inc(exp_made, 1)

            def body(c, first=False):
                for g in range(KV):
                    for kt in range(KT):
                        exps(c, g, kt, first and g == 0)
                        if kt == 1 and not (first and g == 0):
                            values_out(unit(c, g), first and g == 1)
                        if kt == 2 and not (first and g == 0):
                            sums_out(unit(c, g))
                        if g == 0 and not first:
                            if 7 <= kt < 7 + TT:
                                squares(c - 1, kt - 7)
                            if 11 <= kt < 11 + TT:
                                rows_out(c - 1, kt - 11)
                        if g == 1 and not first and kt == 3:
                            sigmoid_exp(c - 1)

            body(0, first=True)
            with act.Fori(1, NC) as i:
                body(i)
            values_out(KV * NC)
            sums_out(KV * NC)
            for t in range(TT):
                squares(NC - 1, t)
            for t in range(TT):
                rows_out(NC - 1, t)
            sigmoid_exp(NC - 1)

        @block.vector
        def _(dve):
            ow_raw = PR[:, 0, :, :]
            nc.vector.memset(f32(KS[96:98, :, :]), 1.0).then_inc(dve_const, 1)
            nc.vector.memset(base[:, TT, :], 0.0).then_inc(dve_const, 1)

            def maximum(u, g, a):
                dve.wait_ge(a_mm, NA * u + a + 1)
                if a == 0 and not (isinstance(u, int) and u == 0):
                    dve.wait_ge(mxv_made, u)
                nc.vector.reduce_max(mxp[:, a // (S // CH), a % (S // CH):a % (S // CH) + 1], ps_a[:, (NA * g + a) % AK, :], AXX).then_inc(mxp_made, 1)

            def maxima(u, first=False):
                dve.wait_ge(mxp_made, NA * (u + 1))
                if not first:
                    dve.wait_ge(m_tr, u)
                nc.vector.reduce_max(mxv[:].rearrange("p t j -> p (t j)"), mxp[:], AXX).then_inc(mxv_made, 1)

            def maxima_split(u, first=False):
                dve.wait_ge(m_tr, u + 1)
                if not first:
                    dve.wait_ge(m_in, 32 * u)
                nc.vector.tensor_scalar(mh[:], ps_m[0:G, :], -1.0, None, ALU.mult).then_inc(mh_made, 1)
                dve.wait_ge(mh_made, u + 1)
                nc.vector.scalar_tensor_tensor(ml[:], ps_m[0:G, :], -1.0, f32(mh[:]), ALU.mult, ALU.subtract).then_inc(ml_made, 1)

            def invert(u, part):
                dve.wait_ge(dens_made, u + 1)
                cols = slice(part * P, (part + 1) * P)
                nc.vector.reciprocal(dens[:, cols], dens[:, cols]).then_inc(inverted, 1)

            def normalise(u, g):
                dve.wait_ge(inverted, TT * u + TT)
                nc.vector.tensor_tensor(att[:], pvs[:], dens[:], ALU.mult).then_inc(att_made, 1)
                dve.wait_ge(att_made, u + 1)
                nc.vector.tensor_copy(at_hi[:, g, :], att[:]).then_inc(ath_made, 1)
                dve.wait_ge(ath_made, u + 1)
                nc.vector.tensor_tensor(at_lo[:, g, :], att[:], f32(at_hi[:, g, :]), ALU.subtract).then_inc(atl_made, 1)

            def project_out(c, t):
                dve.wait_ge(o_mm, TT * c + t + 1)
                if t == 0:
                    dve.wait_ge(y_in, 16 * c + 16)
                    dve.wait_ge(zero_st, 16 * NZ)
                if not (isinstance(c, int) and c == 0) and t == 0:
                    dve.wait_ge(src_st, 16 * c)
                    dve.wait_ge(sent, 16 * 2 * TT * c)
                nc.vector.tensor_tensor(SR[:, t, :], bank(c, t), Y[:, t, :], ALU.add).then_inc(src_made, 1)

            def norm(c, t):
                dve.wait_ge(rstd_made, c + 1)
                nc.vector.scalar_tensor_tensor(SR[:, t, :], SR[:, t, :], sr_rstd[:, t:t + 1], norm_row[:], ALU.mult, ALU.mult).then_inc(sr_made, 1)

            def per_token(ap):
                return ap.rearrange("p (t a) -> p t a", a=1).broadcast_to((P, TT, E))

            def per_expert(ap):
                return ap.rearrange("p (a e) -> p a e", a=1).broadcast_to((P, TT, E))

            def step(c, k):
                dve.wait_ge(route, ROUTES * c + k)

            def choose(c):
                dve.wait_ge(g_mm, c + 1)
                if not (isinstance(c, int) and c == 0):
                    dve.wait_ge(exp_made, c)
                nc.vector.tensor_scalar(lgt[:], ps_m[:, 0:TT * E].rearrange("p (t e) -> p t e", t=TT), 17.5, None, ALU.min).then_inc(lgt_made, 1)
                dve.wait_ge(lgt_made, c + 1)
                gate(dve)
                for t in range(TT):
                    nc.vector.max(top[:, t, :], lgt[:, t, :]).then_inc(route, 1)

            def choose_both(c):
                step(c, TT)
                gate(dve)
                for t in range(TT):
                    nc.vector.max_index(topi[:, t, :], top[:, t, :], lgt[:, t, :]).then_inc(route, 1)
                step(c, 8)
                nc.vector.tensor_copy(topf[:], topi[:, :, 0:2]).then_inc(route, 1)
                step(c, 9)
                for k in range(2):
                    nc.vector.tensor_tensor(oh[:, k, :, :], topf[:, :, k:k + 1].broadcast_to((P, TT, E)), per_expert(iota_e[:]), ALU.is_equal).then_inc(route, 1)
                step(c, 11)
                nc.vector.tensor_tensor(sel[:], oh[:, 0, :, :], oh[:, 1, :, :], ALU.add).then_inc(sel_made, 1)

            def weights(c):
                dve.wait_ge(exp_made, c + 1)
                nc.vector.tensor_scalar(sigm[:], sigm[:], 1.0, None, ALU.add).then_inc(route, 1)
                step(c, 12)
                nc.vector.reciprocal(sigm[:], sigm[:]).then_inc(route, 1)
                step(c, 13)
                nc.vector.scalar_tensor_tensor(wsum[:], sigm[:, :, 0], 1e-6, sigm[:, :, 1], ALU.add, ALU.add).then_inc(route, 1)
                step(c, 14)
                nc.vector.reciprocal(wsum[:], wsum[:]).then_inc(route, 1)

            def rank(c):
                dve.wait_ge(rank_mm, c + 1)
                k0 = 7 * c
                nc.vector.tensor_copy(total[:], ps_m[:, TT * E:2 * TT * E].rearrange("p (t e) -> p t e", t=TT)).then_inc(ranked, 1)
                nc.vector.tensor_copy(base[:, 0, :], base[:, TT, :]).then_inc(ranked, 1)
                for t in range(TT):
                    dve.wait_ge(ranked, k0 + 2 + t)
                    nc.vector.tensor_tensor(base[:, t + 1, :], base[:, t, :], total[:, t, :], ALU.add).then_inc(ranked, 1)
                dve.wait_ge(ranked, k0 + 6)
                nc.vector.tensor_tensor(prefix[:], ps_m[:, 0:TT * E].rearrange("p (t e) -> p t e", t=TT), base[:, 0:TT, :], ALU.add).then_inc(ranked, 1)
                dve.wait_ge(ranked, k0 + 7)
                nc.vector.tensor_scalar(room[:], prefix[:], float(CAP), None, ALU.is_lt).then_inc(route, 1)
                step(c, 16)
                nc.vector.tensor_tensor(prefix[:], prefix[:], per_expert(ecap[:]), ALU.add).then_inc(route, 1)

            def place(c, k):
                step(c, 17)
                if k == 0 and not (isinstance(c, int) and c == 0):
                    dve.wait_ge(sent, 16 * 2 * TT * c)
                    dve.wait_ge(slot_st, 16 * c)
                    dve.wait_ge(wt_st, 16 * c)
                for n, (out, of) in enumerate(((slot, prefix), (ok, room)), start=2 * k):
                    if n > 0:
                        dve.wait_ge(picked, 8 * c + 2 * n)
                    nc.vector.tensor_tensor(prod[:], oh[:, k, :, :], of[:], ALU.mult).then_inc(picked, 1)
                    dve.wait_ge(picked, 8 * c + 2 * n + 1)
                    nc.vector.reduce_sum(out[:, k, :], prod[:], AXX).then_inc(picked, 1)

            def finish(c):
                dve.wait_ge(picked, 8 * c + 8)
                nc.vector.tensor_scalar(far[:], ok[:], -2.0 * E * CAP, 2.0 * E * CAP, ALU.mult, ALU.add).then_inc(route, 1)
                step(c, 18)
                nc.vector.tensor_tensor(to_slot[:], slot[:], far[:], ALU.add).then_inc(route, 1)
                nc.vector.tensor_tensor(from_slot[:], slot[:], ok[:], ALU.mult).then_inc(route, 1)
                nc.vector.tensor_tensor(wt[:], sigm[:].rearrange("p t k -> p k t"), ok[:], ALU.mult).then_inc(route, 1)
                step(c, 21)
                nc.vector.tensor_tensor(wt[:, 0, :], wt[:, 0, :], wsum[:], ALU.mult).then_inc(route, 1)
                nc.vector.tensor_tensor(wt[:, 1, :], wt[:, 1, :], wsum[:], ALU.mult).then_inc(route, 1)
                step(c, 23)
                nc.vector.tensor_copy(base[:, TT, :], base[:, TT, :]).then_inc(slots_made, 1)

            def body(c, first=False, last=False):
                for g in range(KV):
                    u = unit(c, g)
                    for kt in range(KT):
                        split_first = g == 0 and not first and kt == LATE_TURN + 1
                        if split_first:
                            maxima_split(u + 1)
                        for i in range(A_AT[kt + 1] - A_AT[kt]):
                            which = runs_ahead(c, g, kt, i, last)
                            if which:
                                maximum(*which)
                        if not (last and g == KV - 1):
                            if kt == TURN - 1:
                                maxima(u + 1)
                            if kt == TURN and not (g == 0 and not first):
                                maxima_split(u + 1)
                        if not (first and g == 0):
                            parts, done_at = ({3: (0, 1), 4: (2, 3)}, 4) if g == 0 else ({3: (0,), 4: (1,), 5: (2,), 6: (3,)}, 7)
                            for part in parts.get(kt, ()):
                                invert(u - 1, part)
                            if kt == done_at:
                                normalise(u - 1, (g - 1) % KV)
                        if g == 0 and not first:
                            if 6 <= kt < 6 + TT:
                                project_out(c - 1, kt - 6)
                            if 10 <= kt < 10 + TT:
                                norm(c - 1, kt - 10)
                        if g == 1 and not first:
                            if kt == 1:
                                choose(c - 1)
                            if kt == 2:
                                choose_both(c - 1)
                            if kt == 4:
                                weights(c - 1)
                            if kt == 6:
                                rank(c - 1)
                            if kt == 12:
                                place(c - 1, 0)
                            if kt == 15:
                                place(c - 1, 1)
                        if g == 2 and not first and kt == 0:
                            finish(c - 1)

            for a in range(NA):
                maximum(0, 0, a)
            maxima(0, first=True)
            for a in range(EARLY):
                maximum(1, 1, a)
            maxima_split(0, first=True)
            for g in range(KV):
                dve.wait_ge(owh_made, g + 1)
                nc.vector.tensor_tensor(ow_lo[:, g, :], ow_raw[:, g, :], f32(ow_hi[:, g, :]), ALU.subtract).then_inc(owl_made, 1)
            nc.vector.memset(SR[:], 0.0).then_inc(zero_made, 1)
            dve.wait_ge(dve_const, 2)
            dve.wait_ge(const_made, 3 + 2 * E)
            body(0, first=True)
            with dve.Fori(1, NC - 1) as i:
                body(i)
            body(NC - 1, last=True)
            for part in range(TT):
                invert(KV * NC - 1, part)
            normalise(KV * NC - 1, KV - 1)
            for t in range(TT):
                project_out(NC - 1, t)
            for t in range(TT):
                norm(NC - 1, t)
            choose(NC - 1)
            choose_both(NC - 1)
            weights(NC - 1)
            rank(NC - 1)
            place(NC - 1, 0)
            place(NC - 1, 1)
            finish(NC - 1)

        @block.tensor
        def _(pe):
            def score_maxima(u, g, a):
                t, j, kb = a // (G * CB), a // CB % G, a % CB
                n = NA * g + a
                pe.wait_ge(mxp_made, NA * u + a - (AK - 1 if n else 0))
                nc.tensor.matmul(ps_a[:, n % AK, :], QS[0:96, g, j, t * P:(t + 1) * P], KS[0:96, g, kb * CH:(kb + 1) * CH],
                                 start=True, stop=True).then_inc(a_mm, 1)

            def maxima_transposed(u):
                pe.wait_ge(mxv_made, u + 1)
                for t in range(TT):
                    last = nc.tensor.transpose(ps_m[0:G, t * P:(t + 1) * P], mxv[:, t, :], ident[:])
                last.then_inc(m_tr, 1)

            def scores(c, g, kt, j, first):
                n = NSC * g + G * kt + j
                if n >= BK:
                    pe.wait_ge(ex_made, NSC * KV * c + n - BK + 1)
                elif not first:
                    pe.wait_ge(ex_made, NSC * KV * c + n - BK + 1)
                nc.tensor.matmul(ps_b[:, n % BK, :], KS[:, g, kt * P:(kt + 1) * P], QS[:, g, j, :],
                                 start=True, stop=True).then_inc(sc_mm, 1)

            def values(u, g, kt):
                pe.wait_ge(ex_made, NSC * u + G * (kt + 1))
                for j in range(G):
                    last = nc.tensor.matmul(ps_pv[HD * j:HD * (j + 1), :], VS[:, g, kt, :], PR[:, kt % 4, j, :],
                                            start=(kt == 0), stop=(kt == KT - 1))
                last.then_inc(pv_mm, 1)

            def denominators(u, n):
                if isinstance(SUMS[n], tuple):
                    pe.wait_ge(add_made, len(ADDS) * u + SUMS[n][1])
                    src = PP[:, SUMS[n][0], :, :]
                else:
                    src = PR[:, SUMS[n] % 4, :, :]
                for j in range(G):
                    last = nc.tensor.matmul(ps_den[HD * j:HD * (j + 1), :], ones[:, 0:HD], src[:, j, :],
                                            start=(n == 0), stop=(n == NS - 1))
                last.then_inc(den_mm, 1)

            def project_out(c, t):
                if t == 0:
                    pe.wait_ge(atl_made, KV * (c + 1))
                    pe.wait_ge(ml_made, KV * (c + 1) + (0 if final(c) else 1))
                    if final(c):
                        pe.wait_ge(mxp_made, NA * KV * NC)
                elif not final(c):
                    pe.wait_ge(src_made, TT * c + t)
                for g in range(KV):
                    toks = slice(t * P, (t + 1) * P)
                    last = mm3(nc, bank(c, t), at_hi[:, g, toks], at_lo[:, g, toks], ow_hi[:, g, :], ow_lo[:, g, :],
                               g == 0, g == KV - 1)
                last.then_inc(o_mm, 1)

            def rows_transposed(c, t):
                pe.wait_ge(sr_made, TT * c + t + 1)
                if t == 0:
                    pe.wait_ge(src_made, TT * c + TT)
                elif not final(c):
                    pe.wait_ge(srT_made, TT * c + t)
                for k in range(DK):
                    last = nc.tensor.transpose(bank(c, t)[:, k * P:(k + 1) * P], SR[:, t, k * P:(k + 1) * P], ident[:])
                last.then_inc(sr_tr, 1)

            def logits(c, tiles):
                pe.wait_ge(srT_made, TT * c + TT)
                for t in tiles:
                    for k in range(DK):
                        last = nc.tensor.matmul(ps_m[:, t * E:(t + 1) * E], srT[:, t, k, :], gw[:, k, :], start=(k == 0), stop=(k == DK - 1))
                if t == TT - 1:
                    last.then_inc(g_mm, 1)

            def ranks(c):
                pe.wait_ge(sel_made, c + 1)
                nc.tensor.matmul(ps_m[:, 0:TT * E], before[:], sel[:].rearrange("p t e -> p (t e)"), start=True, stop=True)
                nc.tensor.matmul(ps_m[:, TT * E:2 * TT * E], ones[:], sel[:].rearrange("p t e -> p (t e)"), start=True, stop=True).then_inc(rank_mm, 1)

            def body(c, first=False, last=False):
                for g in range(KV):
                    u = unit(c, g)
                    ahead = not (last and g == KV - 1)
                    for kt in range(KT):
                        i, j = 0, 0
                        for what in ORDER[kt]:
                            if what == "A":
                                which = runs_ahead(c, g, kt, i, last)
                                if which:
                                    if which[2] == 0:
                                        pe.wait_ge(q_in[which[1]], 96 * (c + (g + 2) // KV) + 96)
                                    score_maxima(*which)
                                i += 1
                            elif what == "B":
                                if kt == 0 and j == 0:
                                    pe.wait_ge(m_in, 32 * (u + 1))
                                scores(c, g, kt, j, first)
                                j += 1
                            elif what == "V" and kt < 2:
                                if not (first and g == 0):
                                    values(u - 1, (g - 1) % KV, KT - 2 + kt)
                            elif what == "V":
                                if kt == 2:
                                    pe.wait_ge(v_in[g], 16 * c + 16)
                                    if not (first and g == 0):
                                        pe.wait_ge(pvs_made, u)
                                values(u, g, kt - 2)
                            elif SUM_AT[kt] >= NS - 3:
                                if not (first and g == 0):
                                    denominators(u - 1, SUM_AT[kt])
                            else:
                                if SUM_AT[kt] == 0 and not (first and g == 0):
                                    pe.wait_ge(dens_made, u)
                                denominators(u, SUM_AT[kt])
                            if kt == TURN and what == "V" and ahead and not (g == 0 and not first):
                                if g == 1 and not first:
                                    pe.wait_ge(ranked, 7 * c)
                                maxima_transposed(u + 1)
                        if g == 0 and not first:
                            if 6 <= kt < 6 + TT:
                                project_out(c - 1, kt - 6)
                            if 11 <= kt < 11 + TT:
                                rows_transposed(c - 1, kt - 11)
                        if kt == LATE_TURN and ahead and g == 0 and not first:
                            pe.wait_ge(srT_made, TT * c)
                            maxima_transposed(u + 1)
                        if kt == 15 and g == 0 and not first:
                            pe.wait_ge(ml_made, u + 2)
                            logits(c - 1, (0, 1))
                        if kt == 0 and g == 1 and not first:
                            logits(c - 1, (2, 3))
                        if kt == 5 and g == 1 and not first:
                            ranks(c - 1)

            pe.wait_ge(q_in[0], 96)
            for a in range(NA):
                if a < AK:
                    t, j, kb = a // (G * CB), a // CB % G, a % CB
                    nc.tensor.matmul(ps_a[:, a, :], QS[0:96, 0, j, t * P:(t + 1) * P], KS[0:96, 0, kb * CH:(kb + 1) * CH],
                                     start=True, stop=True).then_inc(a_mm, 1)
                else:
                    score_maxima(0, 0, a)
            pe.wait_ge(q_in[1], 96)
            for a in range(EARLY):
                score_maxima(1, 1, a)
            pe.wait_ge(ident_made, 2)
            maxima_transposed(0)
            pe.wait_ge(const_made, 3 + 2 * E)
            pe.wait_ge(dve_const, 2)
            pe.wait_ge(owl_made, KV)
            body(0, first=True)
            with pe.Fori(1, NC - 1) as i:
                body(i)
            body(NC - 1, last=True)
            for kt in range(2):
                values(KV * NC - 1, KV - 1, KT - 2 + kt)
            for n in range(NS - 3, NS):
                denominators(KV * NC - 1, n)
            for t in range(TT):
                project_out(NC - 1, t)
            for t in range(TT):
                rows_transposed(NC - 1, t)
            logits(NC - 1, range(TT))
            ranks(NC - 1)


def phase_experts(nc, xe_d, w1, w2, ye_d, kept, src_d, x1_d, slot_d, wt_d, norm2):
    TILES = [3, 3, 2, 2]
    NB = len(TILES)
    WB = max(TILES)
    FK = F // P
    BETWEEN = {3: (0, 1), 5: (2, 3)}
    W2_SPLIT = {0: (0, 1), 1: (2, 3), 2: (4, 5), 4: (6, 7)}
    HB = 3
    FIRST = [sum(TILES[:b]) for b in range(NB)]
    NT = sum(TILES)
    assert NT * P == CAP and NB % 2 == 0
    with Scope(nc, "p3") as s:
        ident = s.sb("ident", [P, P])
        w1_raw = s.sb("w1_raw", [P, DK, F])
        w2_raw = s.sb("w2_raw", [P, FK, D])
        w1h = s.sb("w1h", [P, DK, F], F32R)
        w1l = s.sb("w1l", [P, DK, F], F32R)
        w2h = s.sb("w2h", [P, FK, D], F32R)
        w2l = s.sb("w2l", [P, FK, D], F32R)
        XE = s.sb("XE", [P, 2, WB, D])
        xTh = s.sb("xTh", [P, 2, DK, WB * P], F32R)
        xTl = s.sb("xTl", [P, 2, DK, WB * P], F32R)
        hf = s.sb("hf", [P, 2, WB * P])
        hh = s.sb("hh", [P, 2, FK, WB * P], F32R)
        hl = s.sb("hl", [P, 2, FK, WB * P], F32R)
        YE = s.sb("YE", [P, 2, D])
        ps_t = s.ps("ps_t", [P, 2, CH])
        ps_h = s.ps("ps_h", [P, HB + 1, CH])
        ps_y = s.ps("ps_y", [P, 2, CH])
        ident_made = s.sem("ident_made")
        w1_in, w2_in, w1h_made, w1l_made, w2h_made, w2l_made = (s.sem(n) for n in ("w1_in", "w2_in", "w1h_made", "w1l_made", "w2h_made", "w2l_made"))
        xe_in = [s.sem("xe_in0"), s.sem("xe_in1")]
        x_tr, xh_made, xl_made, h_mm, hf_made, hh_made, hl_made, y_mm, y_out = (
            s.sem(n) for n in ("x_tr", "xh_made", "xl_made", "h_mm", "hf_made", "hh_made", "hl_made", "y_mm", "y_out"))
        y_st = [s.sem("y_st0"), s.sem("y_st1")]
        kept_in = s.sem("kept_in")
        gate_sem = s.sem("gate")
        block = s.block()

        def hold(eng, sem, n):
            eng.wait_ge(sem, n)
            eng.sem_inc(gate_sem, 1)

        xe_v = xe_d.rearrange("(e t p) d -> e p t d", p=P, t=NT)
        ye_v = ye_d.rearrange("(e t p) d -> e p t d", p=P, t=NT)
        w1_v = w1.rearrange("e (k p) f -> e p k f", p=P)
        w2_v = w2.rearrange("e (k p) d -> e p k d", p=P)

        @block.sync
        def _(sp):
            def load_block(e, b):
                sp.dma_start(XE[:, b % 2, 0:TILES[b], :],
                             xe_v[bass.ds(e, 1), :, FIRST[b]:FIRST[b] + TILES[b], :].rearrange("a p t d -> p (a t) d")).then_inc(xe_in[b % 2], 16)

            def load_w1(e):
                sp.dma_start(w1_raw[:], w1_v[bass.ds(e, 1)].rearrange("a p k f -> p (a k) f")).then_inc(w1_in, 16)

            def load_w2(e):
                sp.dma_start(w2_raw[:], w2_v[bass.ds(e, 1)].rearrange("a p k f -> p (a k) f")).then_inc(w2_in, 16)

            def body(e, last=False):
                for b in range(NB):
                    if b < NB - 2 or not last:
                        hold(sp, x_tr, DK * (NB * e + b + 1))
                        load_block(e + (b + 2) // NB, (b + 2) % NB)
                    if not last and b == 0:
                        hold(sp, w1l_made, DK * (e + 1))
                        load_w1(e + 1)
                    if not last and b == 1:
                        hold(sp, w2l_made, FK * (e + 1))
                        load_w2(e + 1)

            load_w1(0)
            load_block(0, 0)
            load_block(0, 1)
            load_w2(0)
            with sp.Fori(0, E - 1) as e:
                body(e)
            sp.dma_start(kept.slots[:].rearrange("p c k t -> p c (k t)"), slot_d.rearrange("c p n -> p c n")).then_inc(kept_in, 16)
            sp.dma_start(kept.wts[:].rearrange("p c k t -> p c (k t)"), wt_d.rearrange("c p n -> p c n")).then_inc(kept_in, 16)
            sp.dma_start(kept.norm_row[:], over_rows(norm2)).then_inc(kept_in, 16)
            body(E - 1, last=True)
            for c in range(KEEP):
                sp.dma_start(kept.src[:, c, :, :], src_d[c].rearrange("(t p) d -> p t d", p=P)).then_inc(kept_in, 16)
                sp.dma_start(kept.x1[:, c, :, :], x1_d[c].rearrange("(t p) d -> p t d", p=P)).then_inc(kept_in, 16)
            sp.wait_ge(kept_in, 16 * (3 + 2 * KEEP))

        @block.gpsimd
        def _(pool):
            make_identity(nc, pool, ident, ident_made)

            def store(e, b, t):
                n = FIRST[b] + t
                hold(pool, y_out, NT * e + n + 1)
                pool.dma_start(ye_v[bass.ds(e, 1), :, n:n + 1, :].rearrange("a p t d -> p (a t d)"), YE[:, n % 2, :]).then_inc(y_st[n % 2], 16)

            with pool.Fori(0, E) as e:
                for b in range(NB):
                    for t in range(TILES[b]):
                        store(e, b, t)
            for i in range(2):
                pool.wait_ge(y_st[i], 16 * E * NT // 2)

        @block.scalar
        def _(act):
            def split_w1(e):
                act.wait_ge(w1_in, 16 * e + 16)
                if not (isinstance(e, int) and e == 0):
                    act.wait_ge(h_mm, FK * NB * e)
                for k in range(DK):
                    nc.scalar.activation(w1h[:, k, :], w1_raw[:, k, :], ACT.Copy).then_inc(w1h_made, 1)

            def split_w2(e, ks):
                if 0 in ks:
                    act.wait_ge(w2_in, 16 * e + 16)
                    if not (isinstance(e, int) and e == 0):
                        act.wait_ge(y_mm, NT * e)
                for k in ks:
                    nc.scalar.activation(w2h[:, k, :], w2_raw[:, k, :], ACT.Copy).then_inc(w2h_made, 1)

            def rows_high(e, b, ks, first=False):
                n = TILES[b] * P
                m = NB * e + b
                for k in ks:
                    act.wait_ge(x_tr, DK * m + k + 1)
                    if k == 0 and not first:
                        act.wait_ge(h_mm, FK * (m - 1))
                    nc.scalar.activation(xTh[:, b % 2, k, 0:n], ps_t[:, k % 2, 0:n], ACT.Copy).then_inc(xh_made, 1)

            def hidden(e, b, first=False, with_w2=False, last=False):
                n = TILES[b] * P
                m = NB * e + b
                for f in range(FK):
                    act.wait_ge(h_mm, FK * m + f + 1)
                    if not first or f >= 2:
                        act.wait_ge(hl_made, FK * m + f - 1)
                    nc.scalar.activation(hf[:, f % 2, 0:n], ps_h[:, f % (HB + 1), 0:n], ACT.Gelu).then_inc(hf_made, 1)
                    act.wait_ge(hf_made, FK * m + f + 1)
                    if f == 0 and not (first or (isinstance(e, int) and m < 2)):
                        act.wait_ge(y_mm, before_block(e, b))
                    nc.scalar.activation(hh[:, b % 2, f, 0:n], hf[:, f % 2, 0:n], ACT.Copy).then_inc(hh_made, 1)
                    if f in BETWEEN and not last:
                        rows_high(e + (b + 1) // NB, (b + 1) % NB, BETWEEN[f], first)
                    if with_w2 and f in W2_SPLIT:
                        split_w2(e, W2_SPLIT[f])

            def before_block(e, b):
                return NT * e + FIRST[b - 1] if b >= 1 else NT * e - TILES[NB - 1]

            def body(e, first=False, last=False):
                for b in range(NB):
                    hidden(e, b, first and b == 0, b == 1 and not first, last and b == NB - 1)
                    if b == NB - 1 and not last:
                        split_w1(e + 1)

            split_w1(0)
            rows_high(0, 0, range(DK), first=True)
            split_w2(0, range(FK))
            body(0, first=True)
            with act.Fori(1, E - 1) as e:
                body(e)
            body(E - 1, last=True)

        @block.vector
        def _(dve):
            def split_w1(e):
                for k in range(DK):
                    dve.wait_ge(w1h_made, DK * e + k + 1)
                    nc.vector.tensor_tensor(w1l[:, k, :], w1_raw[:, k, :], f32(w1h[:, k, :]), ALU.subtract).then_inc(w1l_made, 1)

            def split_w2(e, ks):
                for k in ks:
                    dve.wait_ge(w2h_made, FK * e + k + 1)
                    nc.vector.tensor_tensor(w2l[:, k, :], w2_raw[:, k, :], f32(w2h[:, k, :]), ALU.subtract).then_inc(w2l_made, 1)

            def rows_low(e, b, ks):
                n = TILES[b] * P
                m = NB * e + b
                for k in ks:
                    dve.wait_ge(xh_made, DK * m + k + 1)
                    nc.vector.tensor_tensor(xTl[:, b % 2, k, 0:n], ps_t[:, k % 2, 0:n], f32(xTh[:, b % 2, k, 0:n]), ALU.subtract).then_inc(xl_made, 1)

            def hidden_low(e, b, with_w2=False, last=False):
                n = TILES[b] * P
                m = NB * e + b
                for f in range(FK):
                    dve.wait_ge(hh_made, FK * m + f + 1)
                    nc.vector.tensor_tensor(hl[:, b % 2, f, 0:n], hf[:, f % 2, 0:n], f32(hh[:, b % 2, f, 0:n]), ALU.subtract).then_inc(hl_made, 1)
                    if f in BETWEEN and not last:
                        rows_low(e + (b + 1) // NB, (b + 1) % NB, BETWEEN[f])
                    if with_w2 and f in W2_SPLIT:
                        split_w2(e, W2_SPLIT[f])

            def rows_out(e, b, first=False):
                for t in range(TILES[b]):
                    n = FIRST[b] + t
                    dve.wait_ge(y_mm, NT * e + n + 1)
                    if not first or n >= 2:
                        dve.wait_ge(y_st[n % 2], 16 * (NT // 2 * e + n // 2))
                    nc.vector.tensor_copy(YE[:, n % 2, :], ps_y[:, n % 2, :]).then_inc(y_out, 1)

            def body(e, first=False, last=False):
                for b in range(NB):
                    hidden_low(e, b, b == 1 and not first, last and b == NB - 1)
                    if b == NB - 1 and not last:
                        split_w1(e + 1)
                    if b > 0:
                        rows_out(e, b - 1, first and b == 1)
                    elif not first:
                        rows_out(e - 1, NB - 1)

            split_w1(0)
            rows_low(0, 0, range(DK))
            split_w2(0, range(FK))
            body(0, first=True)
            with dve.Fori(1, E - 1) as e:
                body(e)
            body(E - 1, last=True)
            rows_out(E - 1, NB - 1)

        @block.tensor
        def _(pe):
            def transposes(e, b, ks, first=False):
                m = NB * e + b
                if 0 in ks:
                    pe.wait_ge(xe_in[b % 2], 16 * (NB // 2 * e + b // 2) + 16)
                for k in ks:
                    if not first or k >= 2:
                        pe.wait_ge(xl_made, DK * m + k - 1)
                    for t in range(TILES[b]):
                        last = nc.tensor.transpose(ps_t[:, k % 2, t * P:(t + 1) * P], XE[:, b % 2, t, k * P:(k + 1) * P], ident[:])
                    last.then_inc(x_tr, 1)

            def up(e, b, first=False, last=False):
                n = TILES[b] * P
                m = NB * e + b
                pe.wait_ge(xl_made, DK * m + DK)
                if b == 0:
                    pe.wait_ge(w1l_made, DK * e + DK)
                for f in range(FK):
                    if not first or f > HB:
                        pe.wait_ge(hf_made, FK * m + f - HB)
                    for k in range(DK):
                        cols = slice(f * P, (f + 1) * P)
                        product = mm3(nc, ps_h[:, f % (HB + 1), 0:n], w1h[:, k, cols], w1l[:, k, cols],
                                   xTh[:, b % 2, k, 0:n], xTl[:, b % 2, k, 0:n], k == 0, k == DK - 1)
                    product.then_inc(h_mm, 1)
                    if f in BETWEEN and not last:
                        transposes(e + (b + 1) // NB, (b + 1) % NB, BETWEEN[f])

            def down(e, b, first=False):
                m = NB * e + b
                pe.wait_ge(hl_made, FK * m + FK)
                if b == 0:
                    pe.wait_ge(w2l_made, FK * e + FK)
                for t in range(TILES[b]):
                    n = FIRST[b] + t
                    if not first or n >= 2:
                        pe.wait_ge(y_out, NT * e + n - 1)
                    toks = slice(t * P, (t + 1) * P)
                    for f in range(FK):
                        last = mm3(nc, ps_y[:, n % 2, :], hh[:, b % 2, f, toks], hl[:, b % 2, f, toks],
                                   w2h[:, f, :], w2l[:, f, :], f == 0, f == FK - 1)
                    last.then_inc(y_mm, 1)

            def body(e, first=False, last=False):
                for b in range(NB):
                    up(e, b, first and b == 0, last and b == NB - 1)
                    if b > 0:
                        down(e, b - 1, first and b == 1)
                    elif not first:
                        down(e - 1, NB - 1)

            pe.wait_ge(ident_made, 2)
            transposes(0, 0, range(DK), first=True)
            body(0, first=True)
            with pe.Fori(1, E - 1) as e:
                body(e)
            body(E - 1, last=True)
            down(E - 1, NB - 1)


class Kept:

    def __init__(self, s):
        self.norm_row = s.sb("norm_row", [P, D])
        self.slots = s.sb("slots", [P, NC, 2, TT], I32)
        self.wts = s.sb("wts", [P, NC, 2, TT])
        self.src = s.sb("src", [P, KEEP, TT, D])
        self.x1 = s.sb("x1", [P, KEEP, TT, D])


def phase_combine(nc, kept, ye_d, src_d, x1_d, out):
    YB = 3
    norm_row, slots, wts = kept.norm_row, kept.slots, kept.wts
    with Scope(nc, "p4") as s:
        half = s.sb("half", [P, TT])
        SR = s.sb("SR", [P, 2, TT, D])
        X1 = s.sb("X1", [P, 2, TT, D])
        YG = s.sb("YG", [P, YB, TT, 2, D])
        OUT = s.sb("OUT", [P, 2, TT, D])
        sq = s.sb("sq", [P, D])
        ss = s.sb("ss", [P, 2, TT])
        sv = s.sb("sv", [P, 2, TT])
        rstd = s.sb("rstd", [P, 2, TT])
        half_made = s.sem("half_made")
        sr_in = [s.sem("sr_in0"), s.sem("sr_in1")]
        x1_in = [s.sem("x1_in0"), s.sem("x1_in1")]
        yg_in = [s.sem(f"yg_in{i}") for i in range(YB)]
        out_st = [s.sem("out_st0"), s.sem("out_st1")]
        add0, add1, ss_made, sv_made, rs_made, n_made, o_made = (s.sem(n) for n in ("add0", "add1", "ss_made", "sv_made", "rs_made", "n_made", "o_made"))
        block = s.block()

        def src_rows(c):
            return kept.src[:, c] if c < KEEP else SR[:, (c - KEEP) % 2]

        def x1_rows(c):
            return kept.x1[:, c] if c < KEEP else X1[:, (c - KEEP) % 2]

        @block.sync
        def _(sp):
            for c in range(KEEP, NC):
                i = (c - KEEP) % 2
                if c >= KEEP + 2:
                    sp.wait_ge(o_made, TT * (c - 1))
                sp.dma_start(SR[:, i, :, :], src_d[c].rearrange("(t p) d -> p t d", p=P)).then_inc(sr_in[i], 16)
                sp.dma_start(X1[:, i, :, :], x1_d[c].rearrange("(t p) d -> p t d", p=P)).then_inc(x1_in[i], 16)

        @block.gpsimd
        def _(pool):
            nc.gpsimd.memset(half[:], -0.5).then_inc(half_made, 1)
            pool.wait_ge(half_made, 1)

            def fetch(c):
                if c >= YB:
                    pool.wait_ge(add1, TT * (c - YB + 1))
                for t in range(TT):
                    for k in range(2):
                        nc.gpsimd.indirect_dma_start(out=YG[:, c % YB, t, k, :], out_offset=None, in_=ye_d,
                                                     in_offset=bass.IndirectOffsetOnAxis(ap=slots[:, c, k, t:t + 1].bitcast(U32), axis=0)).then_inc(yg_in[c % YB], 16)

            for c in range(YB - 1):
                fetch(c)
            for c in range(NC):
                i = c % 2
                if c + YB - 1 < NC:
                    fetch(c + YB - 1)
                pool.wait_ge(ss_made, TT * c + TT)
                nc.gpsimd.tensor_scalar(sv[:, i, :], ss[:, i, :], 1.0 / D, RMS_EPS, ALU.mult, ALU.add).then_inc(sv_made, 1)
                pool.wait_ge(sv_made, c + 1)
                nc.gpsimd.tensor_tensor(rstd[:, i, :], sv[:, i, :], half[:], ALU.pow).then_inc(rs_made, 1)

        @block.scalar
        def _(act):
            def store(c):
                i = c % 2
                act.wait_ge(o_made, TT * c + TT)
                act.dma_start(out[c].rearrange("(t p) d -> p t d", p=P), OUT[:, i, :, :]).then_inc(out_st[i], 16)

            for c in range(NC):
                for t in range(TT):
                    act.wait_ge(add1, TT * c + t + 1)
                    if c + t > 0:
                        act.wait_ge(ss_made, TT * c + t)
                    nc.scalar.activation(sq[:], src_rows(c)[:, t, :], ACT.Square, accum_out=ss[:, c % 2, t:t + 1]).then_inc(ss_made, 1)
                if c > 0:
                    store(c - 1)
            store(NC - 1)
            for i in range(2):
                act.wait_ge(out_st[i], 16 * NC // 2)

        @block.vector
        def _(dve):
            def add(c):
                rows = src_rows(c)
                if c >= KEEP:
                    dve.wait_ge(sr_in[(c - KEEP) % 2], 16 * ((c - KEEP) // 2 + 1))
                dve.wait_ge(yg_in[c % YB], 16 * 2 * TT * (c // YB + 1))
                for k, added in ((0, add0), (1, add1)):
                    for t in range(TT):
                        if k == 1:
                            dve.wait_ge(add0, TT * c + t + 1)
                        nc.vector.scalar_tensor_tensor(rows[:, t, :], YG[:, c % YB, t, k, :], wts[:, c, k, t:t + 1], rows[:, t, :],
                                                       ALU.mult, ALU.add).then_inc(added, 1)

            def finish(c):
                i = c % 2
                dve.wait_ge(rs_made, c + 1)
                if c >= KEEP:
                    dve.wait_ge(x1_in[(c - KEEP) % 2], 16 * ((c - KEEP) // 2 + 1))
                if c >= 2:
                    dve.wait_ge(out_st[i], 16 * (c // 2))
                for t in range(TT):
                    nc.vector.scalar_tensor_tensor(OUT[:, i, t, :], src_rows(c)[:, t, :], rstd[:, i, t:t + 1], norm_row[:],
                                                   ALU.mult, ALU.mult).then_inc(n_made, 1)
                for t in range(TT):
                    dve.wait_ge(n_made, TT * c + t + 1)
                    nc.vector.tensor_tensor(OUT[:, i, t, :], OUT[:, i, t, :], x1_rows(c)[:, t, :], ALU.add).then_inc(o_made, 1)

            add(0)
            for c in range(NC):
                if c + 1 < NC:
                    add(c + 1)
                finish(c)


def build_layer(nc, x, ctx_1024, mask, gamma, beta, qw, qb, kw, kb, vw, vb, ow, ob, gate_w, w1, w2, norm1, norm2, out):
    Scope.taken.clear()

    def scratch(name, shape, dt=F32):
        return nc.dram_tensor(name, shape, dt, kind="Internal").ap()

    x1_d, y_d, src_d = (scratch(n, (NC, CH, D)) for n in ("x1_d", "y_d", "src_d"))
    qh_d, ql_d = scratch("qh_d", (NC, D, CH)), scratch("ql_d", (NC, D, CH))
    kh_d, kl_d, v_d = scratch("kh_d", (NC, P, CH)), scratch("kl_d", (NC, P, CH)), scratch("v_d", (NC, CH, P))
    xe_d, ye_d = scratch("xe_d", (E * CAP, D)), scratch("ye_d", (E * CAP, D))
    slot_d, wt_d = scratch("slot_d", (NC, P, 2 * TT), I32), scratch("wt_d", (NC, P, 2 * TT))

    def chunks(ap):
        return ap.rearrange("b (n q) d -> (b n) q d", q=CH)

    phase_project(nc, chunks(x), ctx_1024, chunks(mask), gamma, beta, qw, qb, kw, kb, vw, vb, ob,
                  x1_d, y_d, qh_d, ql_d, kh_d, kl_d, v_d)
    phase_attend(nc, y_d, qh_d, ql_d, kh_d, kl_d, v_d, ow, norm1, gate_w, src_d, xe_d, slot_d, wt_d)
    with Scope(nc, "kept") as s:
        kept = Kept(s)
        phase_experts(nc, xe_d, w1, w2, ye_d, kept, src_d, x1_d, slot_d, wt_d, norm2)
        phase_combine(nc, kept, ye_d, src_d, x1_d, chunks(out))


INPUTS = ["x", "ctx_1024", "mask_BxSxS2_ik1", "L0_xattn_gamma", "L0_xattn_beta", "L0_ffn_qw", "L0_ffn_qb", "L0_ffn_kw",
          "L0_ffn_kb", "L0_ffn_vw", "L0_ffn_vb", "L0_ffn_ow", "L0_ffn_ob", "L0_ffn_gate_w", "L0_ffn_w1", "L0_ffn_w2",
          "L0_ffn_norm1_w", "L0_ffn_norm2_w"]


def kernel(**inputs):
    import numpy as np
    import concourse.bacc as bacc
    from concourse.bass_utils import run_bass_kernel_spmd

    nc = bacc.Bacc("TRN2", target_bir_lowering=False, num_devices=1)
    arrays, args = {}, []
    for name in INPUTS:
        a = np.ascontiguousarray(inputs[name])
        arrays[f"in_{name}"] = a
        args.append(nc.dram_tensor(f"in_{name}", a.shape, mybir.dt.from_np(a.dtype), kind="ExternalInput").ap())
    args.append(nc.dram_tensor("out_dram", (B, S, D), F32, kind="ExternalOutput").ap())
    build_layer(nc, *args)
    return run_bass_kernel_spmd(nc, [arrays], core_ids=[0]).results[0]["out_dram"]
```
